# Optimizing a Trainium2 kernel written in Bass

```python
import numpy as np
import jax
import jax.numpy as jnp

def _softmax(x, axis=-1):
    return jax.nn.softmax(x, axis=axis)

def _gelu(x):
    return jax.nn.gelu(x, approximate=True)

def _silu(x):
    return jax.nn.silu(x)

def _sigmoid(x):
    return jax.nn.sigmoid(x)

def _layernorm(x, axis=-1, eps=1e-05):
    m = jnp.mean(x, axis=axis, keepdims=True)
    v = jnp.var(x, axis=axis, keepdims=True)
    return (x - m) / jnp.sqrt(v + eps)

def _scatter_add(tgt, idx, src, axis=0):
    return tgt.at[idx].add(src)

def _segment_sum(src, seg, n):
    return jax.ops.segment_sum(src, seg, n)
kernel_name = 'mk_early_fusion_d2_tok_img768_r4_841083'

def setup_inputs(seed: int=0):
    np.random.seed(seed)
    _w = jnp.asarray

    def _rec_inputs():
        import jax
        import jax.numpy as jnp
        _rk = jax.random.key(seed)
        x = -0.000222058 + 0.999998 * jax.random.normal(jax.random.fold_in(_rk, 1), (64, 3, 64, 64), jnp.float32)
        txt = 0.000626447 + 0.554253 * jax.random.normal(jax.random.fold_in(_rk, 2), (64, 32, 192), jnp.float32)
        return (x, txt)
    x, txt = _rec_inputs()

    def _L0_tok_setup():
        import jax, jax.numpy as jnp
        import numpy as np
        from jax import lax
        HIDDEN = 192
        C_IN = 3
        PATCH = 16
        SIDE = 32
        NUM_PATCHES = SIDE * SIDE

        def _position_ids(nb_h, nb_w):
            boundaries = np.arange(1.0 / SIDE, 1.0, 1.0 / SIDE, dtype=np.float32)
            frac_h = np.arange(0.0, 1.0 - 1e-06, 1.0 / nb_h, dtype=np.float32)
            frac_w = np.arange(0.0, 1.0 - 1e-06, 1.0 / nb_w, dtype=np.float32)
            bh = np.searchsorted(boundaries, frac_h, side='right')
            bw = np.searchsorted(boundaries, frac_w, side='right')
            return jnp.asarray((bh[:, None] * SIDE + bw).reshape(-1), dtype=jnp.int32)
        key = jax.random.key(seed)
        k1, k2, k3 = jax.random.split(key, 3)
        pixel_values = jax.random.normal(k1, (32, C_IN, 128, 128), dtype=jnp.float32)
        conv_w = jax.random.normal(k2, (HIDDEN, C_IN, PATCH, PATCH), dtype=jnp.float32) * 0.02
        conv_b = jnp.zeros((HIDDEN,), dtype=jnp.float32)
        pos_table = jax.random.normal(k3, (NUM_PATCHES, HIDDEN), dtype=jnp.float32) * 0.02
        return {'pixel_values': pixel_values, 'conv_w': conv_w, 'conv_b': conv_b, 'pos_table': pos_table}
    _L0_tok_all = _L0_tok_setup()
    _L0_tok_in = {k: v for k, v in _L0_tok_all.items() if k in ('conv_w', 'conv_b', 'pos_table')}
    del _L0_tok_all

    def _L0_attn_setup():
        import jax, jax.numpy as jnp
        import numpy as np
        EPS = 1e-05
        B, T, C = (8, 512, 192)
        H = 4 * C
        LAYER_ID, N_LAYER = (4, 12)

        def _ln(x, w, b):
            mu = x.mean(-1, keepdims=True)
            var = ((x - mu) ** 2).mean(-1, keepdims=True)
            return (x - mu) / jnp.sqrt(var + EPS) * w + b

        def _wkv_scan(w, k, v):
            a0 = jnp.zeros(k.shape[1:], k.dtype)
            b0 = jnp.zeros_like(a0)
            m0 = jnp.full_like(a0, -1e+38)

            def step(carry, kv):
                a, b, m = carry
                kt, vt = kv
                mm = jnp.maximum(m + w, kt)
                e1 = jnp.exp(m + w - mm)
                e2 = jnp.exp(kt - mm)
                return ((e1 * a + e2 * vt, e1 * b + e2, mm), (a, b, m))
            _, (A, Bd, M) = jax.lax.scan(step, (a0, b0, m0), (k, v))
            return (A, Bd, M)

        def bi_wkv(w, u, k, v):
            kt = jnp.swapaxes(k, 0, 1)
            vt = jnp.swapaxes(v, 0, 1)
            af, bf, mf = _wkv_scan(w, kt, vt)
            ab, bb, mb = _wkv_scan(w, kt[::-1], vt[::-1])
            ab, bb, mb = (ab[::-1], bb[::-1], mb[::-1])
            kk = kt + u
            M = jnp.maximum(jnp.maximum(mf, mb), kk)
            ef = jnp.exp(mf - M)
            eb = jnp.exp(mb - M)
            ec = jnp.exp(kk - M)
            y = (ef * af + eb * ab + ec * vt) / (ef * bf + eb * bb + ec)
            return jnp.swapaxes(y, 0, 1)
        key = jax.random.key(seed)
        ks = jax.random.split(key, 9)
        x = jax.random.normal(ks[0], (B, T, C), jnp.float32)
        r01 = LAYER_ID / (N_LAYER - 1)
        h = np.arange(C, dtype=np.float64)
        decay = (-5.0 + 8.0 * (h / (C - 1)) ** (0.7 + 1.3 * r01)).astype(np.float32)
        zigzag = ((np.arange(C) + 1) % 3 - 1).astype(np.float32) * 0.5
        first = (np.float32(np.log(0.3)) + zigzag).astype(np.float32)
        s = 0.02
        return {'x': x, 'ln1_w': jnp.ones((C,), jnp.float32), 'ln1_b': jnp.zeros((C,), jnp.float32), 'ln2_w': jnp.ones((C,), jnp.float32), 'ln2_b': jnp.zeros((C,), jnp.float32), 'decay': jnp.asarray(decay), 'first': jnp.asarray(first), 'Wk_a': s * jax.random.normal(ks[1], (C, C), jnp.float32), 'Wv_a': s * jax.random.normal(ks[2], (C, C), jnp.float32), 'Wr_a': s * jax.random.normal(ks[3], (C, C), jnp.float32), 'Wo_a': s * jax.random.normal(ks[4], (C, C), jnp.float32), 'Wk_f': s * jax.random.normal(ks[5], (H, C), jnp.float32), 'Wv_f': s * jax.random.normal(ks[6], (C, H), jnp.float32), 'Wr_f': s * jax.random.normal(ks[7], (C, C), jnp.float32)}
    _L0_attn_all = _L0_attn_setup()
    _L0_attn_in = {k: v for k, v in _L0_attn_all.items() if k in ('ln1_w', 'ln1_b', 'ln2_w', 'ln2_b', 'decay', 'first', 'Wk_a', 'Wv_a', 'Wr_a', 'Wo_a', 'Wk_f', 'Wv_f', 'Wr_f')}
    del _L0_attn_all

    def _L0_ffn_setup():
        import math
        import jax, jax.numpy as jnp
        import numpy as np
        EMBED_CHOICES = [96, 144, 192]
        RATIO_CHOICES = [2, 3, 4]
        E_MAX = 192
        H_MAX = 768

        def new_gelu(x):
            c = math.sqrt(2.0 / math.pi)
            return 0.5 * x * (1.0 + jnp.tanh(c * (x + 0.044715 * x * x * x)))

        def _mixed_coeffs(alpha_e, alpha_r):
            h_idx = jnp.arange(H_MAX)
            d_idx = jnp.arange(E_MAX)
            C0 = jnp.zeros((H_MAX, E_MAX), jnp.float32)
            c0b = jnp.zeros((H_MAX,), jnp.float32)
            C1 = jnp.zeros((E_MAX, H_MAX), jnp.float32)
            c1b = jnp.zeros((E_MAX,), jnp.float32)
            for i, e in enumerate(EMBED_CHOICES):
                m_in = (d_idx < e).astype(jnp.float32)
                for j, r in enumerate(RATIO_CHOICES):
                    a = alpha_e[i] * alpha_r[j]
                    m_out = (h_idx < r * e).astype(jnp.float32)
                    C0 = C0 + a * (m_out[:, None] * m_in[None, :])
                    c0b = c0b + a * m_out
                    C1 = C1 + a * (m_in[:, None] * m_out[None, :])
                    c1b = c1b + a * m_in
            return (C0, c0b, C1, c1b)
        key = jax.random.key(seed)
        ks = jax.random.split(key, 6)
        x = jax.random.normal(ks[0], (8, 512, E_MAX), jnp.float32)
        w_fc = jax.random.normal(ks[1], (H_MAX, E_MAX), jnp.float32) * 0.02
        b_fc = jnp.zeros((H_MAX,), jnp.float32)
        w_proj = jax.random.normal(ks[2], (E_MAX, H_MAX), jnp.float32) * 0.02
        b_proj = jnp.zeros((E_MAX,), jnp.float32)
        alpha_e = jax.nn.softmax(jax.random.normal(ks[3], (3,), jnp.float32))
        alpha_r = jax.nn.softmax(jax.random.normal(ks[4], (3,), jnp.float32))
        return {'x': x, 'w_fc': w_fc, 'b_fc': b_fc, 'w_proj': w_proj, 'b_proj': b_proj, 'alpha_e': alpha_e, 'alpha_r': alpha_r}
    _L0_ffn_all = _L0_ffn_setup()
    _L0_ffn_in = {k: v for k, v in _L0_ffn_all.items() if k in ('w_fc', 'b_fc', 'w_proj', 'b_proj', 'alpha_e', 'alpha_r')}
    del _L0_ffn_all

    def _L1_attn_setup():
        import jax, jax.numpy as jnp
        import numpy as np
        NUM_HEADS = 12
        BITS = 8
        BN_EPS = 1e-05

        def fake_quant(x, bits=BITS):
            qmax = float(2 ** (bits - 1) - 1)
            scale = jnp.maximum(jnp.max(jnp.abs(x)), 1e-08) / qmax
            q = jnp.clip(jnp.round(x / scale), -qmax, qmax) * scale
            return x + jax.lax.stop_gradient(q - x)
        key = jax.random.key(seed)
        k1, k2, k3 = jax.random.split(key, 3)
        B, S, D = (4, 512, 192)
        x = jax.random.normal(k1, (B, S, D), dtype=jnp.float32)
        w_in = jax.random.normal(k2, (3 * D, D), dtype=jnp.float32) * 0.02
        w_out = jax.random.normal(k3, (D, D), dtype=jnp.float32) * 0.02
        return {'x': x, 'w_in': w_in, 'w_out': w_out}
    _L1_attn_all = _L1_attn_setup()
    _L1_attn_in = {k: v for k, v in _L1_attn_all.items() if k in ('w_in', 'w_out')}
    del _L1_attn_all

    def _L1_ffn_setup():
        import jax, jax.numpy as jnp
        import numpy as np
        DECAY = 0.9
        EPS = 0.01
        TOP_K = 2
        key = jax.random.key(seed)
        k1, k2, k3, k4 = jax.random.split(key, 4)
        B, S, H, I, E = (4, 512, 192, 512, 8)
        return {'hidden_states': jax.random.normal(k1, (B, S, H), jnp.float32), 'router_w': jax.random.normal(k2, (E, H), jnp.float32) * 0.02, 'w1': jax.random.normal(k3, (E, I, H), jnp.float32) * 0.02, 'w2': jax.random.normal(k4, (E, H, I), jnp.float32) * 0.02}
    _L1_ffn_all = _L1_ffn_setup()
    _L1_ffn_in = {k: v for k, v in _L1_ffn_all.items() if k in ('router_w', 'w1', 'w2')}
    del _L1_ffn_all
    return {'x': x, 'txt': txt, 'L0_tok_conv_w': _L0_tok_in['conv_w'], 'L0_tok_conv_b': _L0_tok_in['conv_b'], 'L0_tok_pos_table': _L0_tok_in['pos_table'], 'L0_attn_ln1_w': _L0_attn_in['ln1_w'], 'L0_attn_ln1_b': _L0_attn_in['ln1_b'], 'L0_attn_ln2_w': _L0_attn_in['ln2_w'], 'L0_attn_ln2_b': _L0_attn_in['ln2_b'], 'L0_attn_decay': _L0_attn_in['decay'], 'L0_attn_first': _L0_attn_in['first'], 'L0_attn_Wk_a': _L0_attn_in['Wk_a'], 'L0_attn_Wv_a': _L0_attn_in['Wv_a'], 'L0_attn_Wr_a': _L0_attn_in['Wr_a'], 'L0_attn_Wo_a': _L0_attn_in['Wo_a'], 'L0_attn_Wk_f': _L0_attn_in['Wk_f'], 'L0_attn_Wv_f': _L0_attn_in['Wv_f'], 'L0_attn_Wr_f': _L0_attn_in['Wr_f'], 'L0_ffn_w_fc': _L0_ffn_in['w_fc'], 'L0_ffn_b_fc': _L0_ffn_in['b_fc'], 'L0_ffn_w_proj': _L0_ffn_in['w_proj'], 'L0_ffn_b_proj': _L0_ffn_in['b_proj'], 'L0_ffn_alpha_e': _L0_ffn_in['alpha_e'], 'L0_ffn_alpha_r': _L0_ffn_in['alpha_r'], 'L1_attn_w_in': _L1_attn_in['w_in'], 'L1_attn_w_out': _L1_attn_in['w_out'], 'L1_ffn_router_w': _L1_ffn_in['router_w'], 'L1_ffn_w1': _L1_ffn_in['w1'], 'L1_ffn_w2': _L1_ffn_in['w2']}

def reference(x, txt, L0_tok_conv_w, L0_tok_conv_b, L0_tok_pos_table, L0_attn_ln1_w, L0_attn_ln1_b, L0_attn_ln2_w, L0_attn_ln2_b, L0_attn_decay, L0_attn_first, L0_attn_Wk_a, L0_attn_Wv_a, L0_attn_Wr_a, L0_attn_Wo_a, L0_attn_Wk_f, L0_attn_Wv_f, L0_attn_Wr_f, L0_ffn_w_fc, L0_ffn_b_fc, L0_ffn_w_proj, L0_ffn_b_proj, L0_ffn_alpha_e, L0_ffn_alpha_r, L1_attn_w_in, L1_attn_w_out, L1_ffn_router_w, L1_ffn_w1, L1_ffn_w2):
    import jax
    import jax.numpy as jnp

    def _L0_tok_ref(pixel_values, conv_w, conv_b, pos_table):
        import jax, jax.numpy as jnp
        import numpy as np
        from jax import lax
        HIDDEN = 192
        C_IN = 3
        PATCH = 16
        SIDE = 32
        NUM_PATCHES = SIDE * SIDE

        def _position_ids(nb_h, nb_w):
            boundaries = np.arange(1.0 / SIDE, 1.0, 1.0 / SIDE, dtype=np.float32)
            frac_h = np.arange(0.0, 1.0 - 1e-06, 1.0 / nb_h, dtype=np.float32)
            frac_w = np.arange(0.0, 1.0 - 1e-06, 1.0 / nb_w, dtype=np.float32)
            bh = np.searchsorted(boundaries, frac_h, side='right')
            bw = np.searchsorted(boundaries, frac_w, side='right')
            return jnp.asarray((bh[:, None] * SIDE + bw).reshape(-1), dtype=jnp.int32)
        B, _, H, W = pixel_values.shape
        nb_h, nb_w = (H // PATCH, W // PATCH)
        patches = lax.conv_general_dilated(pixel_values, conv_w, window_strides=(PATCH, PATCH), padding='VALID', dimension_numbers=('NCHW', 'OIHW', 'NCHW'))
        patches = patches + conv_b[None, :, None, None]
        embeddings = patches.reshape(B, HIDDEN, nb_h * nb_w).transpose(0, 2, 1)
        pos_ids = _position_ids(nb_h, nb_w)
        pos_emb = pos_table[pos_ids]
        return embeddings + pos_emb[None, :, :]

    def _L0_attn_ref(x, ln1_w, ln1_b, ln2_w, ln2_b, decay, first, Wk_a, Wv_a, Wr_a, Wo_a, Wk_f, Wv_f, Wr_f):
        import jax, jax.numpy as jnp
        import numpy as np
        EPS = 1e-05
        B, T, C = (8, 512, 192)
        H = 4 * C
        LAYER_ID, N_LAYER = (4, 12)

        def _ln(x, w, b):
            mu = x.mean(-1, keepdims=True)
            var = ((x - mu) ** 2).mean(-1, keepdims=True)
            return (x - mu) / jnp.sqrt(var + EPS) * w + b

        def _wkv_scan(w, k, v):
            a0 = jnp.zeros(k.shape[1:], k.dtype)
            b0 = jnp.zeros_like(a0)
            m0 = jnp.full_like(a0, -1e+38)

            def step(carry, kv):
                a, b, m = carry
                kt, vt = kv
                mm = jnp.maximum(m + w, kt)
                e1 = jnp.exp(m + w - mm)
                e2 = jnp.exp(kt - mm)
                return ((e1 * a + e2 * vt, e1 * b + e2, mm), (a, b, m))
            _, (A, Bd, M) = jax.lax.scan(step, (a0, b0, m0), (k, v))
            return (A, Bd, M)

        def bi_wkv(w, u, k, v):
            kt = jnp.swapaxes(k, 0, 1)
            vt = jnp.swapaxes(v, 0, 1)
            af, bf, mf = _wkv_scan(w, kt, vt)
            ab, bb, mb = _wkv_scan(w, kt[::-1], vt[::-1])
            ab, bb, mb = (ab[::-1], bb[::-1], mb[::-1])
            kk = kt + u
            M = jnp.maximum(jnp.maximum(mf, mb), kk)
            ef = jnp.exp(mf - M)
            eb = jnp.exp(mb - M)
            ec = jnp.exp(kk - M)
            y = (ef * af + eb * ab + ec * vt) / (ef * bf + eb * bb + ec)
            return jnp.swapaxes(y, 0, 1)
        Bn, Tn, Cn = x.shape
        h = _ln(x, ln1_w, ln1_b)
        k = h @ Wk_a.T
        v = h @ Wv_a.T
        sr = jax.nn.sigmoid(h @ Wr_a.T)
        y = bi_wkv(decay / Tn, first / Tn, k, v)
        x = x + sr * y @ Wo_a.T
        h = _ln(x, ln2_w, ln2_b)
        kf = jnp.square(jax.nn.relu(h @ Wk_f.T))
        x = x + jax.nn.sigmoid(h @ Wr_f.T) * (kf @ Wv_f.T)
        return x

    def _L0_ffn_ref(x, w_fc, b_fc, w_proj, b_proj, alpha_e, alpha_r):
        import math
        import jax, jax.numpy as jnp
        import numpy as np
        EMBED_CHOICES = [96, 144, 192]
        RATIO_CHOICES = [2, 3, 4]
        E_MAX = 192
        H_MAX = 768

        def new_gelu(x):
            c = math.sqrt(2.0 / math.pi)
            return 0.5 * x * (1.0 + jnp.tanh(c * (x + 0.044715 * x * x * x)))

        def _mixed_coeffs(alpha_e, alpha_r):
            h_idx = jnp.arange(H_MAX)
            d_idx = jnp.arange(E_MAX)
            C0 = jnp.zeros((H_MAX, E_MAX), jnp.float32)
            c0b = jnp.zeros((H_MAX,), jnp.float32)
            C1 = jnp.zeros((E_MAX, H_MAX), jnp.float32)
            c1b = jnp.zeros((E_MAX,), jnp.float32)
            for i, e in enumerate(EMBED_CHOICES):
                m_in = (d_idx < e).astype(jnp.float32)
                for j, r in enumerate(RATIO_CHOICES):
                    a = alpha_e[i] * alpha_r[j]
                    m_out = (h_idx < r * e).astype(jnp.float32)
                    C0 = C0 + a * (m_out[:, None] * m_in[None, :])
                    c0b = c0b + a * m_out
                    C1 = C1 + a * (m_in[:, None] * m_out[None, :])
                    c1b = c1b + a * m_in
            return (C0, c0b, C1, c1b)
        C0, c0b, C1, c1b = _mixed_coeffs(alpha_e, alpha_r)
        W0 = w_fc * C0
        b0 = b_fc * c0b
        h = jnp.einsum('bte,he->bth', x, W0) + b0
        h = new_gelu(h)
        W1 = w_proj * C1
        b1 = b_proj * c1b
        out = jnp.einsum('bth,eh->bte', h, W1) + b1
        return out

    def _L1_attn_ref(x, w_in, w_out):
        import jax, jax.numpy as jnp
        import numpy as np
        NUM_HEADS = 12
        BITS = 8
        BN_EPS = 1e-05

        def fake_quant(x, bits=BITS):
            qmax = float(2 ** (bits - 1) - 1)
            scale = jnp.maximum(jnp.max(jnp.abs(x)), 1e-08) / qmax
            q = jnp.clip(jnp.round(x / scale), -qmax, qmax) * scale
            return x + jax.lax.stop_gradient(q - x)
        B, S, D = x.shape
        H = NUM_HEADS
        Dh = D // H
        wq_in = fake_quant(w_in)
        wq_out = fake_quant(w_out)
        qkv = jnp.einsum('bsd,ed->bse', x, wq_in)
        q, k, v = jnp.split(qkv, 3, axis=-1)

        def to_heads(t):
            return t.reshape(B, S, H, Dh).transpose(0, 2, 1, 3)
        q = fake_quant(to_heads(q))
        k = fake_quant(to_heads(k))
        v = fake_quant(to_heads(v))
        scores = jnp.einsum('bhqd,bhkd->bhqk', q, k) / jnp.sqrt(jnp.float32(Dh))
        scores = fake_quant(scores)
        attn = fake_quant(jax.nn.softmax(scores, -1))
        ctx = jnp.einsum('bhqk,bhkd->bhqd', attn, v)
        ctx = ctx.transpose(0, 2, 1, 3).reshape(B, S, D)
        ctx = fake_quant(ctx)
        y = jnp.einsum('bsd,ed->bse', ctx, wq_out)
        r = fake_quant(y) + fake_quant(x)
        mean = r.mean(axis=(0, 1))
        var = r.var(axis=(0, 1))
        rn = (r - mean) / jnp.sqrt(var + BN_EPS)
        return fake_quant(rn)

    def _L1_ffn_ref(hidden_states, router_w, w1, w2):
        import jax, jax.numpy as jnp
        import numpy as np
        DECAY = 0.9
        EPS = 0.01
        TOP_K = 2
        B, S, H = hidden_states.shape
        E = router_w.shape[0]
        flat = hidden_states.reshape(B * S, H)
        logits = flat @ router_w.T
        probs = jax.nn.softmax(logits, axis=-1)
        topk_probs, topk_idx = jax.lax.top_k(probs, TOP_K)
        importance = jax.lax.stop_gradient(probs).sum(axis=0)
        running = jnp.ones((E,), dtype=flat.dtype)
        blended = running + (1.0 - DECAY) * (importance - running)
        running = blended + EPS
        balance = running[topk_idx]
        balanced = topk_probs / balance
        balanced = balanced / balanced.sum(axis=-1, keepdims=True)
        h = jnp.einsum('th,eih->tei', flat, w1)
        h = jax.nn.silu(h)
        outs = jnp.einsum('tei,ehi->teh', h, w2)
        sel = jnp.take_along_axis(outs, topk_idx[:, :, None], axis=1)
        combined = (sel * balanced[..., None]).sum(axis=1)
        return combined.reshape(B, S, H)
    h = _L0_tok_ref(x, L0_tok_conv_w, L0_tok_conv_b, L0_tok_pos_table)
    h = jnp.concatenate([h, txt], axis=1)
    h = h + _L0_attn_ref(_layernorm(h, axis=-1), L0_attn_ln1_w, L0_attn_ln1_b, L0_attn_ln2_w, L0_attn_ln2_b, L0_attn_decay, L0_attn_first, L0_attn_Wk_a, L0_attn_Wv_a, L0_attn_Wr_a, L0_attn_Wo_a, L0_attn_Wk_f, L0_attn_Wv_f, L0_attn_Wr_f)
    h = h + _L0_ffn_ref(_layernorm(h, axis=-1), L0_ffn_w_fc, L0_ffn_b_fc, L0_ffn_w_proj, L0_ffn_b_proj, L0_ffn_alpha_e, L0_ffn_alpha_r)
    h = h + _L1_attn_ref(_layernorm(h, axis=-1), L1_attn_w_in, L1_attn_w_out)
    h = h + _L1_ffn_ref(_layernorm(h, axis=-1), L1_ffn_router_w, L1_ffn_w1, L1_ffn_w2)
    return h

_drawn_inputs = setup_inputs


def setup_inputs(seed=0):
    import zlib

    import numpy as np

    out = dict(_drawn_inputs(seed))
    spreads = {'L0_tok_conv_b': (0.0, 0.1),
     'L0_attn_ln1_w': (1.0, 0.6),
     'L0_attn_ln1_b': (0.0, 0.8),
     'L0_attn_ln2_w': (1.0, 0.6),
     'L0_attn_ln2_b': (0.0, 0.8),
     'L0_ffn_b_fc': (0.0, 0.689),
     'L0_ffn_b_proj': (0.0, 0.348)}
    factors = {'L0_tok_pos_table': 2.713,
     'L0_attn_decay': 8.0,
     'L0_attn_first': 64.0,
     'L0_attn_Wk_a': 8.0,
     'L0_attn_Wv_a': 8.0,
     'L0_attn_Wr_a': 8.0,
     'L0_attn_Wo_a': 8.0,
     'L0_attn_Wk_f': 3.1,
     'L0_attn_Wv_f': 3.019,
     'L0_attn_Wr_f': 8.0,
     'L0_ffn_alpha_e': 3.362,
     'L0_ffn_alpha_r': 6.302,
     'L1_attn_w_in': 39.811,
     'L1_attn_w_out': 38.84,
     'L1_ffn_router_w': 27.448,
     'L1_ffn_w1': 24.856,
     'L1_ffn_w2': 23.976}
    for name, (base, spread) in spreads.items():
        noise = np.random.default_rng([zlib.crc32(name.encode()), seed]).standard_normal(out[name].shape)
        drawn = base * np.exp(spread * noise) if base else spread * noise
        out[name] = jnp.asarray(drawn.astype(out[name].dtype))
    for name, factor in factors.items():
        out[name] = (out[name] * factor).astype(out[name].dtype)
    return out
```

```python
from contextlib import ExitStack

import numpy as np

import concourse.bass as bass
from concourse import mybir

F32 = mybir.dt.float32
BF16 = mybir.dt.bfloat16
U32 = mybir.dt.uint32
ALU = mybir.AluOpType
ACT = mybir.ActivationFunctionType
AX = mybir.AxisListType
RMAX = bass.bass_isa.ReduceOp.max
RADD = bass.bass_isa.ReduceOp.add

P = 128
B, T, C = 64, 48, 192
TP, TX = 16, 32
HC = C // 2
NG, GB = 8, 8
GT = GB * T
NT = 3 * NG
KC = 768 // P
HID = 768
HCH = HID // P
ROWS = GB + GB // 2
TS = T + 1
EPS = 1e-5
NEG = -1e38
NH, DH = 12, 16
MAGIC = 12582912.0
EMBEDS, RATIOS = (96, 144, 192), (2, 3, 4)
NE, ID = 8, 512
QMAX = 127.0
NP = B // 2
PP = 112
NS = NP // 2
SETW = 2 * NH * T
BIAS_NAMES = ("conv_b",)


class Straight:

    def __init__(self, sem):
        self.sem, self.n = sem, 0

    def on(self, eng):
        self.eng = eng
        return self

    def did(self, ins):
        self.n += 1
        ins.then_inc(self.sem, 1)

    def settle(self):
        self.eng.wait_ge(self.sem, self.n)


class Steps:

    def __init__(self, eng, sem, per=0):
        self.eng, self.sem, self.per, self.base, self.n = eng, sem, per, 0, 0

    def turn(self, i):
        assert self.n in (0, self.per)
        self.base, self.n = i * self.per, 0

    def did(self, ins):
        self.n += 1
        ins.then_inc(self.sem, 1)

    def settle(self):
        self.eng.wait_ge(self.sem, self.base + self.n)

    def end(self):
        assert self.n == self.per, (self.n, self.per)


def bcast(ap, n, at):
    v = ap.unsqueeze(at)
    shape = list(v.shape)
    shape[at] = n
    return v.broadcast_to(shape)


def program(nc, a, out):
    ctx = ExitStack()
    with ctx:
        def sb(name, shape, dt=F32, scope=ctx):
            return scope.enter_context(nc.sbuf_tensor(name, shape, dt))

        def sem(name):
            return ctx.enter_context(nc.semaphore(name))

        PS = ctx.enter_context(nc.psum_tensor("PS", [P, 8, 512], F32))
        straight = Straight(sem("straight"))
        passed = sem("passed")
        H = sb("H", [P, NT, C])
        ident = sb("ident", [P, P])
        identb = sb("identb", [P, P], BF16)
        neghalf = sb("neghalf", [P, 16])
        stat = sb("stat", [P, 3, 6])
        mv = sb("mv", [P, 3, 2])
        varp = sb("varp", [P, 3])
        rstd = sb("rstd", [P, 3])

        def norm(v, steps, src, dst, var_ready, rstd_ready, count, ready=None):
            for j in range(3):
                steps.did(v.bn_stats(stat[:, j, :], src[:, j, :]))
            steps.settle()
            seen(v, passed)
            for j in range(3):
                steps.did(v.bn_aggr(mv[:, j, :], stat[:, j, :]))
            steps.settle()
            v.tensor_scalar(varp[:, :], mv[:, :, 1], EPS, None, ALU.add).then_inc(var_ready, 1)
            v.wait_ge(rstd_ready, count)
            for j in range(3):
                ins = v.tensor_scalar(dst[:, j, :], src[:, j, :], mv[:, j, 0:1], rstd[:, j:j + 1],
                                      ALU.subtract, ALU.mult)
                if ready is None:
                    steps.did(ins)
                else:
                    ins.then_inc(ready, 1)

        def rsqrt(g, var_ready, rstd_ready, count):
            g.wait_ge(var_ready, count)
            g.tensor_tensor(out=rstd[:, :], in0=varp[:, :], in1=neghalf[:, 0:3],
                            op=ALU.pow).then_inc(rstd_ready, 1)

        embed_and_mix(nc, straight, passed, a, sem, sb, PS, H, ident, identb, neghalf, norm, rsqrt)
        att = ExitStack()
        with att:
            SC = sb("SC", [P, 24], F32, att)
            MX = sb("MX", [P, 16], F32, att)
            wout = sb("wout", [HC, 2, C], BF16, att)
            Vi = sb("Vi", [P, NP, C], BF16, att)
            stage = ExitStack()
            with stage:
                Qp = sb("Qp", [P, 3, B * T], BF16, stage)
                Kp = sb("Kp", [P, 3, B * T], BF16, stage)
                real = ExitStack()
                with real:
                    Q = sb("Qf", [HC, 2, B * T], F32, real)
                    K = sb("Kf", [HC, 2, B * T], F32, real)
                    V = sb("Vf", [P, NP, C], F32, real)
                    ffn_and_project(nc, straight, passed, a, sem, sb, PS, H, ident, norm, rsqrt, Q, K, V, MX, SC, Qp, Kp)
                    quantise_qkv(nc, straight, passed, a, sem, sb, PS, SC, Q, K, V, Qp, Kp, Vi, wout, MX)
                Qs = sb("Qs", [P, 2, 3, GT], BF16, stage)
                Ks = sb("Ks", [P, 2, 3, GT], BF16, stage)
                E = sb("E", [P, NS, SETW], F32, stage)
                RS = sb("RS", [P, NS, 2 * NH], F32, stage)
                score_maximum(nc, straight, passed, sem, sb, PS, SC, Qp, Kp, Qs, Ks)
                softmax_rows(nc, straight, passed, sem, sb, PS, SC, Qp, Kp, Qs, Ks, E, RS)
                CTX = sb("CTX", [P, NP, C], F32, stage)
                context(nc, straight, passed, sem, sb, PS, SC, identb, E, RS, Vi, CTX)
                Y = E[:, 0:4, :].rearrange("p a n -> p (a n)").rearrange("p (j c) -> p j c", c=C)
                R = E[:, 4:8, :].rearrange("p a n -> p (a n)").rearrange("p (j c) -> p j c", c=C)
                project_out(nc, straight, passed, sem, sb, PS, SC, H, identb, norm, rsqrt, CTX, wout, Y, R)
                batch_norm(nc, straight, passed, sem, sb, PS, SC, H, Y, R)
        moe = ExitStack()
        with moe:
            XT = sb("XT", [HC, 2, B * T], F32, moe)
            G = sb("G", [P, NT, NE], F32, moe)
            route(nc, straight, passed, a, sem, sb, PS, H, ident, norm, rsqrt, XT, G)
            experts(nc, straight, passed, a, sem, sb, PS, H, XT, G)
        nc_out(nc, sem, H, out)


def ffn_and_project(nc, straight, passed, a, sem, sb_, PS, H, ident, norm, rsqrt, Q, K, V, MX, SC, Qp, Kp):
    scope = ExitStack()
    with scope:
        def sb(name, shape, dt=F32):
            return sb_(name, shape, dt, scope)

        s = {n: sem("p2_" + n) for n in (
            "weights", "set_ready", "var", "rstd", "norm", "turned", "xT", "up", "gelu", "down",
            "h3", "qk", "qk_in", "v", "v_in", "loop_dve", "wmaxes", "wmax_all", "zeros")}
        w0 = sb("w0", [HC, 2, HID])
        w1 = sb("w1", [P, HCH, C])
        win = sb("win", [HC, 2, 3 * C])
        alpha = sb("alpha", [P, 2, 3])
        aij = sb("aij", [P, 3, 3])
        hmask = sb("hmask", [P, HCH, 9])
        g0 = sb("g0", [P, 3, HID])
        gc = sb("gc", [P, 3, HCH])
        gp_ = sb("gp_", [P, HCH, 9])
        cut = sb("cut", [P, 1])
        bfc = sb("bfc", [P, HCH])
        bpr = sb("bpr", [P, C])
        hn = sb("hn2", [P, 3, C])
        xT = sb("xT", [HC, 2, GT])
        gl = sb("gl", [P, HCH, GT])
        tmp = sb("tmp2", [P, 3, C])
        LOOP_DVE = 20
        wmax = sb("wmax", [P, 4])

        psT = PS[:, 0:2, :]

        def tiles(ps):
            return ps.rearrange("p k (j c) -> p (k j) c", c=256)[:, 0:3, 0:C]

        with nc.Block() as block:
            @block.sync
            def _(sp):
                def load(dst, src):
                    sp.dma_start(dst, src).then_inc(s["weights"], 16)
                load(w0[:, :, :], a["w_fc"])
                load(w1[:, :, :], a["w_proj"])
                load(win[:, :, :], a["w_in"])
                load(alpha[:, 0, :], a["alpha_e"].to_broadcast([P, 3]))
                load(alpha[:, 1, :], a["alpha_r"].to_broadcast([P, 3]))
                load(hmask[:, :, :], a["hmask"])
                load(bfc[:, :], a["b_fc"])
                load(bpr[:, :], a["b_proj"].to_broadcast([P, C]))
                load(cut[:, :], a["cut"])

            NW = 9

            @block.gpsimd
            def _(gp):
                for x in (Qp, Kp):
                    gp.memset(x[:, :, :].rearrange("p c n -> p (c n)").bitcast(F32), 0.0).then_inc(s["zeros"], 1)
                gp.wait_ge(s["wmaxes"], 1)
                gp.partition_all_reduce(wmax[:, 1:2], wmax[:, 0:1], P, RMAX).then_inc(s["wmax_all"], 1)
                with gp.Fori(0, NG) as g:
                    rsqrt(gp, s["var"], s["rstd"], g * 2 + 1)
                    rsqrt(gp, s["var"], s["rstd"], g * 2 + 2)

            @block.vector
            def _(v):
                st = straight.on(v)
                st.did(v.memset(wmax[:, :], 0.0))
                st.did(v.memset(MX[:, :], 0.0))
                st.did(v.memset(PS[:, 6:8, :], 0.0))
                v.wait_ge(s["weights"], 16 * NW)
                st.settle()
                v.tensor_reduce(wmax[0:HC, 0:1], win[:, :, :].rearrange("p c n -> p (c n)"), AX.X, ALU.max,
                                apply_absolute_value=True).then_inc(s["wmaxes"], 1)
                for i in range(3):
                    st.did(v.tensor_scalar(aij[:, i, :], alpha[:, 1, :], alpha[:, 0, i:i + 1], None, ALU.mult))
                st.did(v.memset(g0[:, :, :], 0.0))
                st.settle()
                for j, r in enumerate(RATIOS):
                    for i, e in enumerate(EMBEDS):
                        st.did(v.tensor_scalar(g0[:, i, 0:r * e], g0[:, i, 0:r * e], aij[:, i, j:j + 1], None,
                                               ALU.add))
                    st.settle()
                st.did(v.tensor_tensor(gp_[:, :, :], hmask[:, :, :],
                                       bcast(aij[:, :, :].rearrange("p i j -> p (i j)"), HCH, 1), ALU.mult))
                st.settle()
                for i in range(3):
                    st.did(v.tensor_reduce(gc[:, i, :], gp_[:, :, 3 * i:3 * i + 3], AX.X, ALU.add))
                st.settle()
                st.did(v.tensor_tensor(g0[:, 0, :], g0[:, 0, :], g0[:, 1, :], ALU.add))
                st.did(v.tensor_tensor(gc[:, 1, :], gc[:, 1, :], gc[:, 2, :], ALU.add))
                st.settle()
                st.did(v.tensor_tensor(g0[:, 0, :], g0[:, 0, :], g0[:, 2, :], ALU.add))
                st.did(v.scalar_tensor_tensor(g0[:, 1, :], g0[:, 1, :], cut[:, 0:1], g0[:, 2, :], ALU.mult,
                                              ALU.add))
                st.did(v.tensor_tensor(gc[:, 0, :], gc[:, 0, :], gc[:, 1, :], ALU.add))
                st.settle()
                for c in range(2):
                    st.did(v.tensor_tensor(w0[:, c, :], w0[:, c, :], g0[0:HC, c, :], ALU.mult))
                for i, (e0, e1) in enumerate(((0, 96), (96, 144), (144, 192))):
                    for m in range(HCH):
                        st.did(v.tensor_scalar(w1[:, m, e0:e1], w1[:, m, e0:e1], gc[:, i, m:m + 1], None,
                                               ALU.mult))
                st.did(v.tensor_tensor(bfc[:, :], bfc[:, :], gc[:, 0, :], ALU.mult))
                st.did(v.tensor_reduce(alpha[:, 0, :], aij[:, :, :], AX.X, ALU.add))
                st.settle()
                st.did(v.tensor_scalar(alpha[:, 1, 1:2], alpha[:, 0, 1:2], alpha[:, 0, 2:3], None, ALU.add))
                st.settle()
                st.did(v.tensor_scalar(alpha[:, 1, 0:1], alpha[:, 0, 0:1], alpha[:, 1, 1:2], None, ALU.add))
                st.settle()
                for e0, e1, k in ((0, 96, alpha[:, 1, 0:1]), (96, 144, alpha[:, 1, 1:2]),
                                  (144, 192, alpha[:, 0, 2:3])):
                    st.did(v.tensor_scalar(bpr[:, e0:e1], bpr[:, e0:e1], k, None, ALU.mult))
                v.wait_ge(s["wmax_all"], 1)
                st.did(v.tensor_scalar(wmax[:, 2:3], wmax[:, 1:2], 1e-8, 1.0 / QMAX, ALU.max, ALU.mult))
                st.settle()
                st.did(v.reciprocal(wmax[:, 3:4], wmax[:, 2:3]))
                st.settle()
                st.did(v.tensor_copy(SC[:, S_WIN:S_WIN + 1], wmax[:, 2:3]))
                st.did(v.tensor_scalar(win[:, :, :], win[:, :, :], wmax[0:HC, 3:4], MAGIC, ALU.mult, ALU.add))
                st.settle()
                v.tensor_scalar(win[:, :, :], win[:, :, :], -MAGIC, None, ALU.add).then_inc(s["set_ready"], 1)
                v.wait_ge(s["set_ready"], 1)
                st.settle()

                loop = Steps(v, s["loop_dve"], LOOP_DVE)
                with v.Fori(0, NG) as g:
                    loop.turn(g)
                    hg = H[:, bass.ds(g * 3, 3), :]
                    loop.did(v.tensor_scalar(tmp[:, :, :], hg, 1.0, None, ALU.mult))
                    loop.settle()
                    norm(v, loop, tmp, hn, s["var"], s["rstd"], g * 2 + 1, s["norm"])
                    v.wait_ge(s["down"], g + 1)
                    loop.did(v.tensor_tensor(tmp[:, :, :], tmp[:, :, :], tiles(PS[:, 2:4, :]), ALU.add))
                    loop.settle()
                    loop.did(v.tensor_tensor(tmp[:, :, :], tmp[:, :, :], bcast(bpr[:, :], 3, 1), ALU.add))
                    loop.settle()
                    v.tensor_scalar(H[:, bass.ds(g * 3, 3), :], tmp[:, :, :], 1.0, None, ALU.mult
                                    ).then_inc(s["h3"], 1)
                    norm(v, loop, tmp, hn, s["var"], s["rstd"], g * 2 + 2, s["norm"])
                    v.wait_ge(s["norm"], g * 6 + 6)
                    loop.did(v.tensor_reduce(MX[:, 7:8], hn[:, :, :].rearrange("p j c -> p (j c)"), AX.X,
                                             ALU.max, apply_absolute_value=True))
                    v.wait_ge(s["qk_in"], g * 4 + 4)
                    for k in range(2):
                        loop.did(v.tensor_reduce(MX[0:HC, 4 + k:5 + k], PS[0:HC, 2 + 2 * k:4 + 2 * k, 0:GT], AX.XY,
                                                 ALU.max, apply_absolute_value=True))
                    v.wait_ge(s["v_in"], g + 1)
                    loop.did(v.tensor_reduce(
                        MX[0:PP, 6:7], PS[0:PP, 6:8, :].rearrange("p k (j c) -> p (k j) c", c=256)[:, :, 0:C],
                        AX.XY, ALU.max, apply_absolute_value=True))
                    loop.settle()
                    loop.did(v.tensor_tensor(MX[:, 0:4], MX[:, 0:4], MX[:, 4:8], ALU.max))
                    loop.settle()
                    v.wait_ge(s["v_in"], g + 1)
                    v.wait_ge(s["h3"], g + 1)
                    loop.end()

            @block.tensor
            def _(pe):
                pe.wait_ge(s["set_ready"], 1)
                with pe.Fori(0, NG) as g:
                    def turn(n):
                        pe.wait_ge(s["norm"], g * 6 + n)
                        for c in range(2):
                            for j in range(3):
                                mm = pe.transpose(psT[0:HC, c, j * P:(j + 1) * P],
                                                  hn[:, j, c * HC:(c + 1) * HC], ident[:, :])
                        mm.then_inc(s["turned"], 1)

                    turn(3)
                    pe.wait_ge(s["xT"], g * 6 + 2)
                    for m in range(HCH):
                        for c in range(2):
                            mm = pe.matmul(PS[:, 2 + m, 0:GT], w0[:, c, m * P:(m + 1) * P], xT[:, c, :],
                                           start=c == 0, stop=c == 1)
                        mm.then_inc(s["up"], 1)
                    pe.wait_ge(s["gelu"], g * HCH + HCH)
                    for j in range(3):
                        for m in range(HCH):
                            mm = pe.matmul(PS[:, 2 + j // 2, (j % 2) * 256:(j % 2) * 256 + C],
                                           gl[:, m, j * P:(j + 1) * P], w1[:, m, :],
                                           start=m == 0, stop=m == HCH - 1)
                    mm.then_inc(s["down"], 1)
                    turn(6)
                    pe.wait_ge(s["xT"], g * 6 + 6)
                    for m in range(4):
                        for c in range(2):
                            mm = pe.matmul(PS[0:HC, 2 + m, 0:GT], win[:, c, m * HC:(m + 1) * HC], xT[:, c, :],
                                           start=c == 0, stop=c == 1)
                        mm.then_inc(s["qk"], 1)
                    for half in range(2):
                        for b in range(4):
                            o = 64 * (b % 2)
                            for c in range(2):
                                mm = pe.matmul(PS[o:o + T, 6 + half, (b // 2) * 256:(b // 2) * 256 + C],
                                               xT[:, c, (half * 4 + b) * T:(half * 4 + b + 1) * T],
                                               win[:, c, 2 * C:3 * C], start=c == 0, stop=c == 1,
                                               skip_group_check=True)
                    mm.then_inc(s["v"], 1)
                    pe.wait_ge(s["qk_in"], g * 4 + 4)

            @block.scalar
            def _(act):
                act.wait_ge(s["set_ready"], 1)
                with act.Fori(0, NG) as g:
                    act.wait_ge(s["turned"], g * 2 + 1)
                    for c in range(2):
                        act.activation(xT[:, c, :], psT[0:HC, c, 0:GT], ACT.Identity).then_inc(s["xT"], 1)
                    for m in range(HCH):
                        act.wait_ge(s["up"], g * HCH + m + 1)
                        act.activation(gl[:, m, :], PS[:, 2 + m, 0:GT], ACT.Gelu_apprx_tanh, bias=bfc[:, m:m + 1]
                                       ).then_inc(s["gelu"], 1)
                    act.wait_ge(s["turned"], g * 2 + 2)
                    for c in range(2):
                        for j0, j1, t0, t1 in ((0, P, 0, TP), (P, GT, TP, T)):
                            act.activation(xT[:, c, :].rearrange("p (b t) -> p b t", t=T)[:, :, t0:t1],
                                           psT[0:HC, c, j0:j1].rearrange("p (b t) -> p b t", t=t1 - t0),
                                           ACT.Identity).then_inc(s["xT"], 1)
                    for m in range(4):
                        act.wait_ge(s["qk"], g * 4 + m + 1)
                        dst = (Q, K)[m // 2]
                        act.activation(dst[:, m % 2, bass.ds(g * GT, GT)], PS[0:HC, 2 + m, 0:GT], ACT.Identity,
                                       scale=wmax[0:HC, 2:3]).then_inc(s["qk_in"], 1)
                    act.wait_ge(s["v"], g + 1)
                    act.activation(V[0:PP, bass.ds(g * 4, 4), :],
                                   PS[0:PP, 6:8, :].rearrange("p k (j c) -> p (k j) c", c=256)[:, :, 0:C],
                                   ACT.Identity, scale=wmax[0:PP, 2:3]).then_inc(s["v_in"], 1)


def seen(eng, held):
    eng.sem_inc(held, 1)


(S_WIN, S_WOUT, S_Q, S_K, S_V, S_X, S_SCORE, S_ATT, S_CTX, S_Y, S_RN) = range(11)


class Scales:

    def __init__(self, v, steps, table):
        self.v, self.st, self.t = v, steps, table

    def col(self, k):
        return self.t[:, k:k + 1]

    def op(self, dst, src, s1, s2, op0, op1=None):
        if op1 is None:
            ins = self.v.tensor_scalar(self.col(dst), self.col(src), s1, None, op0)
        else:
            ins = self.v.tensor_scalar(self.col(dst), self.col(src), s1, s2, op0, op1)
        self.st.did(ins)
        self.st.settle()

    def inverse(self, dst, src):
        self.st.did(self.v.reciprocal(self.col(dst), self.col(src)))
        self.st.settle()


def quantise_qkv(nc, straight, passed, a, sem, sb_, PS, SC, Q, K, V, Qp, Kp, Vi, wout, MX):
    scope = ExitStack()
    with scope:
        def sb(name, shape, dt=F32):
            return sb_(name, shape, dt, scope)

        s = {n: sem("p3_" + n) for n in ("wout", "maxes", "all", "q", "k", "v", "padded",
                                         "pool")}
        Qi = sb("Qi", [HC, 2, B * T], BF16)
        Ki = sb("Ki", [HC, 2, B * T], BF16)
        wf = sb("wf", [HC, 2, C])
        F_Q, F_K, F_V, F_W, M_ = 11, 12, 13, 14, 16
        with nc.Block() as block:
            @block.sync
            def _(sp):
                sp.dma_start(wf[:, :, :], a["w_out"]).then_inc(s["wout"], 16)
                n = 0
                for src, dst, ready in ((Qi, Qp, "q"), (Ki, Kp, "k")):
                    sp.wait_ge(s[ready], 1)
                    for h in range(NH):
                        c, r = divmod(h, 6)
                        sp.dma_start(dst[32 * (h % 4):32 * (h % 4) + DH, h // 4, :],
                                     src[DH * r:DH * r + DH, c, :]).then_inc(s["padded"], 16)
                        n += 16
                sp.wait_ge(s["padded"], n)

            @block.gpsimd
            def _(gp):
                gp.wait_ge(s["maxes"], 1)
                gp.partition_all_reduce(MX[:, 8:13], MX[:, 0:5], P, RMAX).then_inc(s["all"], 1)

            @block.vector
            def _(v):
                st = straight.on(v)
                sc = Scales(v, st, SC)
                st.did(v.memset(MX[:, 4:5], 0.0))
                v.wait_ge(s["wout"], 16)
                st.settle()
                v.tensor_reduce(MX[0:HC, 4:5], wf[:, :, :].rearrange("p c n -> p (c n)"), AX.X, ALU.max,
                                apply_absolute_value=True).then_inc(s["maxes"], 1)
                v.wait_ge(s["all"], 1)
                st.did(v.tensor_scalar(MX[:, 8:11], MX[:, 8:11], SC[:, S_WIN:S_WIN + 1], None, ALU.mult))
                st.settle()
                st.did(v.tensor_scalar(SC[:, S_Q:S_Q + 4], MX[:, 8:12], 1e-8, 1.0 / QMAX, ALU.max, ALU.mult))
                st.did(v.tensor_scalar(SC[:, S_WOUT:S_WOUT + 1], MX[:, 12:13], 1e-8, 1.0 / QMAX, ALU.max,
                                       ALU.mult))
                st.settle()
                st.did(v.reciprocal(SC[:, F_Q:F_Q + 3], SC[:, S_Q:S_Q + 3]))
                st.did(v.reciprocal(SC[:, F_W:F_W + 1], SC[:, S_WOUT:S_WOUT + 1]))
                st.settle()
                st.did(v.tensor_scalar(wf[:, :, :], wf[:, :, :], SC[0:HC, F_W:F_W + 1], MAGIC, ALU.mult,
                                       ALU.add))
                st.settle()
                st.did(v.tensor_scalar(wout[:, :, :], wf[:, :, :], -MAGIC, None, ALU.add))
                for X, Xi, f, ready in ((Q, Qi, F_Q, "q"), (K, Ki, F_K, "k"), (V, Vi, F_V, "v")):
                    n = X.shape[0] if X is not V else PP
                    st.did(v.tensor_scalar(X[0:n, :, :], X[0:n, :, :], SC[0:n, f:f + 1], MAGIC, ALU.mult,
                                           ALU.add))
                    st.settle()
                    v.tensor_scalar(Xi[0:n, :, :], X[0:n, :, :], -MAGIC, None, ALU.add).then_inc(s[ready], 1)
                st.did(v.memset(PS[:, :, :], 0.0))
                st.settle()


def score_matmuls(pe, PS, Qs, Ks, buf, half):
    for slot in range(2):
        for e in range(2):
            tok = slice(((half * 2 + slot) * 2 + e) * T, ((half * 2 + slot) * 2 + e + 1) * T)
            for c in range(3):
                for j in range(4):
                    col = slot * 3 * T + c * T
                    mm = pe.matmul(PS[64 * e:64 * e + T, 4 * half + j, col:col + T],
                                   Qs[32 * j:32 * j + DH, buf, c, tok], Ks[32 * j:32 * j + DH, buf, c, tok],
                                   start=True, stop=True, skip_group_check=True)
    return mm


def stage_qk(sp, Qp, Kp, Qs, Ks, g, buf, s):
    for src, dst in ((Qp, Qs), (Kp, Ks)):
        sp.dma_start(dst[:, buf, :, :], src[:, :, bass.ds(g * GT, GT)]).then_inc(s["staged%d" % buf], 16)


def score_maximum(nc, straight, passed, sem, sb_, PS, SC, Qp, Kp, Qs, Ks):
    scope = ExitStack()
    with scope:
        s = {n: sem("p4_" + n) for n in ("staged0", "staged1", "scores", "free", "loop_dve", "maxes",
                                         "all", "used")}
        m = sb_("m4", [P, 4], F32, scope)
        with nc.Block() as block:
            @block.sync
            def _(sp):
                for buf in range(2):
                    stage_qk(sp, Qp, Kp, Qs, Ks, buf, buf, s)
                with sp.Fori(1, NG // 2) as i:
                    for buf in range(2):
                        sp.wait_ge(s["used"], i * 2 + buf - 1)
                        stage_qk(sp, Qp, Kp, Qs, Ks, i * 2 + buf, buf, s)

            @block.tensor
            def _(pe):
                with pe.Fori(0, NG // 2) as i:
                    for buf in range(2):
                        pe.wait_ge(s["staged%d" % buf], i * 32 + 32)
                        for half in range(2):
                            mm = score_matmuls(pe, PS, Qs, Ks, buf, half)
                            if half == 0:
                                mm.then_inc(s["scores"], 1)
                            else:
                                mm.then_inc(s["scores"], 1)
                        pe.wait_ge(s["scores"], i * 4 + buf * 2 + 2)
                        pe.sem_inc(s["used"], 1)
                        pe.wait_ge(s["free"], i * 4 + buf * 2 + 2)

            @block.gpsimd
            def _(gp):
                gp.wait_ge(s["maxes"], 1)
                gp.partition_all_reduce(m[:, 3:4], m[:, 0:1], P, RMAX).then_inc(s["all"], 1)

            @block.vector
            def _(v):
                st = straight.on(v)
                st.did(v.memset(m[:, :], 0.0))
                st.settle()
                loop = Steps(v, s["loop_dve"], 4)
                with v.Fori(0, NG // 2) as i:
                    loop.turn(i)
                    for k in range(4):
                        v.wait_ge(s["scores"], i * 4 + k + 1)
                        h = k % 2
                        v.tensor_reduce(m[0:PP, 1 + h:2 + h], PS[0:PP, 4 * h:4 * h + 4, 0:6 * T], AX.XY, ALU.max,
                                        apply_absolute_value=True).then_inc(s["free"], 1)
                        v.wait_ge(s["free"], i * 4 + k + 1)
                        loop.did(v.tensor_tensor(m[:, 0:1], m[:, 0:1], m[:, 1 + h:2 + h], ALU.max))
                        loop.settle()
                    loop.end()
                v.memset(m[:, 1:2], 0.0).then_inc(s["maxes"], 1)
                v.wait_ge(s["all"], 1)
                sc = Scales(v, st, SC)
                sc.op(15, S_Q, SC[:, S_K:S_K + 1], 0.25, ALU.mult, ALU.mult)
                st.did(v.tensor_scalar(SC[:, S_SCORE:S_SCORE + 1], m[:, 3:4], SC[:, 15:16], 1e-8, ALU.mult,
                                       ALU.max))
                st.settle()
                sc.op(S_SCORE, S_SCORE, 1.0 / QMAX, None, ALU.mult)
                sc.inverse(16, S_SCORE)
                sc.op(16, 16, SC[:, 15:16], None, ALU.mult)
                st.did(v.memset(SC[:, 17:18], MAGIC))
                st.settle()


def softmax_rows(nc, straight, passed, sem, sb_, PS, SC, Qp, Kp, Qs, Ks, E, RS):
    scope = ExitStack()
    with scope:
        def sb(name, shape, dt=F32):
            return sb_(name, shape, dt, scope)

        s = {n: sem("p5_" + n) for n in ("staged0", "staged1", "scores", "free", "rowmax", "less",
                                         "exp", "sums", "maxes", "all", "used")}
        W = sb("W5", [P, 2, SETW])
        rm = sb("rm5", [P, 2, 2 * NH])
        m = sb("m5", [P, 2])
        with nc.Block() as block:
            @block.sync
            def _(sp):
                for buf in range(2):
                    stage_qk(sp, Qp, Kp, Qs, Ks, buf, buf, s)
                with sp.Fori(1, NG // 2) as i:
                    for buf in range(2):
                        sp.wait_ge(s["used"], i * 2 + buf - 1)
                        stage_qk(sp, Qp, Kp, Qs, Ks, i * 2 + buf, buf, s)

            @block.tensor
            def _(pe):
                with pe.Fori(0, NG // 2) as i:
                    for buf in range(2):
                        pe.wait_ge(s["staged%d" % buf], i * 32 + 32)
                        for half in range(2):
                            score_matmuls(pe, PS, Qs, Ks, buf, half).then_inc(s["scores"], 1)
                        pe.wait_ge(s["scores"], i * 4 + buf * 2 + 2)
                        pe.sem_inc(s["used"], 1)
                        pe.wait_ge(s["free"], i * 4 + buf * 2 + 2)

            @block.scalar
            def _(act):
                with act.Fori(0, NG // 2) as i:
                    for k in range(4):
                        h = k % 2
                        act.wait_ge(s["scores"], i * 4 + k + 1)
                        act.activation(W[0:PP, h, :].rearrange("p (k n) -> p k n", k=4),
                                       PS[0:PP, 4 * h:4 * h + 4, 0:6 * T], ACT.Identity,
                                       scale=SC[0:PP, 16:17], bias=SC[0:PP, 17:18]).then_inc(s["free"], 1)
                        act.wait_ge(s["less"], i * 4 + k + 1)
                        act.activation(E[0:PP, bass.ds(i * 4 + k, 1), :], W[0:PP, h:h + 1, :], ACT.Exp,
                                       scale=SC[0:PP, S_SCORE:S_SCORE + 1]).then_inc(s["exp"], 1)

            @block.gpsimd
            def _(gp):
                with gp.Fori(0, NG // 2) as i:
                    for k in range(4):
                        h = k % 2
                        gp.wait_ge(s["rowmax"], i * 4 + k + 1)
                        w = W[0:PP, h, :].rearrange("p (r n) -> p r n", n=T)
                        gp.tensor_tensor(out=w, in0=w, in1=bcast(rm[0:PP, h, :], T, 2), op=ALU.subtract
                                         ).then_inc(s["less"], 1)
                gp.wait_ge(s["maxes"], 1)
                gp.partition_all_reduce(m[:, 1:2], m[:, 0:1], P, RMAX).then_inc(s["all"], 1)

            @block.vector
            def _(v):
                with v.Fori(0, NG // 2) as i:
                    for k in range(4):
                        h = k % 2
                        v.wait_ge(s["free"], i * 4 + k + 1)
                        v.tensor_reduce(rm[0:PP, h, :], W[0:PP, h, :].rearrange("p (r n) -> p r n", n=T), AX.X,
                                        ALU.max).then_inc(s["rowmax"], 1)
                        v.wait_ge(s["exp"], i * 4 + k + 1)
                        seen(v, passed)
                        v.tensor_reduce(RS[0:PP, bass.ds(i * 4 + k, 1), :].rearrange("p a r -> p (a r)"),
                                        E[0:PP, bass.ds(i * 4 + k, 1), :].rearrange(
                                            "p a (r n) -> p (a r) n", n=T), AX.X, ALU.add).then_inc(s["sums"], 1)
                st = straight.on(v)
                sc = Scales(v, st, SC)
                st.did(v.memset(m[:, :], 0.0))
                v.wait_ge(s["sums"], 2 * NG)
                r = RS[0:PP, :, :].rearrange("p a r -> p (a r)")
                st.did(v.reciprocal(r, r))
                st.settle()
                v.tensor_reduce(m[0:PP, 0:1], r, AX.X, ALU.max).then_inc(s["maxes"], 1)
                v.wait_ge(s["all"], 1)
                st.did(v.tensor_scalar(SC[:, S_ATT:S_ATT + 1], m[:, 1:2], 1e-8, 1.0 / QMAX, ALU.max, ALU.mult))
                st.settle()
                sc.inverse(18, S_ATT)
                st.did(v.tensor_scalar(r, r, SC[0:PP, 18:19], None, ALU.mult))
                st.settle()


def context(nc, straight, passed, sem, sb_, PS, SC, identb, E, RS, Vi, CTX):
    scope = ExitStack()
    with scope:
        def sb(name, shape, dt=F32):
            return sb_(name, shape, dt, scope)

        s = {n: sem("p6_" + n) for n in ("staged", "used", "prod", "round", "ai", "turned", "at", "ctx",
                                         "ctx_in", "max", "maxes", "all", "free", "loop_dve")}
        W = sb("W6", [P, 2, SETW])
        Ai = sb("Ai", [P, 2, SETW], BF16)
        AT = sb("AT", [P, 4, 6 * PP], BF16)
        Vs = sb("Vs", [P, 2, 4, C], BF16)
        m = sb("m6", [P, 4])
        with nc.Block() as block:
            @block.sync
            def _(sp):
                def stage(g):
                    for r0, r1, q0, w in ((0, PP, 0, 0), (0, T, 64, 1), (64, PP, 0, 1)):
                        sp.dma_start(Vs[r0:r1, w, :, :], Vi[q0:q0 + r1 - r0, bass.ds(g * 4, 4), :]
                                     ).then_inc(s["staged"], 16)
                stage(0)
                with sp.Fori(1, NG) as g:
                    sp.wait_ge(s["ctx"], g * 1)
                    stage(g)

            @block.gpsimd
            def _(gp):
                with gp.Fori(0, NG) as g:
                    for h in range(2):
                        gp.wait_ge(s["round"], g * 2 + h + 1)
                        seen(gp, passed)
                        gp.tensor_scalar(Ai[0:PP, h, :], W[0:PP, h, :], -MAGIC, None, ALU.add
                                         ).then_inc(s["ai"], 1)
                gp.wait_ge(s["maxes"], 1)
                gp.partition_all_reduce(m[:, 2:3], m[:, 0:1], P, RMAX).then_inc(s["all"], 1)

            @block.tensor
            def _(pe):
                with pe.Fori(0, NG) as g:
                    for q in range(4):
                        h, slot = divmod(q, 2)
                        pe.wait_ge(s["ai"], g * 2 + h + 1)
                        seen(pe, passed)
                        pt = PS[:, q, :].bitcast(BF16)
                        for j in range(4):
                            for c in range(3):
                                o, k = 64 * (j % 2), (j // 2) * 3 + c
                                col = ((j * 2 + slot) * 3 + c) * T
                                mm = pe.transpose(pt[o:o + T, k * PP:(k + 1) * PP], Ai[0:PP, h, col:col + T],
                                                  identb[0:PP, 0:PP])
                        mm.then_inc(s["turned"], 1)
                    pe.wait_ge(s["staged"], g * 48 + 48)
                    for q in range(4):
                        pe.wait_ge(s["at"], g * 4 + q + 1)
                        seen(pe, passed)
                        for j in range(4):
                            for c in range(3):
                                for e in range(2):
                                    o, k, par = 64 * (j % 2), (j // 2) * 3 + c, j % 2
                                    hd = 4 * c + j
                                    mm = pe.matmul(
                                        PS[64 * e:64 * e + T, 4 + par, q * HC + k * DH:q * HC + (k + 1) * DH],
                                        AT[o:o + T, q, k * PP + 64 * e:k * PP + 64 * e + T],
                                        Vs[o:o + T, int(e != par), q, hd * DH:(hd + 1) * DH],
                                        start=True, stop=True, skip_group_check=True)
                    mm.then_inc(s["ctx"], 1)
                    pe.wait_ge(s["ctx_in"], g + 1)
                    pe.wait_ge(s["max"], g + 1)

            @block.scalar
            def _(act):
                with act.Fori(0, NG) as g:
                    for q in range(4):
                        act.wait_ge(s["turned"], g * 4 + q + 1)
                        act.activation(AT[0:PP, q, :], PS[0:PP, q, :].bitcast(BF16)[:, 0:6 * PP], ACT.Identity
                                       ).then_inc(s["at"], 1)
                    act.wait_ge(s["ctx"], g + 1)
                    for par in range(2):
                        act.activation(CTX[0:PP, bass.ds(g * 4, 4), par * HC:(par + 1) * HC],
                                       PS[0:PP, 4 + par, 0:4 * HC].rearrange("p (q n) -> p q n", q=4),
                                       ACT.Identity).then_inc(s["ctx_in" if par else "free"], 1)

            @block.vector
            def _(v):
                st = straight.on(v)
                st.did(v.memset(m[:, :], 0.0))
                st.settle()
                loop = Steps(v, s["loop_dve"], 1)
                with v.Fori(0, NG) as g:
                    loop.turn(g)
                    for h in range(2):
                        e = E[0:PP, bass.ds(g * 2 + h, 1), :].rearrange("p a (r n) -> p (a r) n", n=T)
                        r = RS[0:PP, bass.ds(g * 2 + h, 1), :].rearrange("p a r -> p (a r)")
                        v.tensor_tensor(W[0:PP, h, :].rearrange("p (r n) -> p r n", n=T), e, bcast(r, T, 2),
                                        ALU.mult).then_inc(s["prod"], 1)
                        v.wait_ge(s["prod"], g * 2 + h + 1)
                        v.tensor_scalar(W[0:PP, h, :], W[0:PP, h, :], MAGIC, None, ALU.add
                                        ).then_inc(s["round"], 1)
                    v.wait_ge(s["ctx_in"], g + 1)
                    v.tensor_reduce(m[0:PP, 1:2], PS[0:PP, 4:6, 0:4 * HC], AX.XY, ALU.max,
                                    apply_absolute_value=True).then_inc(s["max"], 1)
                    v.wait_ge(s["max"], g + 1)
                    loop.did(v.tensor_tensor(m[:, 0:1], m[:, 0:1], m[:, 1:2], ALU.max))
                    loop.settle()
                    loop.end()
                v.memset(m[:, 1:2], 0.0).then_inc(s["maxes"], 1)
                v.wait_ge(s["all"], 1)
                sc = Scales(v, st, SC)
                sc.op(15, S_ATT, SC[:, S_V:S_V + 1], None, ALU.mult)
                st.did(v.tensor_scalar(SC[:, S_CTX:S_CTX + 1], m[:, 2:3], SC[:, 15:16], 1e-8, ALU.mult, ALU.max))
                st.settle()
                sc.op(S_CTX, S_CTX, 1.0 / QMAX, None, ALU.mult)
                sc.inverse(16, S_CTX)
                sc.op(16, 16, SC[:, 15:16], None, ALU.mult)


def project_out(nc, straight, passed, sem, sb_, PS, SC, H, identb, norm, rsqrt, CTX, wout, Y, R):
    scope = ExitStack()
    with scope:
        def sb(name, shape, dt=F32):
            return sb_(name, shape, dt, scope)

        s = {n: sem("p7_" + n) for n in ("loop_dve", "cf", "ci", "turned", "cT", "y", "y_in", "max", "var",
                                         "rstd", "norm", "maxes", "all")}
        cf = sb("cf", [P, 4, C])
        Ci = sb("Ci", [P, 4, C], BF16)
        cT = sb("cT", [HC, 2, GT], BF16)
        hx = sb("hx", [P, 3, C])
        hn = sb("hn7", [P, 3, C])
        m = sb("m7", [P, 4])
        LOOP = 10
        with nc.Block() as block:
            @block.gpsimd
            def _(gp):
                with gp.Fori(0, NG) as g:
                    rsqrt(gp, s["var"], s["rstd"], g + 1)
                gp.wait_ge(s["maxes"], 1)
                gp.partition_all_reduce(m[:, 2:3], m[:, 0:1], P, RMAX).then_inc(s["all"], 1)

            @block.scalar
            def _(act):
                with act.Fori(0, NG) as g:
                    act.activation(cf[0:PP, :, :], CTX[0:PP, bass.ds(g * 4, 4), :], ACT.Identity,
                                   scale=SC[0:PP, 16:17], bias=SC[0:PP, 17:18]).then_inc(s["cf"], 1)
                    act.wait_ge(s["turned"], g + 1)
                    pt = PS[0:HC, 0, :].bitcast(BF16)[:, 0:8 * PP].rearrange("p (c q n) -> p c q n", c=2, q=4)
                    for c in range(2):
                        for t0, t1, d0 in ((0, TP, 0), (TP, T, P)):
                            for e in range(2):
                                n = t1 - t0
                                dst = cT[:, c, d0:d0 + GB * n].rearrange("p (q e t) -> p q e t", q=4, e=2)
                                act.activation(dst[:, :, e, :], pt[:, c, :, 64 * e + t0:64 * e + t1], ACT.Identity
                                               ).then_inc(s["cT"], 1)
                    act.wait_ge(s["y"], g + 1)
                    act.activation(Y[:, bass.ds(g * 3, 3), :],
                                   PS[:, 2:4, :].rearrange("p k (j c) -> p (k j) c", c=256)[:, 0:3, 0:C],
                                   ACT.Identity).then_inc(s["y_in"], 1)

            @block.tensor
            def _(pe):
                with pe.Fori(0, NG) as g:
                    pe.wait_ge(s["ci"], g + 1)
                    pt = PS[0:HC, 0, :].bitcast(BF16)
                    for c in range(2):
                        for q in range(4):
                            k = c * 4 + q
                            mm = pe.transpose(pt[:, k * PP:(k + 1) * PP], Ci[0:PP, q, c * HC:(c + 1) * HC],
                                              identb[0:PP, 0:PP])
                    mm.then_inc(s["turned"], 1)
                    pe.wait_ge(s["cT"], g * 8 + 8)
                    for j in range(3):
                        for c in range(2):
                            mm = pe.matmul(PS[:, 2 + j // 2, (j % 2) * 256:(j % 2) * 256 + C],
                                           cT[:, c, j * P:(j + 1) * P], wout[:, c, :], start=c == 0, stop=c == 1)
                    mm.then_inc(s["y"], 1)
                    pe.wait_ge(s["y_in"], g + 1)

            @block.vector
            def _(v):
                st = straight.on(v)
                sc = Scales(v, st, SC)
                st.did(v.memset(m[:, :], 0.0))
                st.did(v.reciprocal(SC[:, 19:20], SC[:, S_X:S_X + 1]))
                st.settle()
                loop = Steps(v, s["loop_dve"], LOOP)
                with v.Fori(0, NG) as g:
                    loop.turn(g)
                    v.wait_ge(s["cf"], g + 1)
                    v.tensor_scalar(Ci[0:PP, :, :], cf[0:PP, :, :], -MAGIC, None, ALU.add).then_inc(s["ci"], 1)
                    loop.did(v.tensor_scalar(hx[:, :, :], H[:, bass.ds(g * 3, 3), :], 1.0, None, ALU.mult))
                    loop.settle()
                    norm(v, loop, hx, hn, s["var"], s["rstd"], g + 1, s["norm"])
                    v.wait_ge(s["norm"], g * 3 + 3)
                    loop.did(v.tensor_scalar(hn[:, :, :], hn[:, :, :], SC[:, 19:20], MAGIC, ALU.mult, ALU.add))
                    loop.settle()
                    loop.did(v.tensor_scalar(R[:, bass.ds(g * 3, 3), :], hn[:, :, :], -MAGIC,
                                             SC[:, S_X:S_X + 1], ALU.add, ALU.mult))
                    v.wait_ge(s["y_in"], g + 1)
                    v.tensor_reduce(m[:, 1:2],
                                    PS[:, 2:4, :].rearrange("p k (j c) -> p (k j) c", c=256)[:, 0:3, 0:C],
                                    AX.XY, ALU.max, apply_absolute_value=True).then_inc(s["max"], 1)
                    v.wait_ge(s["max"], g + 1)
                    loop.did(v.tensor_tensor(m[:, 0:1], m[:, 0:1], m[:, 1:2], ALU.max))
                    loop.settle()
                    v.wait_ge(s["y_in"], g + 1)
                    loop.end()
                v.memset(m[:, 1:2], 0.0).then_inc(s["maxes"], 1)
                v.wait_ge(s["all"], 1)
                sc.op(15, S_CTX, SC[:, S_WOUT:S_WOUT + 1], None, ALU.mult)
                st.did(v.tensor_scalar(SC[:, S_Y:S_Y + 1], m[:, 2:3], SC[:, 15:16], 1e-8, ALU.mult, ALU.max))
                st.settle()
                sc.op(S_Y, S_Y, 1.0 / QMAX, None, ALU.mult)
                sc.inverse(16, S_Y)
                sc.op(16, 16, SC[:, 15:16], None, ALU.mult)


def batch_norm(nc, straight, passed, sem, sb_, PS, SC, H, Y, R):
    scope = ExitStack()
    with scope:
        def sb(name, shape, dt=F32):
            return sb_(name, shape, dt, scope)

        s = {n: sem("p8_" + n) for n in ("ones", "r", "mean", "centred", "square", "var", "vard", "pow",
                                         "maxes", "all", "pool")}
        ones = sb("ones8", [P, P])
        SQ = sb("SQ", [P, NT, C])
        vr = sb("vr", [P, C])
        nhalf = sb("nhalf8", [P, C])
        m = sb("m8", [P, 2])
        NQ = 4
        QT = NT // NQ
        with nc.Block() as block:
            @block.gpsimd
            def _(gp):
                gp.memset(ones[:, :], 1.0 / (B * T)).then_inc(s["ones"], 1)
                gp.memset(nhalf[:, :], -0.5).then_inc(s["pool"], 1)
                gp.wait_ge(s["pool"], 1)
                gp.wait_ge(s["vard"], 1)
                gp.tensor_tensor(out=vr[:, :], in0=vr[:, :], in1=nhalf[:, :], op=ALU.pow).then_inc(s["pow"], 1)
                gp.wait_ge(s["maxes"], 1)
                gp.partition_all_reduce(m[:, 1:2], m[:, 0:1], P, RMAX).then_inc(s["all"], 1)

            @block.scalar
            def _(act):
                for k in range(NQ):
                    act.wait_ge(s["centred"], k + 1)
                    act.activation(SQ[:, k * QT:(k + 1) * QT, :], R[:, k * QT:(k + 1) * QT, :], ACT.Square
                                   ).then_inc(s["square"], 1)

            @block.tensor
            def _(pe):
                pe.wait_ge(s["ones"], 1)
                for n, (src, ready, done) in enumerate(((R, "r", "mean"), (SQ, "square", "var"))):
                    for k in range(NT):
                        if k % QT == 0:
                            pe.wait_ge(s[ready], k // QT + 1)
                        mm = pe.matmul(PS[:, n, 0:C], ones[:, :], src[:, k, :], start=k == 0, stop=k == NT - 1)
                    mm.then_inc(s[done], 1)

            @block.vector
            def _(v):
                st = straight.on(v)
                sc = Scales(v, st, SC)
                quarters = [slice(k * QT, (k + 1) * QT) for k in range(NQ)]
                for q in quarters:
                    st.did(v.tensor_scalar(Y[:, q, :], Y[:, q, :], SC[:, 16:17], MAGIC, ALU.mult, ALU.add))
                    st.settle()
                    st.did(v.tensor_scalar(Y[:, q, :], Y[:, q, :], -MAGIC, SC[:, S_Y:S_Y + 1], ALU.add, ALU.mult))
                    st.settle()
                    v.tensor_tensor(R[:, q, :], R[:, q, :], Y[:, q, :], ALU.add).then_inc(s["r"], 1)
                v.wait_ge(s["mean"], 1)
                v.wait_ge(s["r"], NQ)
                for q in quarters:
                    v.tensor_tensor(R[:, q, :], R[:, q, :], bcast(PS[:, 0, 0:C], QT, 1), ALU.subtract
                                    ).then_inc(s["centred"], 1)
                v.wait_ge(s["var"], 1)
                v.tensor_scalar(vr[:, :], PS[:, 1, 0:C], EPS, None, ALU.add).then_inc(s["vard"], 1)
                v.wait_ge(s["pow"], 1)
                v.wait_ge(s["centred"], NQ)
                for q in quarters:
                    st.did(v.tensor_tensor(R[:, q, :], R[:, q, :], bcast(vr[:, :], QT, 1), ALU.mult))
                st.settle()
                v.tensor_reduce(m[:, 0:1], R[:, :, :], AX.XY, ALU.max, apply_absolute_value=True
                                ).then_inc(s["maxes"], 1)
                v.wait_ge(s["all"], 1)
                st.did(v.tensor_scalar(SC[:, S_RN:S_RN + 1], m[:, 1:2], 1e-8, 1.0 / QMAX, ALU.max, ALU.mult))
                st.settle()
                sc.inverse(16, S_RN)
                st.did(v.tensor_scalar(R[:, :, :], R[:, :, :], SC[:, 16:17], MAGIC, ALU.mult, ALU.add))
                st.settle()
                st.did(v.tensor_scalar(R[:, :, :], R[:, :, :], -MAGIC, SC[:, S_RN:S_RN + 1], ALU.add, ALU.mult))
                st.settle()
                st.did(v.tensor_tensor(H[:, :, :], H[:, :, :], R[:, :, :], ALU.add))
                st.settle()


def route(nc, straight, passed, a, sem, sb_, PS, H, ident, norm, rsqrt, XT, G):
    scope = ExitStack()
    with scope:
        def sb(name, shape, dt=F32):
            return sb_(name, shape, dt, scope)

        s = {n: sem("p9_" + n) for n in ("weights", "var", "rstd", "norm", "turned", "xs", "kept", "logits",
                                         "shifted", "exp", "loop_dve", "part", "importance")}
        rw = sb("rw", [HC, 2, NE])
        iota8 = sb("iota8", [P, NE])
        hx = sb("hx9", [P, 3, C])
        hn = sb("hn9", [P, 3, C])
        xs = sb("xs9", [HC, 2, GT])
        lg = sb("lg", [P, 3, NE])
        ex = sb("ex9", [P, 3, NE])
        t3 = sb("t3", [P, 4, 3])
        PR = sb("PR", [P, NT, NE])
        top = sb("top", [P, NT, 8])
        idx = sb("idx", [P, NT, 8], U32)
        idf = sb("idf", [P, NT, 8])
        one = sb("one9", [P, 2, NT, NE])
        imp = sb("imp", [P, 2, NE])
        den = sb("den9", [P, NT])
        LOOP = 13
        with nc.Block() as block:
            @block.sync
            def _(sp):
                sp.dma_start(rw[:, :, :], a["router"]).then_inc(s["weights"], 16)
                sp.dma_start(iota8[:, :], a["iota8"].to_broadcast([P, NE])).then_inc(s["weights"], 16)

            @block.gpsimd
            def _(gp):
                with gp.Fori(0, NG) as g:
                    rsqrt(gp, s["var"], s["rstd"], g + 1)
                    gp.wait_ge(s["xs"], g * 2 + 2)
                    seen(gp, passed)
                    gp.tensor_copy(XT[:, :, bass.ds(g * GT, GT)], xs[:, :, :]).then_inc(s["kept"], 1)
                gp.wait_ge(s["part"], 1)
                gp.partition_all_reduce(imp[:, 1, :], imp[:, 0, :], P, RADD).then_inc(s["importance"], 1)

            @block.tensor
            def _(pe):
                pe.wait_ge(s["weights"], 32)
                with pe.Fori(0, NG) as g:
                    pe.wait_ge(s["norm"], g * 3 + 3)
                    for c in range(2):
                        for j in range(3):
                            mm = pe.transpose(PS[0:HC, c, j * P:(j + 1) * P], hn[:, j, c * HC:(c + 1) * HC],
                                              ident[:, :])
                    mm.then_inc(s["turned"], 1)
                    pe.wait_ge(s["xs"], g * 2 + 2)
                    for j in range(3):
                        for c in range(2):
                            mm = pe.matmul(PS[:, 2, j * NE:(j + 1) * NE], xs[:, c, j * P:(j + 1) * P], rw[:, c, :],
                                           start=c == 0, stop=c == 1)
                    mm.then_inc(s["logits"], 1)

            @block.scalar
            def _(act):
                with act.Fori(0, NG) as g:
                    act.wait_ge(s["turned"], g + 1)
                    for c in range(2):
                        act.activation(xs[:, c, :], PS[0:HC, c, 0:GT], ACT.Identity).then_inc(s["xs"], 1)
                    act.wait_ge(s["shifted"], g + 1)
                    act.activation(ex[:, :, :], lg[:, :, :], ACT.Exp).then_inc(s["exp"], 1)
                    act.wait_ge(s["kept"], g + 1)

            @block.vector
            def _(v):
                loop = Steps(v, s["loop_dve"], LOOP)
                with v.Fori(0, NG) as g:
                    loop.turn(g)
                    loop.did(v.tensor_scalar(hx[:, :, :], H[:, bass.ds(g * 3, 3), :], 1.0, None, ALU.mult))
                    loop.settle()
                    norm(v, loop, hx, hn, s["var"], s["rstd"], g + 1, s["norm"])
                    v.wait_ge(s["logits"], g + 1)
                    z = PS[:, 2, 0:3 * NE].rearrange("p (j e) -> p j e", e=NE)
                    loop.did(v.tensor_reduce(t3[:, 0, :], z, AX.X, ALU.max))
                    loop.settle()
                    v.tensor_tensor(lg[:, :, :], z, bcast(t3[:, 0, :], NE, 2), ALU.subtract
                                    ).then_inc(s["shifted"], 1)
                    v.wait_ge(s["exp"], g + 1)
                    loop.did(v.tensor_reduce(t3[:, 1, :], ex[:, :, :], AX.X, ALU.add))
                    loop.settle()
                    loop.did(v.reciprocal(t3[:, 2, :], t3[:, 1, :]))
                    loop.settle()
                    loop.did(v.tensor_tensor(PR[:, bass.ds(g * 3, 3), :], ex[:, :, :], bcast(t3[:, 2, :], NE, 2),
                                             ALU.mult))
                    loop.settle()
                    v.wait_ge(s["norm"], g * 3 + 3)
                    loop.did(v.memset(t3[:, 3, 0:1], 0.0))
                    loop.did(v.memset(t3[:, 3, 1:2], 0.0))
                    loop.end()
                st = straight.on(v)
                st.did(v.memset(idf[:, 0, 0:1], 0.0))
                v.wait_ge(s["loop_dve"], LOOP * NG)
                v.tensor_reduce(imp[:, 0, :], PR[:, :, :].rearrange("p t e -> p e t"), AX.X, ALU.add
                                ).then_inc(s["part"], 1)
                for t in range(NT):
                    st.did(v.max(top[:, t, :], PR[:, t, :]))
                st.settle()
                for t in range(NT):
                    st.did(v.max_index(idx[:, t, :], top[:, t, :], PR[:, t, :]))
                st.settle()
                st.did(v.tensor_copy(idf[:, :, :], idx[:, :, :]))
                v.wait_ge(s["importance"], 1)
                st.did(v.tensor_scalar(imp[:, 0, :], imp[:, 1, :], -1.0, 1.0 - 0.9, ALU.add, ALU.mult))
                st.settle()
                st.did(v.tensor_scalar(imp[:, 0, :], imp[:, 0, :], 1.0, 0.01, ALU.add, ALU.add))
                st.settle()
                st.did(v.reciprocal(imp[:, 1, :], imp[:, 0, :]))
                v.wait_ge(s["weights"], 32)
                for k in range(2):
                    st.did(v.tensor_tensor(one[:, k, :, :], bcast(iota8[:, :], NT, 1),
                                           idf[:, :, k:k + 1].broadcast_to([P, NT, NE]), ALU.is_equal))
                st.settle()
                st.did(v.tensor_tensor(one[:, 0, :, :], one[:, 0, :, :], one[:, 1, :, :], ALU.add))
                st.did(v.tensor_tensor(PR[:, :, :], PR[:, :, :], bcast(imp[:, 1, :], NT, 1), ALU.mult))
                st.settle()
                st.did(v.tensor_tensor(PR[:, :, :], PR[:, :, :], one[:, 0, :, :], ALU.mult))
                st.settle()
                st.did(v.tensor_reduce(den[:, :], PR[:, :, :], AX.X, ALU.add))
                st.settle()
                st.did(v.reciprocal(den[:, :], den[:, :]))
                st.settle()
                st.did(v.tensor_tensor(G[:, :, :], PR[:, :, :], bcast(den[:, :], NE, 2), ALU.mult))
                st.settle()


def experts(nc, straight, passed, a, sem, sb_, PS, H, XT, G):
    scope = ExitStack()
    with scope:
        def sb(name, shape, dt=F32):
            return sb_(name, shape, dt, scope)

        s = {n: sem("p10_" + n) for n in ("w0", "w1", "up", "silu", "down", "acc", "gates")}
        w1s = sb("w1s", [HC, 2, 2, ID])
        w2s = sb("w2s", [P, 2, 4, C])
        hb = sb("hb", [P, 2, 4, 512])
        Ge = sb("Ge", [P, 2, NT])
        NB = B * T // 512
        with nc.Block() as block:
            @block.sync
            def _(sp):
                def load(e, buf):
                    sp.dma_start(w1s[:, buf, :, :], a["w1"][bass.ds(e, 1)].rearrange("e p c n -> p (e c) n")
                                 ).then_inc(s["w%d" % buf], 16)
                    sp.dma_start(w2s[:, buf, :, :], a["w2"][bass.ds(e, 1)].rearrange("e p c n -> p (e c) n")
                                 ).then_inc(s["w%d" % buf], 16)
                load(0, 0)
                load(1, 1)
                with sp.Fori(1, NE // 2) as i:
                    for buf in range(2):
                        sp.wait_ge(s["down"], (i * 2 + buf - 1) * NB)
                        load(i * 2 + buf, buf)

            @block.tensor
            def _(pe):
                with pe.Fori(0, NE // 2) as i:
                    for buf in range(2):
                        e = i * 2 + buf
                        pe.wait_ge(s["w%d" % buf], i * 32 + 32)

                        def up(b):
                            for m in range(4):
                                if b:
                                    pe.wait_ge(s["silu"], (e * NB + b - 1) * 4 + m + 1)
                                for c in range(2):
                                    mm = pe.matmul(PS[:, m, :], w1s[:, buf, c, m * P:(m + 1) * P],
                                                   XT[:, c, b * 512:(b + 1) * 512], start=c == 0, stop=c == 1)
                                mm.then_inc(s["up"], 1)

                        def down(b):
                            pe.wait_ge(s["silu"], (e * NB + b + 1) * 4)
                            if b >= 2:
                                pe.wait_ge(s["acc"], e * NB + b - 1)
                            for t in range(4):
                                for m in range(4):
                                    mm = pe.matmul(PS[:, 4 + 2 * (b % 2) + t // 2, (t % 2) * 256:(t % 2) * 256 + C],
                                                   hb[:, b % 2, m, t * P:(t + 1) * P], w2s[:, buf, m, :],
                                                   start=m == 0, stop=m == 3)
                            mm.then_inc(s["down"], 1)

                        up(0)
                        for b in range(1, NB):
                            up(b)
                            down(b - 1)
                        down(NB - 1)
                        pe.wait_ge(s["acc"], (e + 1) * NB)

            @block.scalar
            def _(act):
                with act.Fori(0, NE // 2) as i:
                    for buf in range(2):
                        e = i * 2 + buf
                        for b in range(NB):
                            for m in range(4):
                                act.wait_ge(s["up"], (e * NB + b) * 4 + m + 1)
                                if b >= 2 and m == 0:
                                    act.wait_ge(s["down"], e * NB + b - 1)
                                act.activation(hb[:, b % 2, m, :], PS[:, m, :], ACT.Silu).then_inc(s["silu"], 1)
                        act.wait_ge(s["down"], (e + 1) * NB)

            @block.vector
            def _(v):
                with v.Fori(0, NE // 2) as i:
                    for buf in range(2):
                        e = i * 2 + buf
                        v.tensor_scalar(Ge[:, buf, :].unsqueeze(2), G[:, :, bass.ds(e, 1)], 1.0, None, ALU.mult
                                        ).then_inc(s["gates"], 1)
                        v.wait_ge(s["gates"], e + 1)
                        for b in range(NB):
                            v.wait_ge(s["down"], e * NB + b + 1)
                            for t in range(4):
                                k = b * 4 + t
                                ins = v.scalar_tensor_tensor(
                                    H[:, k, :], PS[:, 4 + 2 * (b % 2) + t // 2, (t % 2) * 256:(t % 2) * 256 + C],
                                    Ge[:, buf, k:k + 1], H[:, k, :], ALU.mult, ALU.add)
                            ins.then_inc(s["acc"], 1)
                        v.wait_ge(s["acc"], (e + 1) * NB)


def nc_out(nc, sem, H, out):
    stored = sem("stored")
    with nc.Block() as block:
        @block.sync
        def _(sp):
            sp.dma_start(out[:, 0:NT // 2, :], H[:, 0:NT // 2, :]).then_inc(stored, 16)
            sp.dma_start(out[:, NT // 2:, :], H[:, NT // 2:, :]).then_inc(stored, 16)
            sp.wait_ge(stored, 32)


def embed_and_mix(nc, straight, passed, a, sem, sb_, PS, H, ident, identb, neghalf, norm, rsqrt):
    scope = ExitStack()
    with scope:
        def sb(name, shape, dt=F32):
            return sb_(name, shape, dt, scope)

        px = sb("px", [P, KC, P])
        tb = sb("tb", [P, 2, C])
        cw = sb("cw", [P, KC, C])
        pos = sb("pos", [P, C])
        cb = sb("cb", [P, C])
        lnv = sb("lnv", [HC, 4, 2])
        wkvr = sb("wkvr", [HC, 2, 3, C])
        wo = sb("wo", [P, 2, C])
        wkf = sb("wkf", [HC, 2, HID])
        wrf = sb("wrf", [HC, 2, C])
        wvf = sb("wvf", [P, HCH, C])
        dec = sb("dec", [P, 2, 2])
        Wf = sb("Wf", [P, 2 * ROWS, TS])
        Uf = sb("Uf", [P, ROWS, T])
        hc = sb("hc", [P, 3, C])
        x0 = sb("x0", [P, 3, C])
        hn = sb("hn", [P, 3, C])
        hT = sb("hT", [HC, 2, GT])
        KK = sb("KK", [P, 2 * ROWS, TS])
        VV = sb("VV", [P, 2 * ROWS, TS])
        SR = sb("SR", [P, ROWS, T])
        M = sb("M", [P, 1 + 2 * ROWS * TS])
        A = sb("A", [P, 1 + 2 * ROWS * TS])
        Bd = sb("Bd", [P, 1 + 2 * ROWS * TS])
        E1 = sb("E1", [P, 2 * ROWS, TS])
        E2 = sb("E2", [P, 2 * ROWS, TS])
        EV = sb("EV", [P, 2 * ROWS, TS])
        EX = sb("EX", [P, 3, ROWS, T])
        MM = sb("MM", [P, ROWS, T])
        N1 = sb("N1", [P, 3, ROWS, T])
        D1 = sb("D1", [P, 2, ROWS, T])
        YP = sb("YP", [P, ROWS, TP])
        YX = sb("YX", [P, ROWS, TX])
        kf = sb("kf", [P, HCH, GT])
        hn2 = sb("hn2a", [P, 3, C])
        hT2 = sb("hT2", [HC, 2, GT])
        xh = sb("xh", [P, 3, C])
        x1 = sb("x1", [P, 3, C])
        gate = sb("gate1", [P, 3, C])
        ff = sb("ff1", [P, 3, C])

        psT = PS[:, 0:2, :]
        psK, psV, psR = PS[:, 2:4, :], PS[:, 4:6, :], PS[:, 6:8, :]

        def rows(ps):
            return ps.rearrange("p k (r t) -> p (k r) t", t=64)

        def flat(ap):
            return ap.rearrange("p r t -> p (r t)")

        def before(buf):
            v = buf[:, 1:1 + 2 * ROWS * TS].rearrange("p (r t) -> p r t", t=TS)
            return v[:, 0:ROWS, 0:T], v[:, ROWS:2 * ROWS, T - 1::-1]

        s = {n: sem("p1_" + n) for n in (
            "weights", "consts", "setup", "inputs", "embedded", "text_taken", "var", "rstd",
            "norm1", "turned1", "hT", "kvr", "k_in", "v_in", "r_in", "m", "d2", "e1", "e2", "ev", "ku", "mm",
            "ex", "dpart", "y", "attn", "norm2", "turned2", "hT2", "up", "relu", "gatemm", "gate", "down",
            "pool", "relu0", "done", "loop_dve", "back_dve", "var2", "rstd2", "hc_free", "b_scan", "a_scan")}
        NW = 19
        FRONT_DVE, BACK_DVE = 30, 8

        with nc.Block() as block:
            @block.sync
            def _(sp):
                def load(dst, src):
                    sp.dma_start(dst, src).then_inc(s["weights"], 16)
                for k in range(GB):
                    load(pos[TP * k:TP * (k + 1), :], a["pos"])
                load(cb[:, :], a["conv_b"].to_broadcast([P, C]))
                load(cw[:, :, :], a["conv_w"])
                load(lnv[:, :, :], a["ln"])
                load(wkvr[:, :, :, :], a["w_kvr"])
                load(dec[:, :, :], a["decfirst"])
                load(wo[:, 0, :], a["Wo"][0:P, :])
                load(wo[0:64, 1, :], a["Wo"][P:C, :])
                load(wo[64:P, 1, :], a["Wo"][P:C, :])
                sp.dma_start(px[:, :, :], a["patches"][0]).then_inc(s["inputs"], 16)
                sp.dma_start(tb[:, :, :], a["text"][0]).then_inc(s["inputs"], 16)
                with sp.Fori(1, NG) as g:
                    sp.wait_ge(s["embedded"], g)
                    sp.wait_ge(s["text_taken"], g)
                    sp.dma_start(px[:, :, :], a["patches"][bass.ds(g, 1)].rearrange("g p k m -> p (g k) m")
                                 ).then_inc(s["inputs"], 16)
                    sp.dma_start(tb[:, :, :], a["text"][bass.ds(g, 1)].rearrange("g p j c -> p (g j) c")
                                 ).then_inc(s["inputs"], 16)

            @block.gpsimd
            def _(gp):
                st = Steps(gp, s["pool"])
                st.did(gp.memset(ident[:, :], 0.0))
                st.did(gp.memset(identb[:, :], 0.0))
                st.did(gp.memset(neghalf[:, :], -0.5))
                st.did(gp.memset(KK[:, :, 0:1], NEG))
                st.did(gp.memset(VV[:, :, 0:1], 0.0))
                st.settle()
                for m in (ident, identb):
                    st.did(gp.affine_select(out=m[:, :], in_=m[:, :], compare_op=ALU.not_equal, fill=1.0,
                                            base=0, pattern=[[-1, P]], channel_multiplier=1))
                st.settle()
                st.did(gp.memset(A[:, 0:1], 0.0))
                st.did(gp.memset(Bd[:, 0:1], 0.0))
                st.settle()
                gp.memset(M[:, 0:1], 0.0).then_inc(s["consts"], 1)

                def front(g):
                    gp.wait_ge(s["inputs"], g * 32 + 32)
                    seen(gp, passed)
                    gp.tensor_copy(hc[:, 1:3, :], tb[:, :, :]).then_inc(s["text_taken"], 1)
                    rsqrt(gp, s["var"], s["rstd"], g * 2 + 1)
                    rsqrt(gp, s["var"], s["rstd"], g * 2 + 2)
                    gp.wait_ge(s["m"], g + 1)
                    gp.wait_ge(s["setup"], 1)
                    gp.tensor_tensor(out=flat(E2[:, :, :]), in0=flat(KK[:, :, :]),
                                     in1=M[:, 1:1 + 2 * ROWS * TS], op=ALU.subtract).then_inc(s["d2"], 1)
                    gp.tensor_tensor(out=EX[:, 2, :, :], in0=KK[:, 0:ROWS, 1:TS], in1=Uf[:, :, :],
                                     op=ALU.add).then_inc(s["ku"], 1)
                    gp.wait_ge(s["e2"], g + 1)
                    gp.tensor_tensor(out=flat(EV[:, :, :]), in0=flat(E2[:, :, :]), in1=flat(VV[:, :, :]),
                                     op=ALU.mult).then_inc(s["ev"], 1)
                    gp.wait_ge(s["ex"], g + 1)
                    gp.wait_ge(s["b_scan"], g + 1)
                    bf, bb = before(Bd)
                    gp.tensor_tensor(out=D1[:, 0, :, :], in0=EX[:, 0, :, :], in1=bf, op=ALU.mult
                                     ).then_inc(s["dpart"], 1)
                    gp.tensor_tensor(out=D1[:, 1, :, :], in0=EX[:, 1, :, :], in1=bb, op=ALU.mult
                                     ).then_inc(s["dpart"], 1)

                front(0)
                with gp.Fori(0, NG - 1) as g:
                    rsqrt(gp, s["var2"], s["rstd2"], g + 1)
                    gp.wait_ge(s["hc_free"], g + 1)
                    front(g + 1)
                rsqrt(gp, s["var2"], s["rstd2"], NG)

            @block.tensor
            def _(pe):
                pe.wait_ge(s["weights"], 16 * NW)
                pe.wait_ge(s["consts"], 1)

                def turn(src, ready, turned):
                    pe.wait_ge(*ready)
                    for c in range(2):
                        for j in range(3):
                            mm = pe.transpose(psT[0:HC, c, j * P:(j + 1) * P],
                                              src[:, j, c * HC:(c + 1) * HC], ident[:, :])
                    mm.then_inc(turned, 1)

                def front(g):
                    pe.wait_ge(s["inputs"], g * 32 + 32)
                    for k in range(KC):
                        mm = pe.matmul(psR[:, 0, 0:C], px[:, k, :], cw[:, k, :], start=k == 0, stop=k == KC - 1)
                    mm.then_inc(s["embedded"], 1)

                    turn(hn, (s["norm1"], g * 3 + 3), s["turned1"])
                    pe.wait_ge(s["hT"], g * 4 + 4)
                    for w, ps in enumerate((psK, psV, psR)):
                        for half in range(2):
                            tok = slice(half * GT // 2, (half + 1) * GT // 2)
                            r = rows(ps)
                            for c in range(2):
                                pe.matmul(r[:, half * 4:half * 4 + 4, 0:T], wkvr[:, c, w, 0:P], hT[:, c, tok],
                                          start=c == 0, stop=c == 1)
                            for c in range(2):
                                mm = pe.matmul(r[64 * half:64 * half + 64, GB:GB + 4, 0:T],
                                               wkvr[:, c, w, P:C], hT[:, c, tok], start=c == 0, stop=c == 1)
                        mm.then_inc(s["kvr"], 1)

                def project(g):
                    pe.wait_ge(s["y"], g * 2 + 2)
                    for j, (Y, r0, nr) in enumerate(((YP, 0, 8), (YX, 0, 4), (YX, 4, 4))):
                        Y = Y[:, :, :]
                        up = Y[:, r0:r0 + nr, :].rearrange("p r t -> p (r t)")
                        low = Y[:, GB:ROWS, :].rearrange("p r t -> p (r t)")
                        o = psT[:, j // 2, (j % 2) * 256:(j % 2) * 256 + C]
                        pe.matmul(o, up, wo[:, 0, :], start=True, stop=False,
                                  skip_group_check=True)
                        if j == 0:
                            for q in (0, 64):
                                mm = pe.matmul(o[q:q + 64, :], low[q:q + 64, :], wo[q:q + 64, 1, :],
                                               start=False, stop=True, skip_group_check=True)
                        else:
                            q = 64 * (j - 1)
                            mm = pe.matmul(o, low[q:q + 64, :], wo[q:q + 64, 1, :],
                                           start=False, stop=True, skip_group_check=True)
                    mm.then_inc(s["attn"], 1)

                def channel_mix(g, last=False):
                    turn(hn2, (s["norm2"], g * 3 + 3), s["turned2"])
                    pe.wait_ge(s["hT2"], g * 2 + 2)
                    for m in range(HCH):
                        if not last and m % 2 == 0:
                            got, n = (("k_in", 2), ("v_in", 2), ("r_in", 1))[m // 2]
                            pe.wait_ge(s[got], (g + 2) * n)
                        for c in range(2):
                            mm = pe.matmul(PS[:, 2 + m, 0:GT], wkf[:, c, m * P:(m + 1) * P], hT2[:, c, :],
                                           start=c == 0, stop=c == 1)
                        mm.then_inc(s["up"], 1)
                    for j in range(3):
                        for c in range(2):
                            mm = pe.matmul(psT[:, j // 2, (j % 2) * 256:(j % 2) * 256 + C],
                                           hT2[:, c, j * P:(j + 1) * P], wrf[:, c, :], start=c == 0, stop=c == 1)
                    mm.then_inc(s["gatemm"], 1)
                    pe.wait_ge(s["relu"], g * HCH + HCH)
                    for j in range(3):
                        for m in range(HCH):
                            mm = pe.matmul(psK[:, j // 2, (j % 2) * 256:(j % 2) * 256 + C],
                                           kf[:, m, j * P:(j + 1) * P], wvf[:, m, :],
                                           start=m == 0, stop=m == HCH - 1)
                    mm.then_inc(s["down"], 1)
                    pe.wait_ge(s["gate"], g + 1)

                front(0)
                with pe.Fori(0, NG - 1) as g:
                    project(g)
                    front(g + 1)
                    channel_mix(g)
                project(NG - 1)
                channel_mix(NG - 1, last=True)

            def tiles(ps):
                return ps.rearrange("p k (j c) -> p (k j) c", c=256)[:, 0:3, 0:C]

            @block.scalar
            def _(act):
                def load(dst, src):
                    act.dma_start(dst, src).then_inc(s["weights"], 16)
                load(wkf[:, :, :], a["Wk_f"])
                load(wrf[:, :, :], a["Wr_f"])
                load(wvf[:, :, :], a["Wv_f"])
                act.wait_ge(s["weights"], 16 * NW)
                act.wait_ge(s["consts"], 1)

                def front(g):
                    act.wait_ge(s["turned1"], g + 1)
                    for c in range(2):
                        for j0, j1, t0, t1 in ((0, P, 0, TP), (P, GT, TP, T)):
                            act.activation(hT[:, c, :].rearrange("p (b t) -> p b t", t=T)[:, :, t0:t1],
                                           psT[0:HC, c, j0:j1].rearrange("p (b t) -> p b t", t=t1 - t0),
                                           ACT.Identity, bias=lnv[:, 1, c:c + 1], scale=lnv[:, 0, c:c + 1]
                                           ).then_inc(s["hT"], 1)
                    for w, (ps, dst, got) in enumerate(((psK, KK, "k_in"), (psV, VV, "v_in"))):
                        act.wait_ge(s["kvr"], g * 3 + w + 1)
                        r = rows(ps)[:, 0:ROWS, 0:T]
                        act.activation(dst[:, 0:ROWS, 1:TS], r, ACT.Identity).then_inc(s[got], 1)
                        act.activation(dst[:, ROWS:2 * ROWS, 1:TS], rows(ps)[:, 0:ROWS, T - 1::-1],
                                       ACT.Identity).then_inc(s[got], 1)
                    act.wait_ge(s["kvr"], g * 3 + 3)
                    act.activation(SR[:, :, :], rows(psR)[:, 0:ROWS, 0:T], ACT.Tanh, scale=0.5
                                   ).then_inc(s["r_in"], 1)

                def decays(g):
                    act.wait_ge(s["d2"], g + 1)
                    act.activation(flat(E2[:, :, :]), flat(E2[:, :, :]), ACT.Exp).then_inc(s["e2"], 1)
                    act.wait_ge(s["e1"], g * 2 + 1)
                    act.activation(flat(E1[:, :, :]), flat(E1[:, :, :]), ACT.Exp).then_inc(s["e1"], 1)

                def shares(g):
                    act.wait_ge(s["mm"], g + 1)
                    act.activation(EX[:, :, :, :].rearrange("p k r t -> p (k r t)"),
                                   EX[:, :, :, :].rearrange("p k r t -> p (k r t)"), ACT.Exp
                                   ).then_inc(s["ex"], 1)

                def turned(g):
                    act.wait_ge(s["turned2"], g + 1)
                    for c in range(2):
                        act.activation(hT2[:, c, :], psT[0:HC, c, 0:GT], ACT.Identity, bias=lnv[:, 3, c:c + 1],
                                       scale=lnv[:, 2, c:c + 1]).then_inc(s["hT2"], 1)

                def relu_squared(g, ms):
                    for m in ms:
                        act.wait_ge(s["up"], g * HCH + m + 1)
                        act.activation(kf[:, m, :], PS[:, 2 + m, 0:GT], ACT.Relu).then_inc(s["relu0"], 1)
                        act.wait_ge(s["relu0"], g * HCH + m + 1)
                        act.activation(kf[:, m, :], kf[:, m, :], ACT.Square).then_inc(s["relu"], 1)

                def gates(g):
                    act.wait_ge(s["gatemm"], g + 1)
                    act.activation(gate[:, :, :], tiles(psT), ACT.Tanh, scale=0.5).then_inc(s["gate"], 1)

                front(0)
                decays(0)
                shares(0)
                with act.Fori(0, NG - 1) as g:
                    front(g + 1)
                    turned(g)
                    decays(g + 1)
                    relu_squared(g, (0, 1, 2))
                    shares(g + 1)
                    relu_squared(g, (3, 4, 5))
                    gates(g)
                turned(NG - 1)
                relu_squared(NG - 1, range(HCH))
                gates(NG - 1)

            @block.vector
            def _(v):
                st = straight.on(v)
                st.did(v.memset(Wf[:, :, :], 0.0))
                st.did(v.memset(Uf[:, :, :], 0.0))
                v.wait_ge(s["weights"], 16 * NW)
                st.settle()
                for k, (r0, r1) in enumerate(((0, GB), (GB, ROWS))):
                    for d in range(2):
                        st.did(v.tensor_scalar(Wf[:, d * ROWS + r0:d * ROWS + r1, :],
                                               Wf[:, d * ROWS + r0:d * ROWS + r1, :], dec[:, 0, k:k + 1], 1.0 / T,
                                               ALU.add, ALU.mult))
                    st.did(v.tensor_scalar(Uf[:, r0:r1, :], Uf[:, r0:r1, :], dec[:, 1, k:k + 1], 1.0 / T,
                                           ALU.add, ALU.mult))
                st.did(v.tensor_tensor(pos[:, :], pos[:, :], cb[:, :], ALU.add))
                st.settle()
                v.wait_ge(s["consts"], 1)
                v.memset(Wf[:, :, 0:1], 3 * NEG).then_inc(s["setup"], 1)
                v.wait_ge(s["setup"], 1)
                loop = Steps(v, s["loop_dve"], FRONT_DVE)
                back = Steps(v, s["back_dve"], BACK_DVE)

                def front(g):
                    loop.turn(g)
                    v.wait_ge(s["embedded"], g + 1)
                    loop.did(v.tensor_tensor(hc[:, 0, :], psR[:, 0, 0:C], pos[:, :], ALU.add))
                    loop.settle()
                    v.wait_ge(s["text_taken"], g + 1)
                    norm(v, loop, hc, x0, s["var"], s["rstd"], g * 2 + 1)
                    loop.settle()
                    norm(v, loop, x0, hn, s["var"], s["rstd"], g * 2 + 2, s["norm1"])
                    v.wait_ge(s["k_in"], g * 2 + 2)
                    v.tensor_tensor_scan(M[:, 1:1 + 2 * ROWS * TS], flat(Wf[:, :, :]), flat(KK[:, :, :]), NEG,
                                         ALU.add, ALU.max).then_inc(s["m"], 1)
                    v.wait_ge(s["m"], g + 1)
                    loop.did(v.tensor_tensor(flat(E1[:, :, :]), M[:, 0:2 * ROWS * TS], flat(Wf[:, :, :]), ALU.add))
                    loop.settle()
                    v.tensor_tensor(flat(E1[:, :, :]), flat(E1[:, :, :]), M[:, 1:1 + 2 * ROWS * TS],
                                    ALU.subtract).then_inc(s["e1"], 1)
                    mf, mb = before(M)
                    loop.did(v.tensor_tensor(MM[:, :, :], mf, mb, ALU.max))
                    v.wait_ge(s["ku"], g + 1)
                    loop.settle()
                    loop.did(v.tensor_tensor(MM[:, :, :], MM[:, :, :], EX[:, 2, :, :], ALU.max))
                    loop.settle()
                    loop.did(v.tensor_tensor(EX[:, 0, :, :], mf, MM[:, :, :], ALU.subtract))
                    loop.did(v.tensor_tensor(EX[:, 1, :, :], mb, MM[:, :, :], ALU.subtract))
                    v.tensor_tensor(EX[:, 2, :, :], EX[:, 2, :, :], MM[:, :, :], ALU.subtract
                                    ).then_inc(s["mm"], 1)
                    v.wait_ge(s["e1"], g * 2 + 2)
                    v.wait_ge(s["e2"], g + 1)
                    v.tensor_tensor_scan(Bd[:, 1:1 + 2 * ROWS * TS], flat(E1[:, :, :]), flat(E2[:, :, :]), 0.0,
                                         ALU.mult, ALU.add).then_inc(s["b_scan"], 1)
                    v.wait_ge(s["ev"], g + 1)
                    v.tensor_tensor_scan(A[:, 1:1 + 2 * ROWS * TS], flat(E1[:, :, :]), flat(EV[:, :, :]), 0.0,
                                         ALU.mult, ALU.add).then_inc(s["a_scan"], 1)
                    af, ab = before(A)
                    v.wait_ge(s["ex"], g + 1)
                    v.wait_ge(s["a_scan"], g + 1)
                    loop.did(v.tensor_tensor(N1[:, 0, :, :], EX[:, 0, :, :], af, ALU.mult))
                    loop.did(v.tensor_tensor(N1[:, 1, :, :], EX[:, 1, :, :], ab, ALU.mult))
                    loop.did(v.tensor_tensor(N1[:, 2, :, :], EX[:, 2, :, :], VV[:, 0:ROWS, 1:TS], ALU.mult))
                    loop.settle()
                    loop.did(v.tensor_tensor(N1[:, 0, :, :], N1[:, 0, :, :], N1[:, 1, :, :], ALU.add))
                    v.wait_ge(s["dpart"], g * 2 + 2)
                    loop.did(v.tensor_tensor(D1[:, 0, :, :], D1[:, 0, :, :], D1[:, 1, :, :], ALU.add))
                    loop.settle()
                    loop.did(v.tensor_tensor(N1[:, 0, :, :], N1[:, 0, :, :], N1[:, 2, :, :], ALU.add))
                    loop.did(v.tensor_tensor(D1[:, 0, :, :], D1[:, 0, :, :], EX[:, 2, :, :], ALU.add))
                    loop.settle()
                    loop.did(v.reciprocal(D1[:, 1, :, :], D1[:, 0, :, :]))
                    v.wait_ge(s["r_in"], g + 1)
                    loop.did(v.scalar_tensor_tensor(N1[:, 1, :, :], SR[:, :, :], 1.0, N1[:, 0, :, :], ALU.add,
                                                    ALU.mult))
                    loop.settle()
                    for Y, t0, t1 in ((YP, 0, TP), (YX, TP, T)):
                        v.scalar_tensor_tensor(Y[:, :, :], N1[:, 1, :, t0:t1], 0.5, D1[:, 1, :, t0:t1], ALU.mult,
                                               ALU.mult).then_inc(s["y"], 1)
                    loop.end()

                def mixed(g):
                    back.turn(g)
                    v.wait_ge(s["attn"], g + 1)
                    back.did(v.tensor_tensor(x1[:, :, :], tiles(psT), x0[:, :, :], ALU.add))
                    back.settle()
                    norm(v, back, x1, hn2, s["var2"], s["rstd2"], g + 1, s["norm2"])
                    v.tensor_tensor(xh[:, :, :], x1[:, :, :], hc[:, :, :], ALU.add).then_inc(s["hc_free"], 1)

                def finish(g):
                    v.wait_ge(s["down"], g + 1)
                    v.wait_ge(s["gate"], g + 1)
                    v.wait_ge(s["hc_free"], g + 1)
                    back.did(v.scalar_tensor_tensor(ff[:, :, :], gate[:, :, :], 1.0, tiles(psK), ALU.add, ALU.mult))
                    back.settle()
                    v.scalar_tensor_tensor(H[:, bass.ds(g * 3, 3), :], ff[:, :, :], 0.5, xh[:, :, :], ALU.mult,
                                           ALU.add).then_inc(s["done"], 1)
                    back.end()

                front(0)
                with v.Fori(0, NG - 1) as g:
                    mixed(g)
                    v.wait_ge(s["hc_free"], g + 1)
                    front(g + 1)
                    finish(g)
                    v.wait_ge(s["done"], g + 1)
                mixed(NG - 1)
                finish(NG - 1)

def _layouts(np_, i):
    t = {}
    x = i["x"].reshape(NG, GB, 3, 4, 16, 4, 16)
    x = x.transpose(0, 2, 4, 6, 1, 3, 5).reshape(NG, KC, P, P)
    t["patches"] = x.transpose(0, 2, 1, 3)
    t["text"] = i["txt"].reshape(NG, 2, P, C).transpose(0, 2, 1, 3)
    t["conv_w"] = i["L0_tok_conv_w"].reshape(C, KC, P).transpose(2, 1, 0)
    t["conv_b"] = i["L0_tok_conv_b"].reshape(1, C)
    t["pos"] = i["L0_tok_pos_table"].reshape(32, 32, C)[::8, ::8].reshape(TP, C)
    t["ln"] = np_.stack([i["L0_attn_" + n].reshape(2, HC).T for n in ("ln1_w", "ln1_b", "ln2_w", "ln2_b")], 1)

    def fold(w):
        return w.T.reshape(2, HC, w.shape[0]).transpose(1, 0, 2)

    t["w_kvr"] = np_.stack([fold(i["L0_attn_" + n]) for n in ("Wk_a", "Wv_a", "Wr_a")], 2)
    t["Wo"] = i["L0_attn_Wo_a"].T
    t["Wk_f"] = fold(i["L0_attn_Wk_f"])
    t["Wr_f"] = fold(i["L0_attn_Wr_f"])
    t["Wv_f"] = i["L0_attn_Wv_f"].T.reshape(HCH, P, C).transpose(1, 0, 2)
    t["w_fc"] = fold(i["L0_ffn_w_fc"])
    t["w_proj"] = i["L0_ffn_w_proj"].T.reshape(HCH, P, C).transpose(1, 0, 2)
    t["w_in"] = fold(i["L1_attn_w_in"])
    wo = i["L1_attn_w_out"].T.reshape(3, 2, 2, DH, C).transpose(2, 1, 0, 3, 4)
    t["w_out"] = wo.reshape(2, HC, C).transpose(1, 0, 2)
    t["alpha_e"] = i["L0_ffn_alpha_e"].reshape(1, 3)
    t["alpha_r"] = i["L0_ffn_alpha_r"].reshape(1, 3)
    t["b_fc"] = i["L0_ffn_b_fc"].reshape(HCH, P).T
    t["b_proj"] = i["L0_ffn_b_proj"].reshape(1, C)
    widths = np_.array([r * e for e in EMBEDS for r in RATIOS])
    t["hmask"] = (np_.arange(HID).reshape(HCH, P).T[:, :, None] < widths).astype(np_.float32)
    t["cut"] = (np_.arange(P)[:, None] < EMBEDS[1] - HC).astype(np_.float32)
    t["iota8"] = np_.arange(NE, dtype=np_.float32).reshape(1, NE)
    t["router"] = fold(i["L1_ffn_router_w"])
    t["w1"] = i["L1_ffn_w1"].transpose(0, 2, 1).reshape(NE, 2, HC, ID).transpose(0, 2, 1, 3)
    t["w2"] = i["L1_ffn_w2"].transpose(0, 2, 1).reshape(NE, 4, P, C).transpose(0, 2, 1, 3)
    df = np_.stack([i["L0_attn_decay"], i["L0_attn_first"]])
    t["decfirst"] = np_.stack([df[:, 0:P], np_.concatenate([df[:, P:C], df[:, P:C]], 1)], 2).transpose(1, 0, 2)
    return {n: np_.ascontiguousarray(v) for n, v in t.items()}


def kernel(**inputs):
    import numpy as _np
    import concourse.bacc as _bacc
    from concourse import mybir as _mybir
    from concourse.bass_utils import run_bass_kernel_spmd as _run

    nc = _bacc.Bacc("TRN2", target_bir_lowering=False, num_devices=1)
    laid = _layouts(_np, {n: _np.asarray(v) for n, v in inputs.items()})
    a = {n: nc.dram_tensor("in_" + n, v.shape, _mybir.dt.from_np(v.dtype), kind="ExternalInput").ap()
         for n, v in laid.items()}
    out = nc.dram_tensor("out_dram", (P, NT, C), F32, kind="ExternalOutput").ap()
    program(nc, a, out)
    r = _run(nc, [{"in_" + n: v for n, v in laid.items()}], core_ids=[0])
    o = r.results[0]["out_dram"].reshape(P, NG, 3, C).transpose(1, 2, 0, 3)
    got = _np.empty((B, T, C), _np.float32)
    got[:, 0:TP] = o[:, 0].reshape(B, TP, C)
    got[:, TP:T] = o[:, 1:3].reshape(B, TX, C)
    return got
```

```python
from contextlib import ExitStack

import numpy as np

import concourse.bass as bass
from concourse import mybir

F32 = mybir.dt.float32
BF16 = mybir.dt.bfloat16
U32 = mybir.dt.uint32
I32 = mybir.dt.int32
ALU = mybir.AluOpType
ACT = mybir.ActivationFunctionType
AX = mybir.AxisListType
RMAX = bass.bass_isa.ReduceOp.max
RADD = bass.bass_isa.ReduceOp.add

P = 128
B, T, C = 64, 48, 192
TP, TX = 16, 32
HC = C // 2
NG, GB = 8, 8
GT = GB * T
NT = 3 * NG
KC = 768 // P
HID = 768
HCH = HID // P
ROWS = GB + GB // 2
TS = T + 1
EPS = 1e-5
NEG = -1e38
NH, DH = 12, 16
MAGIC = 12582912.0
EMBEDS, RATIOS = (96, 144, 192), (2, 3, 4)
NE, ID = 8, 512
NQ = 4
QT = NT // NQ
NBLK = 2 * B * T // P + NE - 1
QMAX = 127.0
NP = B // 2
PP = 112
NS = NP // 2
SETW = 2 * NH * T
BIAS_NAMES = ("conv_b",)


class Straight:

    def __init__(self, sem):
        self.sem, self.n = sem, 0

    def on(self, eng):
        self.eng = eng
        return self

    def did(self, ins):
        self.n += 1
        ins.then_inc(self.sem, 1)

    def settle(self):
        self.eng.wait_ge(self.sem, self.n)


class Steps:

    def __init__(self, eng, sem, per=0):
        self.eng, self.sem, self.per, self.base, self.n = eng, sem, per, 0, 0

    def turn(self, i):
        assert self.n in (0, self.per)
        self.base, self.n = i * self.per, 0

    def did(self, ins):
        self.n += 1
        ins.then_inc(self.sem, 1)

    def settle(self):
        self.eng.wait_ge(self.sem, self.base + self.n)

    def end(self):
        assert self.n == self.per, (self.n, self.per)


def bcast(ap, n, at):
    v = ap.unsqueeze(at)
    shape = list(v.shape)
    shape[at] = n
    return v.broadcast_to(shape)


def program(nc, a, out, X_rows, Y_rows):
    ctx = ExitStack()
    with ctx:
        def sb(name, shape, dt=F32, scope=ctx):
            return scope.enter_context(nc.sbuf_tensor(name, shape, dt))

        def sem(name):
            return ctx.enter_context(nc.semaphore(name))

        class EarlySems:

            def __enter__(self):
                self.scope, self.all = ExitStack(), []
                return self

            def __call__(self, name):
                self.all.append(self.scope.enter_context(nc.semaphore(name)))
                return self.all[-1]

            def __exit__(self, *_):
                with nc.Block() as block:
                    @block.gpsimd
                    def _(gp):
                        for x in self.all:
                            gp.sem_clear(x)
                self.scope.close()

        PS = ctx.enter_context(nc.psum_tensor("PS", [P, 8, 512], F32))
        straight = Straight(sem("straight"))
        passed = sem("passed")
        H = sb("H", [P, NT, C])
        ident = sb("ident", [P, P])
        identb = sb("identb", [P, P], BF16)
        neghalf = sb("neghalf", [P, 16])
        stat = sb("stat", [P, 3, 6])
        mv = sb("mv", [P, 3, 2])
        varp = sb("varp", [P, 3])
        rstd = sb("rstd", [P, 3])

        def norm(v, steps, src, dst, var_ready, rstd_ready, count, ready=None):
            for j in range(3):
                steps.did(v.bn_stats(stat[:, j, :], src[:, j, :]))
            steps.settle()
            seen(v, passed)
            for j in range(3):
                steps.did(v.bn_aggr(mv[:, j, :], stat[:, j, :]))
            steps.settle()
            v.tensor_scalar(varp[:, :], mv[:, :, 1], EPS, None, ALU.add).then_inc(var_ready, 1)
            v.wait_ge(rstd_ready, count)
            for j in range(3):
                ins = v.tensor_scalar(dst[:, j, :], src[:, j, :], mv[:, j, 0:1], rstd[:, j:j + 1],
                                      ALU.subtract, ALU.mult)
                if ready is None:
                    steps.did(ins)
                else:
                    ins.then_inc(ready, 1)

        def rsqrt(g, var_ready, rstd_ready, count):
            g.wait_ge(var_ready, count)
            g.tensor_tensor(out=rstd[:, :], in0=varp[:, :], in1=neghalf[:, 0:3],
                            op=ALU.pow).then_inc(rstd_ready, 1)

        with EarlySems() as early:
            embed_and_mix(nc, straight, passed, a, early, sb, PS, H, ident, identb, neghalf, norm, rsqrt)
        att = ExitStack()
        with att:
            SC = sb("SC", [P, 24], F32, att)
            MX = sb("MX", [P, 16], F32, att)
            wout = sb("wout", [HC, 2, C], BF16, att)
            Vi = sb("Vi", [P, NP, C], BF16, att)
            stage = ExitStack()
            with stage:
                Qp = sb("Qp", [P, 3, B * T], BF16, stage)
                Kp = sb("Kp", [P, 3, B * T], BF16, stage)
                real = ExitStack()
                with real:
                    Q = sb("Qf", [HC, 2, B * T], F32, real)
                    K = sb("Kf", [HC, 2, B * T], F32, real)
                    V = sb("Vf", [P, NP, C], F32, real)
                    ffn_and_project(nc, straight, passed, a, sem, sb, PS, H, ident, norm, rsqrt, Q, K, V, MX, SC, Qp, Kp)
                    quantise_qkv(nc, straight, passed, a, sem, sb, PS, SC, Q, K, V, Qp, Kp, Vi, wout, MX)
                Qs = sb("Qs", [P, 2, 3, GT], BF16, stage)
                Ks = sb("Ks", [P, 2, 3, GT], BF16, stage)
                E = sb("E", [P, NS, SETW], F32, stage)
                RS = sb("RS", [P, NS, 2 * NH], F32, stage)
                score_maximum(nc, straight, passed, sem, sb, PS, SC, Qp, Kp, Qs, Ks)
                softmax_rows(nc, straight, passed, sem, sb, PS, SC, Qp, Kp, Qs, Ks, E, RS)
                CTX = sb("CTX", [P, NP, C], F32, stage)
                context(nc, straight, passed, sem, sb, PS, SC, identb, E, RS, Vi, CTX)
                Y = E[:, 0:4, :].rearrange("p a n -> p (a n)").rearrange("p (j c) -> p j c", c=C)
                R = E[:, 4:8, :].rearrange("p a n -> p (a n)").rearrange("p (j c) -> p j c", c=C)
                project_out(nc, straight, passed, sem, sb, PS, SC, H, identb, norm, rsqrt, CTX, wout, Y, R)
                batch_norm(nc, straight, passed, sem, sb, PS, SC, H, ident, neghalf, Y, R)
        moe = ExitStack()
        with moe:
            GK = sb("GK", [P, 2, NT], F32, moe)
            slots = sb("slots", [P, 2, NT], U32, moe)
            owner = sb("owner", [P, NBLK], I32, moe)
            W1 = sb("W1", [HC, NE * 2, ID], F32, moe)
            W2 = sb("W2", [P, NE * 4, C], F32, moe)
            route(nc, straight, passed, a, sem, sb, PS, H, ident, norm, rsqrt, W1, W2, GK, slots, owner, X_rows)
            experts(nc, sem, sb, PS, ident, W1, W2, owner, X_rows, Y_rows)
            combine(nc, passed, sem, sb, H, GK, slots, Y_rows, out)


def ffn_and_project(nc, straight, passed, a, sem, sb_, PS, H, ident, norm, rsqrt, Q, K, V, MX, SC, Qp, Kp):
    scope = ExitStack()
    with scope:
        def sb(name, shape, dt=F32):
            return sb_(name, shape, dt, scope)

        s = {n: sem("p2_" + n) for n in (
            "weights", "set_ready", "var", "rstd", "norm", "turned_f", "turned_g", "xf", "xg", "up", "gelu",
            "down", "h3", "qk", "qk_in", "v", "v_in", "f_dve", "g_dve", "m_dve", "wmaxes", "wmax_all",
            "zeros")}
        w0 = sb("w0", [HC, 2, HID])
        w1 = sb("w1", [P, HCH, C])
        win = sb("win", [HC, 2, 3 * C])
        alpha = sb("alpha", [P, 2, 3])
        aij = sb("aij", [P, 3, 3])
        hmask = sb("hmask", [P, HCH, 9])
        g0 = sb("g0", [P, 3, HID])
        gc = sb("gc", [P, 3, HCH])
        gp_ = sb("gp_", [P, HCH, 9])
        cut = sb("cut", [P, 1])
        bfc = sb("bfc", [P, HCH])
        bpr = sb("bpr", [P, C])
        hf = sb("hf", [P, 3, C])
        hg = sb("hg", [P, 3, C])
        xf = sb("xf", [HC, 2, GT])
        xg = sb("xg", [HC, 2, GB, 64])
        gl = sb("gl", [P, HCH, GT])
        x2 = sb("x2", [P, 3, C])
        x2b = sb("x2b", [P, 3, C])
        x3 = sb("x3", [P, 3, C])
        F_DVE, G_DVE, M_DVE = 8, 6, 5
        wmax = sb("wmax", [P, 4])

        psF, psG = PS[:, 0:2, :], PS[:, 2:4, :]

        def tiles(ps):
            return ps.rearrange("p k (j c) -> p (k j) c", c=256)[:, 0:3, 0:C]

        def values(ps):
            return ps[0:PP].rearrange("p k (j c) -> p (k j) c", c=256)[:, :, 0:C]

        with nc.Block() as block:
            @block.sync
            def _(sp):
                def load(dst, src):
                    sp.dma_start(dst, src).then_inc(s["weights"], 16)
                load(w0[:, :, :], a["w_fc"])
                load(w1[:, :, :], a["w_proj"])
                load(win[:, :, :], a["w_in"])
                load(alpha[:, 0, :], a["alpha_e"].to_broadcast([P, 3]))
                load(alpha[:, 1, :], a["alpha_r"].to_broadcast([P, 3]))
                load(hmask[:, :, :], a["hmask"])
                load(bfc[:, :], a["b_fc"])
                load(bpr[:, :], a["b_proj"].to_broadcast([P, C]))
                load(cut[:, :], a["cut"])

            NW = 9

            @block.gpsimd
            def _(gp):
                for x in (Qp, Kp):
                    gp.memset(x[:, :, :].rearrange("p c n -> p (c n)").bitcast(F32), 0.0).then_inc(s["zeros"], 1)
                gp.wait_ge(s["wmaxes"], 1)
                gp.partition_all_reduce(wmax[:, 1:2], wmax[:, 0:1], P, RMAX).then_inc(s["wmax_all"], 1)
                with gp.Fori(0, 2 * NG) as n:
                    rsqrt(gp, s["var"], s["rstd"], n + 1)

            @block.vector
            def _(v):
                st = straight.on(v)
                st.did(v.memset(wmax[:, :], 0.0))
                st.did(v.memset(MX[:, :], 0.0))
                st.did(v.memset(xg[:, :, :, :], 0.0))
                v.wait_ge(s["weights"], 16 * NW)
                st.settle()
                v.tensor_reduce(wmax[0:HC, 0:1], win[:, :, :].rearrange("p c n -> p (c n)"), AX.X, ALU.max,
                                apply_absolute_value=True).then_inc(s["wmaxes"], 1)
                for i in range(3):
                    st.did(v.tensor_scalar(aij[:, i, :], alpha[:, 1, :], alpha[:, 0, i:i + 1], None, ALU.mult))
                st.did(v.memset(g0[:, :, :], 0.0))
                st.settle()
                for j, r in enumerate(RATIOS):
                    for i, e in enumerate(EMBEDS):
                        st.did(v.tensor_scalar(g0[:, i, 0:r * e], g0[:, i, 0:r * e], aij[:, i, j:j + 1], None,
                                               ALU.add))
                    st.settle()
                st.did(v.tensor_tensor(gp_[:, :, :], hmask[:, :, :],
                                       bcast(aij[:, :, :].rearrange("p i j -> p (i j)"), HCH, 1), ALU.mult))
                st.settle()
                for i in range(3):
                    st.did(v.tensor_reduce(gc[:, i, :], gp_[:, :, 3 * i:3 * i + 3], AX.X, ALU.add))
                st.settle()
                st.did(v.tensor_tensor(g0[:, 0, :], g0[:, 0, :], g0[:, 1, :], ALU.add))
                st.did(v.tensor_tensor(gc[:, 1, :], gc[:, 1, :], gc[:, 2, :], ALU.add))
                st.settle()
                st.did(v.tensor_tensor(g0[:, 0, :], g0[:, 0, :], g0[:, 2, :], ALU.add))
                st.did(v.scalar_tensor_tensor(g0[:, 1, :], g0[:, 1, :], cut[:, 0:1], g0[:, 2, :], ALU.mult,
                                              ALU.add))
                st.did(v.tensor_tensor(gc[:, 0, :], gc[:, 0, :], gc[:, 1, :], ALU.add))
                st.settle()
                for c in range(2):
                    st.did(v.tensor_tensor(w0[:, c, :], w0[:, c, :], g0[0:HC, c, :], ALU.mult))
                for i, (e0, e1) in enumerate(((0, 96), (96, 144), (144, 192))):
                    for m in range(HCH):
                        st.did(v.tensor_scalar(w1[:, m, e0:e1], w1[:, m, e0:e1], gc[:, i, m:m + 1], None,
                                               ALU.mult))
                st.did(v.tensor_tensor(bfc[:, :], bfc[:, :], gc[:, 0, :], ALU.mult))
                st.did(v.tensor_reduce(alpha[:, 0, :], aij[:, :, :], AX.X, ALU.add))
                st.settle()
                st.did(v.tensor_scalar(alpha[:, 1, 1:2], alpha[:, 0, 1:2], alpha[:, 0, 2:3], None, ALU.add))
                st.settle()
                st.did(v.tensor_scalar(alpha[:, 1, 0:1], alpha[:, 0, 0:1], alpha[:, 1, 1:2], None, ALU.add))
                st.settle()
                for e0, e1, k in ((0, 96, alpha[:, 1, 0:1]), (96, 144, alpha[:, 1, 1:2]),
                                  (144, 192, alpha[:, 0, 2:3])):
                    st.did(v.tensor_scalar(bpr[:, e0:e1], bpr[:, e0:e1], k, None, ALU.mult))
                v.wait_ge(s["wmax_all"], 1)
                st.did(v.tensor_scalar(wmax[:, 2:3], wmax[:, 1:2], 1e-8, 1.0 / QMAX, ALU.max, ALU.mult))
                st.settle()
                st.did(v.reciprocal(wmax[:, 3:4], wmax[:, 2:3]))
                st.settle()
                st.did(v.tensor_copy(SC[:, S_WIN:S_WIN + 1], wmax[:, 2:3]))
                st.did(v.tensor_scalar(win[:, :, :], win[:, :, :], wmax[0:HC, 3:4], MAGIC, ALU.mult, ALU.add))
                st.settle()
                v.tensor_scalar(win[:, :, :], win[:, :, :], -MAGIC, None, ALU.add).then_inc(s["set_ready"], 1)
                v.wait_ge(s["set_ready"], 1)
                st.settle()

                ffn = Steps(v, s["f_dve"], F_DVE)
                proj = Steps(v, s["g_dve"], G_DVE)
                maxima = Steps(v, s["m_dve"], M_DVE)

                def norm_ffn(g, first=False):
                    ffn.turn(g)
                    if not first:
                        v.wait_ge(s["turned_f"], g)
                    ffn.did(v.tensor_scalar(x2[:, :, :], H[:, bass.ds(g * 3, 3), :], 1.0, None, ALU.mult))
                    ffn.settle()
                    norm(v, ffn, x2, hf, s["var"], s["rstd"], g * 2 + 1, s["norm"])
                    ffn.did(v.tensor_tensor(x2b[:, :, :], x2[:, :, :], bcast(bpr[:, :], 3, 1), ALU.add))
                    ffn.end()

                def norm_project(g, first=False):
                    proj.turn(g)
                    v.wait_ge(s["down"], g + 1)
                    ffn.settle()
                    v.tensor_tensor(x3[:, :, :], x2b[:, :, :], tiles(psF), ALU.add).then_inc(s["h3"], 1)
                    v.tensor_tensor(H[:, bass.ds(g * 3, 3), :], x2b[:, :, :], tiles(psF), ALU.add
                                    ).then_inc(s["h3"], 1)
                    v.wait_ge(s["h3"], g * 2 + 2)
                    if not first:
                        v.wait_ge(s["turned_g"], g)
                    seen(v, passed)
                    norm(v, proj, x3, hg, s["var"], s["rstd"], g * 2 + 2, s["norm"])
                    proj.end()

                def largest(g, behind):
                    maxima.turn(g)
                    v.wait_ge(s["norm"], (g + behind) * 6 + 6)
                    maxima.did(v.tensor_reduce(MX[:, 7:8], hg[:, :, :].rearrange("p j c -> p (j c)"), AX.X,
                                               ALU.max, apply_absolute_value=True))
                    for k in range(2):
                        v.wait_ge(s["qk_in"], g * 4 + 2 * k + 2)
                        maxima.did(v.tensor_reduce(MX[0:HC, 4 + k:5 + k], PS[0:HC, 4 + 2 * k:6 + 2 * k, 0:GT],
                                                   AX.XY, ALU.max, apply_absolute_value=True))
                    v.wait_ge(s["v_in"], g + 1)
                    maxima.did(v.tensor_reduce(MX[0:PP, 6:7], values(psG), AX.XY, ALU.max,
                                               apply_absolute_value=True))
                    maxima.settle()
                    maxima.did(v.tensor_tensor(MX[:, 0:4], MX[:, 0:4], MX[:, 4:8], ALU.max))
                    maxima.settle()
                    maxima.end()

                norm_ffn(0, first=True)
                norm_project(0, first=True)
                st.did(v.memset(MX[:, 14:15], 0.0))
                v.wait_ge(s["norm"], 6)
                st.did(v.tensor_reduce(MX[:, 3:4], hg[:, :, :].rearrange("p j c -> p (j c)"), AX.X, ALU.max,
                                       apply_absolute_value=True))
                norm_ffn(1)
                with v.Fori(0, NG - 2) as g:
                    norm_project(g + 1)
                    norm_ffn(g + 2)
                    largest(g, 1)
                norm_project(NG - 1)
                largest(NG - 2, 1)
                largest(NG - 1, 0)

            @block.tensor
            def _(pe):
                pe.wait_ge(s["set_ready"], 1)

                def turn(src, dst, turned):
                    for c in range(2):
                        for j in range(3):
                            mm = pe.transpose(dst[0:HC, c, j * P:(j + 1) * P], src[:, j, c * HC:(c + 1) * HC],
                                              ident[:, :])
                    mm.then_inc(turned, 1)

                def dense(g, first=False):
                    pe.wait_ge(s["norm"], g * 6 + 3)
                    turn(hf, psF, s["turned_f"])
                    pe.wait_ge(s["xf"], g * 2 + 2)
                    for m in range(HCH):
                        if m == 0 and not first:
                            pe.wait_ge(s["m_dve"], g * M_DVE - M_DVE)
                        for c in range(2):
                            mm = pe.matmul(PS[:, 2 + m, 0:GT], w0[:, c, m * P:(m + 1) * P], xf[:, c, :],
                                           start=c == 0, stop=c == 1)
                        mm.then_inc(s["up"], 1)
                    pe.wait_ge(s["gelu"], g * HCH + HCH)
                    for j in range(3):
                        for m in range(HCH):
                            mm = pe.matmul(psF[:, j // 2, (j % 2) * 256:(j % 2) * 256 + C],
                                           gl[:, m, j * P:(j + 1) * P], w1[:, m, :],
                                           start=m == 0, stop=m == HCH - 1)
                    mm.then_inc(s["down"], 1)

                def project(g):
                    pe.wait_ge(s["norm"], g * 6 + 6)
                    turn(hg, psG, s["turned_g"])
                    pe.wait_ge(s["xg"], g * 4 + 4)
                    for m in range(4):
                        for c in range(2):
                            mm = pe.matmul(PS[0:HC, 4 + m, 0:GT].rearrange("p (b t) -> p b t", t=T),
                                           win[:, c, m * HC:(m + 1) * HC], xg[:, c, :, 0:T],
                                           start=c == 0, stop=c == 1)
                        mm.then_inc(s["qk"], 1)
                    for q in range(4):
                        for c in range(2):
                            mm = pe.matmul(psG[0:PP, q // 2, (q % 2) * 256:(q % 2) * 256 + C],
                                           xg[:, c, 2 * q:2 * q + 2, :].rearrange("p b t -> p (b t)")[:, 0:PP],
                                           win[:, c, 2 * C:3 * C], start=c == 0, stop=c == 1)
                    mm.then_inc(s["v"], 1)

                dense(0, first=True)
                pe.wait_ge(s["h3"], 2)
                dense(1, first=True)
                project(0)
                with pe.Fori(1, NG - 1) as g:
                    pe.wait_ge(s["h3"], g * 2 + 2)
                    dense(g + 1)
                    project(g)
                pe.wait_ge(s["m_dve"], (NG - 1) * M_DVE)
                project(NG - 1)

            @block.scalar
            def _(act):
                act.wait_ge(s["set_ready"], 1)

                def dense(g):
                    act.wait_ge(s["turned_f"], g + 1)
                    for c in range(2):
                        act.activation(xf[:, c, :], psF[0:HC, c, 0:GT], ACT.Copy).then_inc(s["xf"], 1)
                    for m in range(HCH):
                        act.wait_ge(s["up"], g * HCH + m + 1)
                        act.activation(gl[:, m, :], PS[:, 2 + m, 0:GT], ACT.Gelu_apprx_tanh, bias=bfc[:, m:m + 1]
                                       ).then_inc(s["gelu"], 1)

                def project(g):
                    act.wait_ge(s["turned_g"], g + 1)
                    for c in range(2):
                        for j0, j1, t0, t1 in ((0, P, 0, TP), (P, GT, TP, T)):
                            act.activation(xg[:, c, :, t0:t1],
                                           psG[0:HC, c, j0:j1].rearrange("p (b t) -> p b t", t=t1 - t0),
                                           ACT.Copy).then_inc(s["xg"], 1)
                    for m in range(4):
                        act.wait_ge(s["qk"], g * 4 + m + 1)
                        dst = (Q, K)[m // 2]
                        act.activation(dst[:, m % 2, bass.ds(g * GT, GT)], PS[0:HC, 4 + m, 0:GT], ACT.Copy,
                                       scale=wmax[0:HC, 2:3]).then_inc(s["qk_in"], 1)
                    act.wait_ge(s["v"], g + 1)
                    act.activation(V[0:PP, bass.ds(g * 4, 4), :], values(psG), ACT.Copy, scale=wmax[0:PP, 2:3]
                                   ).then_inc(s["v_in"], 1)

                dense(0)
                with act.Fori(0, NG - 1) as g:
                    dense(g + 1)
                    project(g)
                project(NG - 1)


def seen(eng, held):
    eng.sem_inc(held, 1)


(S_WIN, S_WOUT, S_Q, S_K, S_V, S_X, S_SCORE, S_ATT, S_CTX, S_Y, S_RN) = range(11)


class Scales:

    def __init__(self, v, steps, table):
        self.v, self.st, self.t = v, steps, table

    def col(self, k):
        return self.t[:, k:k + 1]

    def op(self, dst, src, s1, s2, op0, op1=None):
        if op1 is None:
            ins = self.v.tensor_scalar(self.col(dst), self.col(src), s1, None, op0)
        else:
            ins = self.v.tensor_scalar(self.col(dst), self.col(src), s1, s2, op0, op1)
        self.st.did(ins)
        self.st.settle()

    def inverse(self, dst, src):
        self.st.did(self.v.reciprocal(self.col(dst), self.col(src)))
        self.st.settle()


def quantise_qkv(nc, straight, passed, a, sem, sb_, PS, SC, Q, K, V, Qp, Kp, Vi, wout, MX):
    scope = ExitStack()
    with scope:
        def sb(name, shape, dt=F32):
            return sb_(name, shape, dt, scope)

        s = {n: sem("p3_" + n) for n in ("wout", "maxes", "all", "q", "k", "v", "padded",
                                         "pool")}
        Qi = sb("Qi", [HC, 2, B * T], BF16)
        Ki = sb("Ki", [HC, 2, B * T], BF16)
        wf = sb("wf", [HC, 2, C])
        F_Q, F_K, F_V, F_W, M_ = 11, 12, 13, 14, 16
        with nc.Block() as block:
            @block.sync
            def _(sp):
                sp.dma_start(wf[:, :, :], a["w_out"]).then_inc(s["wout"], 16)
                n = 0
                for src, dst, ready in ((Qi, Qp, "q"), (Ki, Kp, "k")):
                    sp.wait_ge(s[ready], 1)
                    for h in range(NH):
                        c, r = divmod(h, 6)
                        sp.dma_start(dst[32 * (h % 4):32 * (h % 4) + DH, h // 4, :],
                                     src[DH * r:DH * r + DH, c, :]).then_inc(s["padded"], 16)
                        n += 16
                sp.wait_ge(s["padded"], n)

            @block.gpsimd
            def _(gp):
                gp.wait_ge(s["maxes"], 1)
                gp.partition_all_reduce(MX[:, 8:13], MX[:, 0:5], P, RMAX).then_inc(s["all"], 1)

            @block.vector
            def _(v):
                st = straight.on(v)
                sc = Scales(v, st, SC)
                st.did(v.memset(MX[:, 4:5], 0.0))
                v.wait_ge(s["wout"], 16)
                st.settle()
                v.tensor_reduce(MX[0:HC, 4:5], wf[:, :, :].rearrange("p c n -> p (c n)"), AX.X, ALU.max,
                                apply_absolute_value=True).then_inc(s["maxes"], 1)
                v.wait_ge(s["all"], 1)
                st.did(v.tensor_scalar(MX[:, 8:11], MX[:, 8:11], SC[:, S_WIN:S_WIN + 1], None, ALU.mult))
                st.settle()
                st.did(v.tensor_scalar(SC[:, S_Q:S_Q + 4], MX[:, 8:12], 1e-8, 1.0 / QMAX, ALU.max, ALU.mult))
                st.did(v.tensor_scalar(SC[:, S_WOUT:S_WOUT + 1], MX[:, 12:13], 1e-8, 1.0 / QMAX, ALU.max,
                                       ALU.mult))
                st.settle()
                st.did(v.reciprocal(SC[:, F_Q:F_Q + 3], SC[:, S_Q:S_Q + 3]))
                st.did(v.reciprocal(SC[:, F_W:F_W + 1], SC[:, S_WOUT:S_WOUT + 1]))
                st.settle()
                st.did(v.tensor_scalar(wf[:, :, :], wf[:, :, :], SC[0:HC, F_W:F_W + 1], MAGIC, ALU.mult,
                                       ALU.add))
                st.settle()
                st.did(v.tensor_scalar(wout[:, :, :], wf[:, :, :], -MAGIC, None, ALU.add))
                for X, Xi, f, ready in ((Q, Qi, F_Q, "q"), (K, Ki, F_K, "k"), (V, Vi, F_V, "v")):
                    n = X.shape[0] if X is not V else PP
                    st.did(v.tensor_scalar(X[0:n, :, :], X[0:n, :, :], SC[0:n, f:f + 1], MAGIC, ALU.mult,
                                           ALU.add))
                    st.settle()
                    v.tensor_scalar(Xi[0:n, :, :], X[0:n, :, :], -MAGIC, None, ALU.add).then_inc(s[ready], 1)
                st.did(v.memset(PS[:, :, :], 0.0))
                st.settle()


def score_matmuls(pe, PS, Qs, Ks, buf, half):
    for slot in range(2):
        for e in range(2):
            tok = slice(((half * 2 + slot) * 2 + e) * T, ((half * 2 + slot) * 2 + e + 1) * T)
            for c in range(3):
                for j in range(4):
                    col = slot * 3 * T + c * T
                    mm = pe.matmul(PS[64 * e:64 * e + T, 4 * half + j, col:col + T],
                                   Qs[32 * j:32 * j + DH, buf, c, tok], Ks[32 * j:32 * j + DH, buf, c, tok],
                                   start=True, stop=True, skip_group_check=True)
    return mm


def turns(eng, turn):
    turn(0)
    with eng.Fori(1, NG // 2 - 1) as i:
        turn(i)
    turn(NG // 2 - 1)


def is_first(i):
    return isinstance(i, int) and i == 0


def is_last(i):
    return isinstance(i, int) and i == NG // 2 - 1


def all_scores(pe, PS, Qs, Ks, s):
    def turn(i):
        for k in range(4):
            if k % 2 == 0:
                pe.wait_ge(s["staged%d" % (k // 2)], i * 32 + 32)
            if not is_first(i) or k >= 2:
                pe.wait_ge(s["free"], i * 4 + k - 1)
            score_matmuls(pe, PS, Qs, Ks, k // 2, k % 2).then_inc(s["scores"], 1)
    turns(pe, turn)


def stage_all(sp, Qp, Kp, Qs, Ks, s):
    for buf in range(2):
        stage_qk(sp, Qp, Kp, Qs, Ks, buf, buf, s)
    with sp.Fori(1, NG // 2) as i:
        for buf in range(2):
            sp.wait_ge(s["scores"], (i * 2 + buf - 1) * 2)
            stage_qk(sp, Qp, Kp, Qs, Ks, i * 2 + buf, buf, s)


def stage_qk(sp, Qp, Kp, Qs, Ks, g, buf, s):
    for src, dst in ((Qp, Qs), (Kp, Ks)):
        sp.dma_start(dst[:, buf, :, :], src[:, :, bass.ds(g * GT, GT)]).then_inc(s["staged%d" % buf], 16)


def score_maximum(nc, straight, passed, sem, sb_, PS, SC, Qp, Kp, Qs, Ks):
    scope = ExitStack()
    with scope:
        s = {n: sem("p4_" + n) for n in ("staged0", "staged1", "scores", "free", "loop_dve", "maxes",
                                         "all")}
        m = sb_("m4", [P, 4], F32, scope)
        with nc.Block() as block:
            @block.sync
            def _(sp):
                stage_all(sp, Qp, Kp, Qs, Ks, s)

            @block.tensor
            def _(pe):
                all_scores(pe, PS, Qs, Ks, s)

            @block.gpsimd
            def _(gp):
                gp.wait_ge(s["maxes"], 1)
                gp.partition_all_reduce(m[:, 3:4], m[:, 0:1], P, RMAX).then_inc(s["all"], 1)

            @block.vector
            def _(v):
                st = straight.on(v)
                st.did(v.memset(m[:, :], 0.0))
                st.settle()
                loop = Steps(v, s["loop_dve"], 4)
                with v.Fori(0, NG // 2) as i:
                    loop.turn(i)
                    for k in range(4):
                        v.wait_ge(s["scores"], i * 4 + k + 1)
                        h = k % 2
                        v.tensor_reduce(m[0:PP, 1 + h:2 + h], PS[0:PP, 4 * h:4 * h + 4, 0:6 * T], AX.XY, ALU.max,
                                        apply_absolute_value=True).then_inc(s["free"], 1)
                        v.wait_ge(s["free"], i * 4 + k + 1)
                        loop.did(v.tensor_tensor(m[:, 0:1], m[:, 0:1], m[:, 1 + h:2 + h], ALU.max))
                        loop.settle()
                    loop.end()
                v.memset(m[:, 1:2], 0.0).then_inc(s["maxes"], 1)
                v.wait_ge(s["all"], 1)
                sc = Scales(v, st, SC)
                sc.op(15, S_Q, SC[:, S_K:S_K + 1], 0.25, ALU.mult, ALU.mult)
                st.did(v.tensor_scalar(SC[:, S_SCORE:S_SCORE + 1], m[:, 3:4], SC[:, 15:16], 1e-8, ALU.mult,
                                       ALU.max))
                st.settle()
                sc.op(S_SCORE, S_SCORE, 1.0 / QMAX, None, ALU.mult)
                sc.inverse(16, S_SCORE)
                sc.op(16, 16, SC[:, 15:16], None, ALU.mult)
                st.did(v.memset(SC[:, 17:18], MAGIC))
                st.settle()


def softmax_rows(nc, straight, passed, sem, sb_, PS, SC, Qp, Kp, Qs, Ks, E, RS):
    scope = ExitStack()
    with scope:
        def sb(name, shape, dt=F32):
            return sb_(name, shape, dt, scope)

        s = {n: sem("p5_" + n) for n in ("staged0", "staged1", "scores", "free", "rowmax", "less",
                                         "exp", "sums", "maxes", "all")}
        W = sb("W5", [P, 4, SETW])
        rm = sb("rm5", [P, 4, 2 * NH])
        m = sb("m5", [P, 2])
        with nc.Block() as block:
            @block.sync
            def _(sp):
                stage_all(sp, Qp, Kp, Qs, Ks, s)

            @block.tensor
            def _(pe):
                all_scores(pe, PS, Qs, Ks, s)

            @block.scalar
            def _(act):
                def steps(n, k):
                    act.wait_ge(s["scores"], n + 1)
                    if not isinstance(n, int) or n >= 4:
                        act.wait_ge(s["exp"], n - 3)
                    act.activation(W[0:PP, k, :].rearrange("p (k n) -> p k n", k=4),
                                   PS[0:PP, 4 * (k % 2):4 * (k % 2) + 4, 0:6 * T], ACT.Identity,
                                   scale=SC[0:PP, 16:17], bias=SC[0:PP, 17:18]).then_inc(s["free"], 1)

                def turn(i):
                    for k in range(4):
                        if not is_last(i) or k < 2:
                            steps(i * 4 + k + 2, (k + 2) % 4)
                        act.wait_ge(s["less"], i * 4 + k + 1)
                        act.activation(E[0:PP, bass.ds(i * 4 + k, 1), :], W[0:PP, k:k + 1, :], ACT.Exp,
                                       scale=SC[0:PP, S_SCORE:S_SCORE + 1]).then_inc(s["exp"], 1)
                steps(0, 0)
                steps(1, 1)
                turns(act, turn)

            @block.gpsimd
            def _(gp):
                with gp.Fori(0, NG // 2) as i:
                    for k in range(4):
                        gp.wait_ge(s["rowmax"], i * 4 + k + 1)
                        w = W[0:PP, k, :].rearrange("p (r n) -> p r n", n=T)
                        gp.tensor_tensor(out=w, in0=w, in1=bcast(rm[0:PP, k, :], T, 2), op=ALU.subtract
                                         ).then_inc(s["less"], 1)
                gp.wait_ge(s["maxes"], 1)
                gp.partition_all_reduce(m[:, 1:2], m[:, 0:1], P, RMAX).then_inc(s["all"], 1)

            @block.vector
            def _(v):
                def row_maxima(n, k):
                    v.wait_ge(s["free"], n + 1)
                    v.tensor_reduce(rm[0:PP, k, :], W[0:PP, k, :].rearrange("p (r n) -> p r n", n=T), AX.X,
                                    ALU.max).then_inc(s["rowmax"], 1)

                def turn(i):
                    for k in range(4):
                        if not is_last(i) or k < 2:
                            row_maxima(i * 4 + k + 2, (k + 2) % 4)
                        v.wait_ge(s["exp"], i * 4 + k + 1)
                        seen(v, passed)
                        v.tensor_reduce(RS[0:PP, bass.ds(i * 4 + k, 1), :].rearrange("p a r -> p (a r)"),
                                        E[0:PP, bass.ds(i * 4 + k, 1), :].rearrange(
                                            "p a (r n) -> p (a r) n", n=T), AX.X, ALU.add).then_inc(s["sums"], 1)
                row_maxima(0, 0)
                row_maxima(1, 1)
                turns(v, turn)
                st = straight.on(v)
                sc = Scales(v, st, SC)
                st.did(v.memset(m[:, :], 0.0))
                v.wait_ge(s["sums"], 2 * NG)
                r = RS[0:PP, :, :].rearrange("p a r -> p (a r)")
                st.did(v.reciprocal(r, r))
                st.settle()
                v.tensor_reduce(m[0:PP, 0:1], r, AX.X, ALU.max).then_inc(s["maxes"], 1)
                v.wait_ge(s["all"], 1)
                st.did(v.tensor_scalar(SC[:, S_ATT:S_ATT + 1], m[:, 1:2], 1e-8, 1.0 / QMAX, ALU.max, ALU.mult))
                st.settle()
                sc.inverse(18, S_ATT)
                st.did(v.tensor_scalar(r, r, SC[0:PP, 18:19], None, ALU.mult))
                st.settle()


def context(nc, straight, passed, sem, sb_, PS, SC, identb, E, RS, Vi, CTX):
    scope = ExitStack()
    with scope:
        def sb(name, shape, dt=F32):
            return sb_(name, shape, dt, scope)

        s = {n: sem("p6_" + n) for n in ("staged0", "staged1", "prod", "ai", "turned", "at", "ctx",
                                         "ctx_in", "max", "maxes", "all", "loop_dve")}
        W = sb("W6", [P, 2, SETW])
        Ai = sb("Ai", [P, 2, SETW], BF16)
        AT = sb("AT", [P, 4, 6 * PP], BF16)
        Vs = sb("Vs", [P, 2, 2, 4, C], BF16)
        m = sb("m6", [P, 4])
        with nc.Block() as block:
            @block.sync
            def _(sp):
                def stage(g, par):
                    for r0, r1, q0, w in ((0, PP, 0, 0), (0, T, 64, 1), (64, PP, 0, 1)):
                        sp.dma_start(Vs[r0:r1, par, w, :, :], Vi[q0:q0 + r1 - r0, bass.ds(g * 4, 4), :]
                                     ).then_inc(s["staged%d" % par], 16)
                stage(0, 0)
                stage(1, 1)
                with sp.Fori(1, NG // 2) as i:
                    for par in range(2):
                        sp.wait_ge(s["ctx"], i * 2 + par - 1)
                        stage(i * 2 + par, par)

            @block.gpsimd
            def _(gp):
                gp.wait_ge(s["maxes"], 1)
                gp.partition_all_reduce(m[:, 2:3], m[:, 0:1], P, RMAX).then_inc(s["all"], 1)

            @block.tensor
            def _(pe):
                def turn_round(g):
                    for q in range(4):
                        h, slot = divmod(q, 2)
                        pe.wait_ge(s["ai"], g * 2 + h + 1)
                        seen(pe, passed)
                        pt = PS[:, q, :].bitcast(BF16)
                        for j in range(4):
                            for c in range(3):
                                o, k = 64 * (j % 2), (j // 2) * 3 + c
                                col = ((j * 2 + slot) * 3 + c) * T
                                mm = pe.transpose(pt[o:o + T, k * PP:(k + 1) * PP], Ai[0:PP, h, col:col + T],
                                                  identb[0:PP, 0:PP])
                        mm.then_inc(s["turned"], 1)

                def products(g, par, n):
                    pe.wait_ge(s["staged%d" % par], n * 48 + 48)
                    for q in range(4):
                        pe.wait_ge(s["at"], g * 4 + q + 1)
                        seen(pe, passed)
                        for j in range(4):
                            for c in range(3):
                                for e in range(2):
                                    o, k, odd = 64 * (j % 2), (j // 2) * 3 + c, j % 2
                                    hd = 4 * c + j
                                    mm = pe.matmul(
                                        PS[64 * e:64 * e + T, 4 + odd, q * HC + k * DH:q * HC + (k + 1) * DH],
                                        AT[o:o + T, q, k * PP + 64 * e:k * PP + 64 * e + T],
                                        Vs[o:o + T, par, int(e != odd), q, hd * DH:(hd + 1) * DH],
                                        start=True, stop=True, skip_group_check=True)
                    mm.then_inc(s["ctx"], 1)

                def turn(i):
                    for par in range(2):
                        g = i * 2 + par
                        products(g, par, i)
                        if not is_last(i) or par == 0:
                            turn_round(g + 1)
                            pe.wait_ge(s["ctx_in"], g * 2 + 2)
                            pe.wait_ge(s["max"], g + 1)
                turn_round(0)
                turns(pe, turn)

            @block.scalar
            def _(act):
                def turned(g):
                    for q in range(4):
                        act.wait_ge(s["turned"], g * 4 + q + 1)
                        act.activation(AT[0:PP, q, :], PS[0:PP, q, :].bitcast(BF16)[:, 0:6 * PP], ACT.Identity
                                       ).then_inc(s["at"], 1)

                def contexts(g):
                    act.wait_ge(s["ctx"], g + 1)
                    for odd in range(2):
                        act.activation(CTX[0:PP, bass.ds(g * 4, 4), odd * HC:(odd + 1) * HC],
                                       PS[0:PP, 4 + odd, 0:4 * HC].rearrange("p (q n) -> p q n", q=4),
                                       ACT.Identity).then_inc(s["ctx_in"], 1)
                turned(0)
                with act.Fori(0, NG - 1) as g:
                    contexts(g)
                    turned(g + 1)
                contexts(NG - 1)

            @block.vector
            def _(v):
                st = straight.on(v)
                st.did(v.memset(m[:, :], 0.0))
                st.settle()
                loop = Steps(v, s["loop_dve"], 1)

                def quantise(g):
                    for h in range(2):
                        e = E[0:PP, bass.ds(g * 2 + h, 1), :].rearrange("p a (r n) -> p (a r) n", n=T)
                        r = RS[0:PP, bass.ds(g * 2 + h, 1), :].rearrange("p a r -> p (a r)")
                        v.tensor_tensor(W[0:PP, h, :].rearrange("p (r n) -> p r n", n=T), e, bcast(r, T, 2),
                                        ALU.mult).then_inc(s["prod"], 1)
                        v.wait_ge(s["prod"], g * 2 + h + 1)
                        if not isinstance(g, int):
                            v.wait_ge(s["turned"], g * 4 + 2 * h - 2)
                        v.tensor_scalar(Ai[0:PP, h, :], W[0:PP, h, :], MAGIC, -MAGIC, ALU.add, ALU.add
                                        ).then_inc(s["ai"], 1)

                def largest(g):
                    loop.turn(g)
                    v.wait_ge(s["ctx_in"], g * 2 + 2)
                    v.tensor_reduce(m[0:PP, 1:2], PS[0:PP, 4:6, 0:4 * HC], AX.XY, ALU.max,
                                    apply_absolute_value=True).then_inc(s["max"], 1)
                    v.wait_ge(s["max"], g + 1)
                    loop.did(v.tensor_tensor(m[:, 0:1], m[:, 0:1], m[:, 1:2], ALU.max))
                    loop.settle()
                    loop.end()
                quantise(0)
                with v.Fori(0, NG - 1) as g:
                    quantise(g + 1)
                    v.wait_ge(s["ai"], g * 2 + 4)
                    largest(g)
                largest(NG - 1)
                v.memset(m[:, 1:2], 0.0).then_inc(s["maxes"], 1)
                v.wait_ge(s["all"], 1)
                sc = Scales(v, st, SC)
                sc.op(15, S_ATT, SC[:, S_V:S_V + 1], None, ALU.mult)
                st.did(v.tensor_scalar(SC[:, S_CTX:S_CTX + 1], m[:, 2:3], SC[:, 15:16], 1e-8, ALU.mult, ALU.max))
                st.settle()
                sc.op(S_CTX, S_CTX, 1.0 / QMAX, None, ALU.mult)
                sc.inverse(16, S_CTX)
                sc.op(16, 16, SC[:, 15:16], None, ALU.mult)


def project_out(nc, straight, passed, sem, sb_, PS, SC, H, identb, norm, rsqrt, CTX, wout, Y, R):
    scope = ExitStack()
    with scope:
        def sb(name, shape, dt=F32):
            return sb_(name, shape, dt, scope)

        s = {n: sem("p7_" + n) for n in ("loop_dve", "cf", "ci", "turned", "cT", "y", "y_in", "max", "var",
                                         "rstd", "norm", "maxes", "all")}
        cf = sb("cf", [P, 4, C])
        Ci = sb("Ci", [P, 4, C], BF16)
        cT = sb("cT", [HC, 2, GT], BF16)
        hx = sb("hx", [P, 3, C])
        hn = sb("hn7", [P, 3, C])
        m = sb("m7", [P, 4])
        LOOP = 10
        with nc.Block() as block:
            @block.gpsimd
            def _(gp):
                with gp.Fori(0, NG) as g:
                    rsqrt(gp, s["var"], s["rstd"], g + 1)
                gp.wait_ge(s["maxes"], 1)
                gp.partition_all_reduce(m[:, 2:3], m[:, 0:1], P, RMAX).then_inc(s["all"], 1)

            @block.scalar
            def _(act):
                with act.Fori(0, NG) as g:
                    act.activation(cf[0:PP, :, :], CTX[0:PP, bass.ds(g * 4, 4), :], ACT.Identity,
                                   scale=SC[0:PP, 16:17], bias=SC[0:PP, 17:18]).then_inc(s["cf"], 1)
                    act.wait_ge(s["turned"], g + 1)
                    pt = PS[0:HC, 0, :].bitcast(BF16)[:, 0:8 * PP].rearrange("p (c q n) -> p c q n", c=2, q=4)
                    for c in range(2):
                        for t0, t1, d0 in ((0, TP, 0), (TP, T, P)):
                            for e in range(2):
                                n = t1 - t0
                                dst = cT[:, c, d0:d0 + GB * n].rearrange("p (q e t) -> p q e t", q=4, e=2)
                                act.activation(dst[:, :, e, :], pt[:, c, :, 64 * e + t0:64 * e + t1], ACT.Identity
                                               ).then_inc(s["cT"], 1)
                    act.wait_ge(s["y"], g + 1)
                    act.activation(Y[:, bass.ds(g * 3, 3), :],
                                   PS[:, 2:4, :].rearrange("p k (j c) -> p (k j) c", c=256)[:, 0:3, 0:C],
                                   ACT.Identity).then_inc(s["y_in"], 1)

            @block.tensor
            def _(pe):
                with pe.Fori(0, NG) as g:
                    pe.wait_ge(s["ci"], g + 1)
                    pt = PS[0:HC, 0, :].bitcast(BF16)
                    for c in range(2):
                        for q in range(4):
                            k = c * 4 + q
                            mm = pe.transpose(pt[:, k * PP:(k + 1) * PP], Ci[0:PP, q, c * HC:(c + 1) * HC],
                                              identb[0:PP, 0:PP])
                    mm.then_inc(s["turned"], 1)
                    pe.wait_ge(s["cT"], g * 8 + 8)
                    for j in range(3):
                        for c in range(2):
                            mm = pe.matmul(PS[:, 2 + j // 2, (j % 2) * 256:(j % 2) * 256 + C],
                                           cT[:, c, j * P:(j + 1) * P], wout[:, c, :], start=c == 0, stop=c == 1)
                    mm.then_inc(s["y"], 1)
                    pe.wait_ge(s["y_in"], g + 1)

            @block.vector
            def _(v):
                st = straight.on(v)
                sc = Scales(v, st, SC)
                st.did(v.memset(m[:, :], 0.0))
                st.did(v.reciprocal(SC[:, 19:20], SC[:, S_X:S_X + 1]))
                st.settle()
                loop = Steps(v, s["loop_dve"], LOOP)
                with v.Fori(0, NG) as g:
                    loop.turn(g)
                    v.wait_ge(s["cf"], g + 1)
                    v.tensor_scalar(Ci[0:PP, :, :], cf[0:PP, :, :], -MAGIC, None, ALU.add).then_inc(s["ci"], 1)
                    loop.did(v.tensor_scalar(hx[:, :, :], H[:, bass.ds(g * 3, 3), :], 1.0, None, ALU.mult))
                    loop.settle()
                    norm(v, loop, hx, hn, s["var"], s["rstd"], g + 1, s["norm"])
                    v.wait_ge(s["norm"], g * 3 + 3)
                    loop.did(v.tensor_scalar(hn[:, :, :], hn[:, :, :], SC[:, 19:20], MAGIC, ALU.mult, ALU.add))
                    loop.settle()
                    loop.did(v.tensor_scalar(R[:, bass.ds(g * 3, 3), :], hn[:, :, :], -MAGIC,
                                             SC[:, S_X:S_X + 1], ALU.add, ALU.mult))
                    v.wait_ge(s["y_in"], g + 1)
                    v.tensor_reduce(m[:, 1:2],
                                    PS[:, 2:4, :].rearrange("p k (j c) -> p (k j) c", c=256)[:, 0:3, 0:C],
                                    AX.XY, ALU.max, apply_absolute_value=True).then_inc(s["max"], 1)
                    v.wait_ge(s["max"], g + 1)
                    loop.did(v.tensor_tensor(m[:, 0:1], m[:, 0:1], m[:, 1:2], ALU.max))
                    loop.settle()
                    v.wait_ge(s["y_in"], g + 1)
                    loop.end()
                v.memset(m[:, 1:2], 0.0).then_inc(s["maxes"], 1)
                v.wait_ge(s["all"], 1)
                sc.op(15, S_CTX, SC[:, S_WOUT:S_WOUT + 1], None, ALU.mult)
                st.did(v.tensor_scalar(SC[:, S_Y:S_Y + 1], m[:, 2:3], SC[:, 15:16], 1e-8, ALU.mult, ALU.max))
                st.settle()
                sc.op(S_Y, S_Y, 1.0 / QMAX, None, ALU.mult)
                sc.inverse(16, S_Y)
                sc.op(16, 16, SC[:, 15:16], None, ALU.mult)


def batch_norm(nc, straight, passed, sem, sb_, PS, SC, H, ident, neghalf, Y, R):
    scope = ExitStack()
    with scope:
        def sb(name, shape, dt=F32):
            return sb_(name, shape, dt, scope)

        s = {n: sem("p8_" + n) for n in ("ones", "r", "mean", "centred", "square", "var", "vard", "column",
                                         "columns_in", "pow", "diag", "spread", "maxes", "all")}
        ones = sb("ones8", [P, P])
        SQ = sb("SQ", [P, NT, C])
        vr = sb("vr", [P, C])
        one = sb("one8", [HC, P])
        vc = sb("vc", [HC, 2])
        diag = sb("diag", [HC, 2, HC])
        m = sb("m8", [P, 2])
        with nc.Block() as block:
            @block.gpsimd
            def _(gp):
                gp.memset(ones[:, :], 1.0 / (B * T)).then_inc(s["ones"], 1)
                gp.memset(one[:, :], 1.0).then_inc(s["ones"], 1)
                gp.wait_ge(s["columns_in"], 1)
                gp.tensor_tensor(out=vc[:, :], in0=vc[:, :], in1=neghalf[0:HC, 0:2], op=ALU.pow
                                 ).then_inc(s["pow"], 1)
                gp.wait_ge(s["maxes"], 1)
                gp.partition_all_reduce(m[:, 1:2], m[:, 0:1], P, RMAX).then_inc(s["all"], 1)

            @block.scalar
            def _(act):
                for k in range(NQ):
                    act.wait_ge(s["centred"], k + 1)
                    act.activation(SQ[:, k * QT:(k + 1) * QT, :], R[:, k * QT:(k + 1) * QT, :], ACT.Square
                                   ).then_inc(s["square"], 1)

            @block.tensor
            def _(pe):
                pe.wait_ge(s["ones"], 2)
                for n, (src, ready, done) in enumerate(((R, "r", "mean"), (SQ, "square", "var"))):
                    for k in range(NT):
                        if k % QT == 0:
                            pe.wait_ge(s[ready], k // QT + 1)
                        mm = pe.matmul(PS[:, n, 0:C], ones[:, :], src[:, k, :], start=k == 0, stop=k == NT - 1)
                    mm.then_inc(s[done], 1)
                pe.wait_ge(s["vard"], 1)
                for c in range(2):
                    mm = pe.matmul(PS[0:HC, 2, c:c + 1], vr[0:1, c * HC:(c + 1) * HC], one[0:1, 0:1],
                                   start=True, stop=True)
                mm.then_inc(s["column"], 1)
                pe.wait_ge(s["diag"], 2)
                for c in range(2):
                    mm = pe.matmul(PS[:, 3, c * HC:(c + 1) * HC], one[:, :], diag[:, c, :], start=True, stop=True)
                mm.then_inc(s["spread"], 1)

            @block.vector
            def _(v):
                st = straight.on(v)
                sc = Scales(v, st, SC)
                quarters = [slice(k * QT, (k + 1) * QT) for k in range(NQ)]
                for q in quarters:
                    st.did(v.tensor_scalar(Y[:, q, :], Y[:, q, :], SC[:, 16:17], MAGIC, ALU.mult, ALU.add))
                    st.settle()
                    st.did(v.tensor_scalar(Y[:, q, :], Y[:, q, :], -MAGIC, SC[:, S_Y:S_Y + 1], ALU.add, ALU.mult))
                    st.settle()
                    v.tensor_tensor(R[:, q, :], R[:, q, :], Y[:, q, :], ALU.add).then_inc(s["r"], 1)
                v.wait_ge(s["mean"], 1)
                v.wait_ge(s["r"], NQ)
                for q in quarters:
                    v.tensor_tensor(R[:, q, :], R[:, q, :], bcast(PS[:, 0, 0:C], QT, 1), ALU.subtract
                                    ).then_inc(s["centred"], 1)
                v.wait_ge(s["var"], 1)
                v.tensor_scalar(vr[:, :], PS[:, 1, 0:C], EPS, None, ALU.add).then_inc(s["vard"], 1)
                v.wait_ge(s["column"], 1)
                v.tensor_copy(vc[:, :], PS[0:HC, 2, 0:2]).then_inc(s["columns_in"], 1)
                v.wait_ge(s["pow"], 1)
                for c in range(2):
                    v.tensor_scalar(diag[:, c, :], ident[0:HC, 0:HC], vc[:, c:c + 1], None, ALU.mult
                                    ).then_inc(s["diag"], 1)
                v.wait_ge(s["spread"], 1)
                v.wait_ge(s["centred"], NQ)
                for q in quarters:
                    st.did(v.tensor_tensor(R[:, q, :], R[:, q, :], bcast(PS[:, 3, 0:C], QT, 1), ALU.mult))
                st.settle()
                v.tensor_reduce(m[:, 0:1], R[:, :, :], AX.XY, ALU.max, apply_absolute_value=True
                                ).then_inc(s["maxes"], 1)
                v.wait_ge(s["all"], 1)
                st.did(v.tensor_scalar(SC[:, S_RN:S_RN + 1], m[:, 1:2], 1e-8, 1.0 / QMAX, ALU.max, ALU.mult))
                st.settle()
                sc.inverse(16, S_RN)
                st.did(v.tensor_scalar(R[:, :, :], R[:, :, :], SC[:, 16:17], MAGIC, ALU.mult, ALU.add))
                st.settle()
                st.did(v.tensor_scalar(R[:, :, :], R[:, :, :], -MAGIC, SC[:, S_RN:S_RN + 1], ALU.add, ALU.mult))
                st.settle()
                st.did(v.tensor_tensor(H[:, :, :], H[:, :, :], R[:, :, :], ALU.add))
                st.settle()


def route(nc, straight, passed, a, sem, sb_, PS, H, ident, norm, rsqrt, W1, W2, GK, slots, owner, X_rows):
    scope = ExitStack()
    with scope:
        def sb(name, shape, dt=F32):
            return sb_(name, shape, dt, scope)

        s = {n: sem("p9_" + n) for n in ("weights", "var", "rstd", "norm", "turned", "xs", "kept", "logits",
                                         "shifted", "exp", "loop_dve", "part", "importance", "experts",
                                         "zero", "cleared", "chosen", "ranks", "slots", "sent")}
        rw = sb("rw", [HC, 2, NE])
        iota8 = sb("iota8", [P, NE])
        hx = sb("hx9", [P, 3, C])
        hn = sb("hn9", [P, 3, C])
        xs = sb("xs9", [HC, 2, GT])
        lg = sb("lg", [P, 3, NE])
        ex = sb("ex9", [P, 3, NE])
        t3 = sb("t3", [P, 3, 3])
        PR = sb("PR", [P, NT, NE])
        top = sb("top", [P, NT, 8])
        idx = sb("idx", [P, NT, 8], U32)
        idf = sb("idf", [P, NT, 8])
        one = sb("one9", [P, 2, NT, NE])
        imp = sb("imp", [P, 2, NE])
        G = sb("G", [P, NT, NE])
        XN = sb("XN", [P, NT, C])
        zero = sb("zero", [P, C])
        tri = sb("tri", [P, P])
        ones = sb("ones9", [P, P])
        blocks = sb("blocks", [P, NBLK])
        sel = sb("sel", [P, NT, NE])
        tot = sb("tot", [P, NE, NT])
        incl = sb("incl", [P, NE, NT])
        off = sb("off", [P, NE, NT])
        goon = sb("goon", [P, NE, NT])
        nb = sb("nb", [P, 4, NE])
        pick = sb("pick", [P, 2, NT, NE])
        slf = sb("slf", [P, 2, NT])
        own = sb("own", [P, NBLK, NE])
        ownf = sb("ownf", [P, NBLK])
        den = sb("den9", [P, NT])
        LOOP = 11
        with nc.Block() as block:
            @block.sync
            def _(sp):
                sp.dma_start(rw[:, :, :], a["router"]).then_inc(s["weights"], 16)
                sp.dma_start(iota8[:, :], a["iota8"].to_broadcast([P, NE])).then_inc(s["weights"], 16)
                sp.dma_start(tri[:, :], a["tri"]).then_inc(s["weights"], 16)
                sp.dma_start(blocks[:, :], a["blocks"].to_broadcast([P, NBLK])).then_inc(s["weights"], 16)
                sp.wait_ge(s["zero"], 1)
                sp.dma_start(X_rows.rearrange("(p b) c -> p b c", p=P), bcast(zero[:, :], NBLK, 1)
                             ).then_inc(s["cleared"], 16)
                sp.dma_start(W1[:, :, :], a["w1"]).then_inc(s["experts"], 16)
                sp.dma_start(W2[:, :, :], a["w2"]).then_inc(s["experts"], 16)
                sp.wait_ge(s["experts"], 32)

            @block.gpsimd
            def _(gp):
                with gp.Fori(0, NG) as g:
                    rsqrt(gp, s["var"], s["rstd"], g + 1)
                    gp.wait_ge(s["norm"], g * 3 + 3)
                    seen(gp, passed)
                    gp.tensor_copy(XN[:, bass.ds(g * 3, 3), :], hn[:, :, :]).then_inc(s["kept"], 1)
                gp.wait_ge(s["part"], 1)
                gp.partition_all_reduce(imp[:, 1, :], imp[:, 0, :], P, RADD).then_inc(s["importance"], 1)
                gp.wait_ge(s["slots"], 1)
                gp.wait_ge(s["cleared"], 16)
                gp.wait_ge(s["kept"], NG)
                for t in range(NT):
                    for k in range(2):
                        gp.indirect_dma_start(X_rows, bass.IndirectOffsetOnAxis(slots[:, k, t:t + 1], 0),
                                              XN[:, t, :], None).then_inc(s["sent"], 16)
                gp.wait_ge(s["sent"], 16 * 2 * NT)

            @block.tensor
            def _(pe):
                pe.wait_ge(s["weights"], 64)
                with pe.Fori(0, NG) as g:
                    pe.wait_ge(s["norm"], g * 3 + 3)
                    for c in range(2):
                        for j in range(3):
                            mm = pe.transpose(PS[0:HC, c, j * P:(j + 1) * P], hn[:, j, c * HC:(c + 1) * HC],
                                              ident[:, :])
                    mm.then_inc(s["turned"], 1)
                    pe.wait_ge(s["xs"], g * 2 + 2)
                    for j in range(3):
                        for c in range(2):
                            mm = pe.matmul(PS[:, 2, j * NE:(j + 1) * NE], xs[:, c, j * P:(j + 1) * P], rw[:, c, :],
                                           start=c == 0, stop=c == 1)
                    mm.then_inc(s["logits"], 1)
                pe.wait_ge(s["chosen"], 1)
                for n, w in enumerate((tri, ones)):
                    mm = pe.matmul(PS[:, 3 + n, 0:NT * NE], w[:, :], sel[:, :, :].rearrange("p t e -> p (t e)"),
                                   start=True, stop=True)
                mm.then_inc(s["ranks"], 1)

            @block.scalar
            def _(act):
                with act.Fori(0, NG) as g:
                    act.wait_ge(s["turned"], g + 1)
                    for c in range(2):
                        act.activation(xs[:, c, :], PS[0:HC, c, 0:GT], ACT.Identity).then_inc(s["xs"], 1)
                    act.wait_ge(s["shifted"], g + 1)
                    act.activation(ex[:, :, :], lg[:, :, :], ACT.Exp).then_inc(s["exp"], 1)

            @block.vector
            def _(v):
                st = straight.on(v)
                v.memset(zero[:, :], 0.0).then_inc(s["zero"], 1)
                st.did(v.memset(ones[:, :], 1.0))
                st.did(v.memset(goon[:, :, 1:NT], 1.0))
                st.did(v.memset(goon[:, :, 0:1], 0.0))
                loop = Steps(v, s["loop_dve"], LOOP)
                with v.Fori(0, NG) as g:
                    loop.turn(g)
                    loop.did(v.tensor_scalar(hx[:, :, :], H[:, bass.ds(g * 3, 3), :], 1.0, None, ALU.mult))
                    loop.settle()
                    norm(v, loop, hx, hn, s["var"], s["rstd"], g + 1, s["norm"])
                    v.wait_ge(s["logits"], g + 1)
                    z = PS[:, 2, 0:3 * NE].rearrange("p (j e) -> p j e", e=NE)
                    loop.did(v.tensor_reduce(t3[:, 0, :], z, AX.X, ALU.max))
                    loop.settle()
                    v.tensor_tensor(lg[:, :, :], z, bcast(t3[:, 0, :], NE, 2), ALU.subtract
                                    ).then_inc(s["shifted"], 1)
                    v.wait_ge(s["exp"], g + 1)
                    loop.did(v.tensor_reduce(t3[:, 1, :], ex[:, :, :], AX.X, ALU.add))
                    loop.settle()
                    loop.did(v.reciprocal(t3[:, 2, :], t3[:, 1, :]))
                    loop.settle()
                    loop.did(v.tensor_tensor(PR[:, bass.ds(g * 3, 3), :], ex[:, :, :], bcast(t3[:, 2, :], NE, 2),
                                             ALU.mult))
                    loop.settle()
                    v.wait_ge(s["kept"], g + 1)
                    seen(v, passed)
                    loop.end()
                v.wait_ge(s["loop_dve"], LOOP * NG)
                v.tensor_reduce(imp[:, 0, :], PR[:, :, :].rearrange("p t e -> p e t"), AX.X, ALU.add
                                ).then_inc(s["part"], 1)
                for t in range(NT):
                    st.did(v.max(top[:, t, :], PR[:, t, :]))
                st.settle()
                for t in range(NT):
                    st.did(v.max_index(idx[:, t, :], top[:, t, :], PR[:, t, :]))
                st.settle()
                st.did(v.tensor_copy(idf[:, :, :], idx[:, :, :]))
                v.wait_ge(s["weights"], 64)
                st.settle()
                for k in range(2):
                    st.did(v.tensor_tensor(one[:, k, :, :], bcast(iota8[:, :], NT, 1),
                                           idf[:, :, k:k + 1].broadcast_to([P, NT, NE]), ALU.is_equal))
                st.settle()
                v.tensor_tensor(sel[:, :, :], one[:, 0, :, :], one[:, 1, :, :], ALU.add).then_inc(s["chosen"], 1)
                v.wait_ge(s["ranks"], 1)
                st.did(v.tensor_copy(tot[:, :, :], PS[:, 4, 0:NT * NE].rearrange("p (t e) -> p e t", e=NE)))
                st.settle()

                def flat(x):
                    return x.rearrange("p e t -> p (e t)")

                st.did(v.tensor_tensor_scan(flat(incl[:, :, :]), flat(goon[:, :, :]), flat(tot[:, :, :]), 0.0,
                                            ALU.mult, ALU.add))
                st.settle()
                st.did(v.tensor_scalar(nb[:, 0, :], incl[:, :, NT - 1], 1.0 / P, (P - 1) / P - 0.5 + 0.5 / P,
                                       ALU.mult, ALU.add))
                st.did(v.tensor_tensor(off[:, :, :], incl[:, :, :], tot[:, :, :], ALU.subtract))
                st.settle()
                st.did(v.tensor_scalar(nb[:, 1, :], nb[:, 0, :], MAGIC, None, ALU.add))
                st.settle()
                st.did(v.tensor_scalar(nb[:, 0, :], nb[:, 1, :], -MAGIC, None, ALU.add))
                st.settle()
                st.did(v.tensor_tensor_scan(nb[:, 2, :], ones[:, 0:NE], nb[:, 0, :], 0.0, ALU.mult, ALU.add))
                st.settle()
                st.did(v.tensor_tensor(nb[:, 3, :], nb[:, 2, :], nb[:, 0, :], ALU.subtract))
                st.settle()
                st.did(v.scalar_tensor_tensor(off[:, :, :], bcast(nb[:, 3, :], NT, 2), float(P), off[:, :, :],
                                              ALU.mult, ALU.add))
                st.settle()
                st.did(v.tensor_tensor(off[:, :, :], off[:, :, :],
                                       PS[:, 3, 0:NT * NE].rearrange("p (t e) -> p e t", e=NE), ALU.add))
                st.settle()
                for k in range(2):
                    st.did(v.tensor_tensor(pick[:, k, :, :], one[:, k, :, :],
                                           off[:, :, :].rearrange("p e t -> p t e"), ALU.mult))
                st.settle()
                for k in range(2):
                    st.did(v.tensor_reduce(slf[:, k, :], pick[:, k, :, :], AX.X, ALU.add))
                st.settle()
                v.tensor_copy(slots[:, :, :], slf[:, :, :]).then_inc(s["slots"], 1)
                st.did(v.tensor_tensor(own[:, :, :], bcast(blocks[:, :], NE, 2), bcast(nb[:, 2, :], NBLK, 1),
                                       ALU.is_ge))
                st.settle()
                st.did(v.tensor_reduce(ownf[:, :], own[:, :, :], AX.X, ALU.add))
                st.settle()
                st.did(v.tensor_scalar(ownf[:, :], ownf[:, :], float(NE - 1), None, ALU.min))
                st.settle()
                st.did(v.tensor_copy(owner[:, :], ownf[:, :]))
                v.wait_ge(s["importance"], 1)
                st.did(v.tensor_scalar(imp[:, 0, :], imp[:, 1, :], -1.0, 1.0 - 0.9, ALU.add, ALU.mult))
                st.settle()
                st.did(v.tensor_scalar(imp[:, 0, :], imp[:, 0, :], 1.0, 0.01, ALU.add, ALU.add))
                st.settle()
                st.did(v.reciprocal(imp[:, 1, :], imp[:, 0, :]))
                st.settle()
                st.did(v.tensor_tensor(PR[:, :, :], PR[:, :, :], bcast(imp[:, 1, :], NT, 1), ALU.mult))
                st.settle()
                st.did(v.tensor_tensor(PR[:, :, :], PR[:, :, :], sel[:, :, :], ALU.mult))
                st.settle()
                st.did(v.tensor_reduce(den[:, :], PR[:, :, :], AX.X, ALU.add))
                st.settle()
                st.did(v.reciprocal(den[:, :], den[:, :]))
                st.settle()
                st.did(v.tensor_tensor(G[:, :, :], PR[:, :, :], bcast(den[:, :], NE, 2), ALU.mult))
                st.settle()
                for k in range(2):
                    st.did(v.tensor_tensor(pick[:, k, :, :], one[:, k, :, :], G[:, :, :], ALU.mult))
                st.settle()
                for k in range(2):
                    st.did(v.tensor_reduce(GK[:, k, :], pick[:, k, :, :], AX.X, ALU.add))
                st.settle()


def experts(nc, sem, sb_, PS, ident, W1, W2, owner, X_rows, Y_rows):
    scope = ExitStack()
    with scope:
        def sb(name, shape, dt=F32):
            return sb_(name, shape, dt, scope)

        s = {n: sem("p10_" + n) for n in ("x0", "x1", "turned", "xT", "up", "silu", "h_turned", "hT", "down", "y",
                                          "y_out0", "y_out1")}
        xb = sb("xb", [P, 2, C])
        xT = sb("xT10", [HC, 2, 2, P])
        h = sb("h10", [P, 2, ID])
        hT = sb("hT10", [P, 2, ID])
        yb = sb("yb", [P, 2, C])

        def steps(eng, step, first, last):
            for b in range(first):
                step(b, b % 2, b // 2)
            with eng.Fori(first // 2, last // 2) as i:
                for par in range(2):
                    step(i * 2 + par, par, i)
            for b in range(last, NBLK):
                step(b, b % 2, b // 2)

        def static(b):
            return isinstance(b, int)

        with nc.Block() as block:
            @block.sync
            def _(sp):
                def load(b, par, n):
                    if not static(b) or b >= 2:
                        sp.wait_ge(s["turned"], b - 1)
                    sp.dma_start(xb[:, par, :], X_rows[bass.ds(b * P, P), :]).then_inc(s["x%d" % par], 16)
                steps(sp, load, 2, NBLK - 1)

            @block.gpsimd
            def _(gp):
                def store(b, par, n):
                    gp.wait_ge(s["y"], b + 1)
                    gp.dma_start(Y_rows[bass.ds(b * P, P), :], yb[:, par, :]).then_inc(s["y_out%d" % par], 16)
                steps(gp, store, 2, NBLK - 1)
                for par in range(2):
                    gp.wait_ge(s["y_out%d" % par], 16 * ((NBLK + 1 - par) // 2))

            @block.tensor
            def _(pe):
                def turn(b, par, n):
                    pe.wait_ge(s["x%d" % par], n * 16 + 16)
                    for c in range(2):
                        mm = pe.transpose(PS[0:HC, par, c * P:(c + 1) * P], xb[:, par, c * HC:(c + 1) * HC],
                                          ident[:, :])
                    mm.then_inc(s["turned"], 1)

                def up(b, par, e):
                    pe.wait_ge(s["xT"], b + 1)
                    for c in range(2):
                        mm = pe.matmul(PS[:, 2 + par, :], xT[:, par, c, :],
                                       W1[:, bass.ds(e * 2 + c, 1), :].rearrange("p a n -> p (a n)"),
                                       start=c == 0, stop=c == 1)
                    mm.then_inc(s["up"], 1)

                def turn_hidden(b, par):
                    pe.wait_ge(s["silu"], b + 1)
                    for m in range(4):
                        mm = pe.transpose(PS[:, 4 + par, m * P:(m + 1) * P], h[:, par, m * P:(m + 1) * P],
                                          ident[:, :])
                    mm.then_inc(s["h_turned"], 1)

                def down(b, par, e):
                    pe.wait_ge(s["hT"], b + 1)
                    if not static(b) or b >= 2:
                        pe.wait_ge(s["y"], b - 1)
                    for m in range(4):
                        mm = pe.matmul(PS[:, 6 + par, 0:C], hT[:, par, m * P:(m + 1) * P],
                                       W2[:, bass.ds(e * 4 + m, 1), :].rearrange("p a n -> p (a n)"),
                                       start=m == 0, stop=m == 3)
                    mm.then_inc(s["down"], 1)

                def expert(b):
                    return pe.value_load(owner[0:1, bass.ds(b, 1)], min_val=0, max_val=NE - 1)

                def step(b, par, n):
                    turn_hidden(b, par)
                    if not static(b) or b + 1 < NBLK:
                        up(b + 1, 1 - par, expert(b + 1))
                    down(b, par, expert(b))
                    if not static(b) or b + 2 < NBLK:
                        turn(b + 2, par, n + 1)

                turn(0, 0, 0)
                turn(1, 1, 0)
                up(0, 0, expert(0))
                steps(pe, step, 2, NBLK - 3)

            @block.scalar
            def _(act):
                def taken(b, par, n):
                    act.wait_ge(s["turned"], b + 1)
                    if not static(b) or b >= 2:
                        act.wait_ge(s["up"], b - 1)
                    act.activation(xT[:, par, :, :], PS[0:HC, par, 0:2 * P].rearrange("p (c n) -> p c n", c=2),
                                   ACT.Copy).then_inc(s["xT"], 1)

                def silu(b, par, n):
                    act.wait_ge(s["up"], b + 1)
                    if not static(b) or b >= 2:
                        act.wait_ge(s["h_turned"], b - 1)
                    act.activation(h[:, par, :], PS[:, 2 + par, :], ACT.Silu).then_inc(s["silu"], 1)

                def step(b, par, n):
                    silu(b - 1, 1 - par, n)
                    taken(b, par, n)

                taken(0, 0, 0)
                taken(1, 1, 0)
                silu(0, 0, 0)
                silu(1, 1, 0)
                taken(2, 0, 1)
                silu(2, 0, 1)
                taken(3, 1, 1)
                with act.Fori(2, (NBLK - 1) // 2) as i:
                    for par in range(2):
                        step(i * 2 + par, par, i)
                step(NBLK - 1, 0, NBLK // 2)
                silu(NBLK - 1, 0, NBLK // 2)

            @block.vector
            def _(v):
                def step(b, par, n):
                    v.wait_ge(s["h_turned"], b + 1)
                    if not static(b) or b >= 2:
                        v.wait_ge(s["down"], b - 1)
                    v.tensor_copy(hT[:, par, :], PS[:, 4 + par, :]).then_inc(s["hT"], 1)
                    v.wait_ge(s["down"], b + 1)
                    if not static(b) or b >= 2:
                        v.wait_ge(s["y_out%d" % par], n * 16)
                    v.tensor_copy(yb[:, par, :], PS[:, 6 + par, 0:C]).then_inc(s["y"], 1)
                steps(v, step, 2, NBLK - 1)


def combine(nc, passed, sem, sb_, H, GK, slots, Y_rows, out):
    scope = ExitStack()
    with scope:
        s = {n: sem("p11_" + n) for n in ["rows%d" % q for q in range(NQ)] + ["added", "stored"]}
        yk = sb_("yk", [P, 2, NT, C], F32, scope)
        with nc.Block() as block:
            @block.gpsimd
            def _(gp):
                for q in range(NQ):
                    for t in range(q * QT, (q + 1) * QT):
                        for k in range(2):
                            gp.indirect_dma_start(yk[:, k, t, :], None, Y_rows,
                                                  bass.IndirectOffsetOnAxis(slots[:, k, t:t + 1], 0)
                                                  ).then_inc(s["rows%d" % q], 16)

            @block.vector
            def _(v):
                for q in range(NQ):
                    v.wait_ge(s["rows%d" % q], 16 * 2 * QT)
                    for k in range(2):
                        for t in range(q * QT, (q + 1) * QT):
                            ins = v.scalar_tensor_tensor(H[:, t, :], yk[:, k, t, :], GK[:, k, t:t + 1], H[:, t, :],
                                                         ALU.mult, ALU.add)
                        ins.then_inc(s["added"], 1)
                        v.wait_ge(s["added"], 2 * q + k + 1)

            @block.sync
            def _(sp):
                for q in range(NQ):
                    sp.wait_ge(s["added"], 2 * q + 2)
                    sp.dma_start(out[:, q * QT:(q + 1) * QT, :], H[:, q * QT:(q + 1) * QT, :]
                                 ).then_inc(s["stored"], 16)
                sp.wait_ge(s["stored"], 16 * NQ)


def embed_and_mix(nc, straight, passed, a, sem, sb_, PS, H, ident, identb, neghalf, norm, rsqrt):
    scope = ExitStack()
    with scope:
        def sb(name, shape, dt=F32):
            return sb_(name, shape, dt, scope)

        px = sb("px", [P, KC, P])
        tb = sb("tb", [P, 2, C])
        cw = sb("cw", [P, KC, C])
        pos = sb("pos", [P, C])
        cb = sb("cb", [P, C])
        lnv = sb("lnv", [HC, 4, 2])
        wkvr = sb("wkvr", [HC, 2, 3, C])
        wo = sb("wo", [P, 2, C])
        wkf = sb("wkf", [HC, 2, HID])
        wrf = sb("wrf", [HC, 2, C])
        wvf = sb("wvf", [P, HCH, C])
        dec = sb("dec", [P, 2, 2])
        Wf = sb("Wf", [P, 2 * ROWS, TS])
        Uf = sb("Uf", [P, ROWS, T])
        em = sb("em", [P, C])
        hc = sb("hc", [P, 3, C])
        x0 = sb("x0", [P, 3, C])
        hck = sb("hck", [P, 3, C])
        x0k = sb("x0k", [P, 3, C])
        hn = sb("hn", [P, 3, C])
        hT = sb("hT", [HC, 2, GT])
        KK = sb("KK", [P, 2 * ROWS, TS])
        VV = sb("VV", [P, 2 * ROWS, TS])
        SR = sb("SR", [P, ROWS, T])
        M = sb("M", [P, 1 + 2 * ROWS * TS])
        A = sb("A", [P, 1 + 2 * ROWS * TS])
        Bd = sb("Bd", [P, 1 + 2 * ROWS * TS])
        E1 = sb("E1", [P, 2 * ROWS, TS])
        E2 = sb("E2", [P, 2 * ROWS, TS])
        EV = sb("EV", [P, 2 * ROWS, TS])
        EX = sb("EX", [P, 3, ROWS, T])
        MM = sb("MM", [P, ROWS, T])
        N1 = sb("N1", [P, 3, ROWS, T])
        D1 = sb("D1", [P, 2, ROWS, T])
        YP = sb("YP", [P, ROWS, TP])
        YX = sb("YX", [P, ROWS, TX])
        kf = sb("kf", [P, HCH, GT])
        hn2 = sb("hn2a", [P, 3, C])
        hT2 = sb("hT2", [HC, 2, GT])
        xh = sb("xh", [P, 3, C])
        x1 = sb("x1", [P, 3, C])
        gate = sb("gate1", [P, 3, C])
        ff = sb("ff1", [P, 3, C])

        psT = PS[:, 0:2, :]
        psK, psV, psR = PS[:, 2:4, :], PS[:, 4:6, :], PS[:, 6:8, :]

        def rows(ps):
            return ps.rearrange("p k (r t) -> p (k r) t", t=64)

        def flat(ap):
            return ap.rearrange("p r t -> p (r t)")

        def before(buf):
            v = buf[:, 1:1 + 2 * ROWS * TS].rearrange("p (r t) -> p r t", t=TS)
            return v[:, 0:ROWS, 0:T], v[:, ROWS:2 * ROWS, T - 1::-1]

        s = {n: sem("p1_" + n) for n in (
            "weights", "consts", "setup", "inputs", "embedded", "text_taken", "var", "rstd",
            "norm1", "turned1", "hT", "kvr", "k_in", "v_in", "r_in", "m", "d2", "e1", "e2", "ev", "ku", "mm",
            "ex", "dpart", "y", "attn", "norm2", "turned2", "hT2", "up", "relu", "gatemm", "gate", "down",
            "pool", "relu0", "done", "loop_dve", "back_dve", "norm_dve", "var2", "rstd2", "hc_free", "b_scan",
            "a_scan", "patches_out", "patches_in", "kept", "x1")}
        NW = 19
        NORM_DVE, FRONT_DVE, BACK_DVE = 15, 14, 7

        with nc.Block() as block:
            @block.sync
            def _(sp):
                def load(dst, src):
                    sp.dma_start(dst, src).then_inc(s["weights"], 16)
                for k in range(GB):
                    load(pos[TP * k:TP * (k + 1), :], a["pos"])
                load(cb[:, :], a["conv_b"].to_broadcast([P, C]))
                load(cw[:, :, :], a["conv_w"])
                load(lnv[:, :, :], a["ln"])
                load(wkvr[:, :, :, :], a["w_kvr"])
                load(dec[:, :, :], a["decfirst"])
                load(wo[:, 0, :], a["Wo"][0:P, :])
                load(wo[0:64, 1, :], a["Wo"][P:C, :])
                load(wo[64:P, 1, :], a["Wo"][P:C, :])
                sp.dma_start(px[:, :, :], a["patches"][0]).then_inc(s["inputs"], 16)
                sp.dma_start(tb[:, :, :], a["text"][0]).then_inc(s["inputs"], 16)
                with sp.Fori(1, NG) as g:
                    sp.wait_ge(s["embedded"], g)
                    sp.wait_ge(s["text_taken"], g)
                    sp.dma_start(px[:, :, :], a["patches"][bass.ds(g, 1)].rearrange("g p k m -> p (g k) m")
                                 ).then_inc(s["inputs"], 16)
                    sp.dma_start(tb[:, :, :], a["text"][bass.ds(g, 1)].rearrange("g p j c -> p (g j) c")
                                 ).then_inc(s["inputs"], 16)

            @block.gpsimd
            def _(gp):
                st = Steps(gp, s["pool"])
                st.did(gp.memset(ident[:, :], 0.0))
                st.did(gp.memset(identb[:, :], 0.0))
                st.did(gp.memset(neghalf[:, :], -0.5))
                st.did(gp.memset(KK[:, :, 0:1], NEG))
                st.did(gp.memset(VV[:, :, 0:1], 0.0))
                st.settle()
                for m in (ident, identb):
                    st.did(gp.affine_select(out=m[:, :], in_=m[:, :], compare_op=ALU.not_equal, fill=1.0,
                                            base=0, pattern=[[-1, P]], channel_multiplier=1))
                st.settle()
                st.did(gp.memset(A[:, 0:1], 0.0))
                st.did(gp.memset(Bd[:, 0:1], 0.0))
                st.settle()
                gp.memset(M[:, 0:1], 0.0).then_inc(s["consts"], 1)

                def front(g, norms=True, last=None):
                    gp.wait_ge(s["m"], g + 1)
                    gp.wait_ge(s["setup"], 1)
                    gp.tensor_tensor(out=flat(E2[:, :, :]), in0=flat(KK[:, :, :]),
                                     in1=M[:, 1:1 + 2 * ROWS * TS], op=ALU.subtract).then_inc(s["d2"], 1)
                    gp.tensor_tensor(out=EX[:, 2, :, :], in0=KK[:, 0:ROWS, 1:TS], in1=Uf[:, :, :],
                                     op=ALU.add).then_inc(s["ku"], 1)
                    if last is not None:
                        rsqrt(gp, s["var2"], s["rstd2"], last + 1)
                    if norms:
                        rsqrt(gp, s["var"], s["rstd"], g * 2 + 3)
                    gp.wait_ge(s["e2"], g + 1)
                    gp.tensor_tensor(out=flat(EV[:, :, :]), in0=flat(E2[:, :, :]), in1=flat(VV[:, :, :]),
                                     op=ALU.mult).then_inc(s["ev"], 1)
                    if norms:
                        rsqrt(gp, s["var"], s["rstd"], g * 2 + 4)
                    gp.wait_ge(s["ex"], g + 1)
                    gp.wait_ge(s["b_scan"], g + 1)
                    bf, bb = before(Bd)
                    gp.tensor_tensor(out=D1[:, 0, :, :], in0=EX[:, 0, :, :], in1=bf, op=ALU.mult
                                     ).then_inc(s["dpart"], 1)
                    gp.tensor_tensor(out=D1[:, 1, :, :], in0=EX[:, 1, :, :], in1=bb, op=ALU.mult
                                     ).then_inc(s["dpart"], 1)

                rsqrt(gp, s["var"], s["rstd"], 1)
                rsqrt(gp, s["var"], s["rstd"], 2)
                front(0)
                with gp.Fori(0, NG - 2) as g:
                    front(g + 1, last=g)
                front(NG - 1, norms=False, last=NG - 2)
                rsqrt(gp, s["var2"], s["rstd2"], NG)

            @block.tensor
            def _(pe):
                pe.wait_ge(s["weights"], 16 * NW)
                pe.wait_ge(s["consts"], 1)

                def turn(src, ready, turned):
                    pe.wait_ge(*ready)
                    for c in range(2):
                        for j in range(3):
                            mm = pe.transpose(psT[0:HC, c, j * P:(j + 1) * P],
                                              src[:, j, c * HC:(c + 1) * HC], ident[:, :])
                    mm.then_inc(turned, 1)

                def embed(g):
                    pe.wait_ge(s["inputs"], g * 32 + 32)
                    for k in range(KC):
                        mm = pe.matmul(psT[:, 0, 0:C], px[:, k, :], cw[:, k, :], start=k == 0, stop=k == KC - 1)
                    mm.then_inc(s["embedded"], 1)

                def part(w, ps):
                    for half in range(2):
                        tok = slice(half * GT // 2, (half + 1) * GT // 2)
                        r = rows(ps)
                        for c in range(2):
                            pe.matmul(r[:, half * 4:half * 4 + 4, 0:T], wkvr[:, c, w, 0:P], hT[:, c, tok],
                                      start=c == 0, stop=c == 1)
                        for c in range(2):
                            mm = pe.matmul(r[64 * half:64 * half + 64, GB:GB + 4, 0:T],
                                           wkvr[:, c, w, P:C], hT[:, c, tok], start=c == 0, stop=c == 1)
                    mm.then_inc(s["kvr"], 1)

                def keys(g):
                    turn(hn, (s["norm1"], g * 3 + 3), s["turned1"])
                    pe.wait_ge(s["hT"], g * 4 + 4)
                    pe.wait_ge(s["done"], g if not isinstance(g, int) or g else 1)
                    part(0, psK)

                def values_and_receptance():
                    part(1, psV)
                    part(2, psR)

                def project(g):
                    pe.wait_ge(s["y"], g * 2 + 2)
                    for j, (Y, r0, nr) in enumerate(((YP, 0, 8), (YX, 0, 4), (YX, 4, 4))):
                        Y = Y[:, :, :]
                        up = Y[:, r0:r0 + nr, :].rearrange("p r t -> p (r t)")
                        low = Y[:, GB:ROWS, :].rearrange("p r t -> p (r t)")
                        o = psT[:, j // 2, (j % 2) * 256:(j % 2) * 256 + C]
                        pe.matmul(o, up, wo[:, 0, :], start=True, stop=False,
                                  skip_group_check=True)
                        if j == 0:
                            for q in (0, 64):
                                mm = pe.matmul(o[q:q + 64, :], low[q:q + 64, :], wo[q:q + 64, 1, :],
                                               start=False, stop=True, skip_group_check=True)
                        else:
                            q = 64 * (j - 1)
                            mm = pe.matmul(o, low[q:q + 64, :], wo[q:q + 64, 1, :],
                                           start=False, stop=True, skip_group_check=True)
                    mm.then_inc(s["attn"], 1)

                def channel_mix(g, last=False):
                    turn(hn2, (s["norm2"], g * 3 + 3), s["turned2"])
                    pe.wait_ge(s["hT2"], g * 2 + 2)
                    for m in range(HCH):
                        if not last and m % 2 == 0:
                            got, n = (("k_in", 2), ("v_in", 2), ("r_in", 1))[m // 2]
                            pe.wait_ge(s[got], (g + 2) * n)
                        for c in range(2):
                            mm = pe.matmul(PS[:, 2 + m, 0:GT], wkf[:, c, m * P:(m + 1) * P], hT2[:, c, :],
                                           start=c == 0, stop=c == 1)
                        mm.then_inc(s["up"], 1)
                    for j in range(3):
                        for c in range(2):
                            mm = pe.matmul(psT[:, j // 2, (j % 2) * 256:(j % 2) * 256 + C],
                                           hT2[:, c, j * P:(j + 1) * P], wrf[:, c, :], start=c == 0, stop=c == 1)
                    mm.then_inc(s["gatemm"], 1)
                    pe.wait_ge(s["relu"], g * HCH + HCH)
                    for j in range(3):
                        for m in range(HCH):
                            mm = pe.matmul(psK[:, j // 2, (j % 2) * 256:(j % 2) * 256 + C],
                                           kf[:, m, j * P:(j + 1) * P], wvf[:, m, :],
                                           start=m == 0, stop=m == HCH - 1)
                    mm.then_inc(s["down"], 1)
                    pe.wait_ge(s["gate"], g + 1)

                embed(0)
                keys(0)
                values_and_receptance()
                embed(1)
                pe.wait_ge(s["patches_in"], 2)
                with pe.Fori(0, NG - 2) as g:
                    keys(g + 1)
                    project(g)
                    values_and_receptance()
                    pe.wait_ge(s["x1"], g + 1)
                    embed(g + 2)
                    pe.wait_ge(s["patches_in"], g + 3)
                    channel_mix(g)
                keys(NG - 1)
                project(NG - 2)
                values_and_receptance()
                pe.wait_ge(s["x1"], NG - 1)
                channel_mix(NG - 2)
                project(NG - 1)
                channel_mix(NG - 1, last=True)

            def tiles(ps):
                return ps.rearrange("p k (j c) -> p (k j) c", c=256)[:, 0:3, 0:C]

            @block.scalar
            def _(act):
                def load(dst, src):
                    act.dma_start(dst, src).then_inc(s["weights"], 16)
                load(wkf[:, :, :], a["Wk_f"])
                load(wrf[:, :, :], a["Wr_f"])
                load(wvf[:, :, :], a["Wv_f"])
                act.wait_ge(s["weights"], 16 * NW)
                act.wait_ge(s["consts"], 1)

                def embedded(g):
                    act.wait_ge(s["embedded"], g + 1)
                    if not (isinstance(g, int) and g == 0):
                        act.wait_ge(s["patches_out"], g)
                    act.activation(em[:, :], psT[:, 0, 0:C], ACT.Copy).then_inc(s["patches_in"], 1)

                def keep(g):
                    act.wait_ge(s["norm1"], g * 3 + 3)
                    if not (isinstance(g, int) and g == 0):
                        act.wait_ge(s["hc_free"], g)
                    act.activation(x0k[:, :, :], x0[:, :, :], ACT.Copy).then_inc(s["kept"], 1)
                    act.activation(hck[:, :, :], hc[:, :, :], ACT.Copy).then_inc(s["kept"], 1)

                def text(g):
                    act.wait_ge(s["inputs"], g * 32 + 32)
                    if not (isinstance(g, int) and g == 0):
                        act.wait_ge(s["kept"], g * 2)
                    act.activation(hc[:, 1:3, :], tb[:, :, :], ACT.Copy).then_inc(s["text_taken"], 1)

                def front(g):
                    act.wait_ge(s["turned1"], g + 1)
                    for c in range(2):
                        for j0, j1, t0, t1 in ((0, P, 0, TP), (P, GT, TP, T)):
                            act.activation(hT[:, c, :].rearrange("p (b t) -> p b t", t=T)[:, :, t0:t1],
                                           psT[0:HC, c, j0:j1].rearrange("p (b t) -> p b t", t=t1 - t0),
                                           ACT.Identity, bias=lnv[:, 1, c:c + 1], scale=lnv[:, 0, c:c + 1]
                                           ).then_inc(s["hT"], 1)
                    for w, (ps, dst, got) in enumerate(((psK, KK, "k_in"), (psV, VV, "v_in"))):
                        act.wait_ge(s["kvr"], g * 3 + w + 1)
                        if w and not (isinstance(g, int) and g == 0):
                            act.wait_ge(s["y"], g * 2)
                        r = rows(ps)[:, 0:ROWS, 0:T]
                        act.activation(dst[:, 0:ROWS, 1:TS], r, ACT.Identity).then_inc(s[got], 1)
                        act.activation(dst[:, ROWS:2 * ROWS, 1:TS], rows(ps)[:, 0:ROWS, T - 1::-1],
                                       ACT.Identity).then_inc(s[got], 1)
                    act.wait_ge(s["kvr"], g * 3 + 3)
                    act.activation(SR[:, :, :], rows(psR)[:, 0:ROWS, 0:T], ACT.Tanh, scale=0.5
                                   ).then_inc(s["r_in"], 1)

                def decays(g):
                    act.wait_ge(s["d2"], g + 1)
                    act.activation(flat(E2[:, :, :]), flat(E2[:, :, :]), ACT.Exp).then_inc(s["e2"], 1)
                    act.wait_ge(s["e1"], g * 2 + 1)
                    act.activation(flat(E1[:, :, :]), flat(E1[:, :, :]), ACT.Exp).then_inc(s["e1"], 1)

                def shares(g):
                    act.wait_ge(s["mm"], g + 1)
                    act.activation(EX[:, :, :, :].rearrange("p k r t -> p (k r t)"),
                                   EX[:, :, :, :].rearrange("p k r t -> p (k r t)"), ACT.Exp
                                   ).then_inc(s["ex"], 1)

                def turned(g):
                    act.wait_ge(s["turned2"], g + 1)
                    for c in range(2):
                        act.activation(hT2[:, c, :], psT[0:HC, c, 0:GT], ACT.Identity, bias=lnv[:, 3, c:c + 1],
                                       scale=lnv[:, 2, c:c + 1]).then_inc(s["hT2"], 1)

                def relu_squared(g, ms):
                    for m in ms:
                        act.wait_ge(s["up"], g * HCH + m + 1)
                        act.activation(kf[:, m, :], PS[:, 2 + m, 0:GT], ACT.Relu).then_inc(s["relu0"], 1)
                        act.wait_ge(s["relu0"], g * HCH + m + 1)
                        act.activation(kf[:, m, :], kf[:, m, :], ACT.Square).then_inc(s["relu"], 1)

                def gates(g):
                    act.wait_ge(s["gatemm"], g + 1)
                    act.activation(gate[:, :, :], tiles(psT), ACT.Tanh, scale=0.5).then_inc(s["gate"], 1)

                def turn(g, last=False):
                    front(g + 1)
                    if not last:
                        embedded(g + 2)
                    turned(g)
                    keep(g + 1)
                    if not last:
                        text(g + 2)
                    decays(g + 1)
                    relu_squared(g, (0, 1, 2))
                    shares(g + 1)
                    relu_squared(g, (3, 4, 5))
                    gates(g)

                embedded(0)
                text(0)
                front(0)
                embedded(1)
                keep(0)
                text(1)
                decays(0)
                shares(0)
                with act.Fori(0, NG - 2) as g:
                    turn(g)
                turn(NG - 2, last=True)
                turned(NG - 1)
                relu_squared(NG - 1, range(HCH))
                gates(NG - 1)

            @block.vector
            def _(v):
                st = straight.on(v)
                st.did(v.memset(Wf[:, :, :], 0.0))
                st.did(v.memset(Uf[:, :, :], 0.0))
                v.wait_ge(s["weights"], 16 * NW)
                st.settle()
                for k, (r0, r1) in enumerate(((0, GB), (GB, ROWS))):
                    for d in range(2):
                        st.did(v.tensor_scalar(Wf[:, d * ROWS + r0:d * ROWS + r1, :],
                                               Wf[:, d * ROWS + r0:d * ROWS + r1, :], dec[:, 0, k:k + 1], 1.0 / T,
                                               ALU.add, ALU.mult))
                    st.did(v.tensor_scalar(Uf[:, r0:r1, :], Uf[:, r0:r1, :], dec[:, 1, k:k + 1], 1.0 / T,
                                           ALU.add, ALU.mult))
                st.did(v.tensor_tensor(pos[:, :], pos[:, :], cb[:, :], ALU.add))
                st.settle()
                v.wait_ge(s["consts"], 1)
                v.memset(Wf[:, :, 0:1], 3 * NEG).then_inc(s["setup"], 1)
                v.wait_ge(s["setup"], 1)
                loop = Steps(v, s["loop_dve"], FRONT_DVE)
                back = Steps(v, s["back_dve"], BACK_DVE)

                norms = Steps(v, s["norm_dve"], NORM_DVE)

                def first_norm(g):
                    norms.turn(g)
                    v.wait_ge(s["text_taken"], g + 1)
                    v.wait_ge(s["patches_in"], g + 1)
                    v.tensor_tensor(hc[:, 0, :], em[:, :], pos[:, :], ALU.add).then_inc(s["patches_out"], 1)
                    v.wait_ge(s["patches_out"], g + 1)
                    seen(v, passed)
                    norm(v, norms, hc, x0, s["var"], s["rstd"], g * 2 + 1)
                    norms.settle()

                def second_norm(g):
                    norm(v, norms, x0, hn, s["var"], s["rstd"], g * 2 + 2, s["norm1"])
                    norms.end()

                def front(g, following=True, last=None):
                    loop.turn(g)
                    v.wait_ge(s["k_in"], g * 2 + 2)
                    v.tensor_tensor_scan(M[:, 1:1 + 2 * ROWS * TS], flat(Wf[:, :, :]), flat(KK[:, :, :]), NEG,
                                         ALU.add, ALU.max).then_inc(s["m"], 1)
                    v.wait_ge(s["m"], g + 1)
                    loop.did(v.tensor_tensor(flat(E1[:, :, :]), M[:, 0:2 * ROWS * TS], flat(Wf[:, :, :]), ALU.add))
                    loop.settle()
                    v.tensor_tensor(flat(E1[:, :, :]), flat(E1[:, :, :]), M[:, 1:1 + 2 * ROWS * TS],
                                    ALU.subtract).then_inc(s["e1"], 1)
                    if last is not None:
                        mixed(last)
                    mf, mb = before(M)
                    loop.did(v.tensor_tensor(MM[:, :, :], mf, mb, ALU.max))
                    v.wait_ge(s["ku"], g + 1)
                    loop.settle()
                    loop.did(v.tensor_tensor(MM[:, :, :], MM[:, :, :], EX[:, 2, :, :], ALU.max))
                    loop.settle()
                    loop.did(v.tensor_tensor(EX[:, 0, :, :], mf, MM[:, :, :], ALU.subtract))
                    loop.did(v.tensor_tensor(EX[:, 1, :, :], mb, MM[:, :, :], ALU.subtract))
                    v.tensor_tensor(EX[:, 2, :, :], EX[:, 2, :, :], MM[:, :, :], ALU.subtract
                                    ).then_inc(s["mm"], 1)
                    if following:
                        first_norm(g + 1)
                    v.wait_ge(s["e1"], g * 2 + 2)
                    v.wait_ge(s["e2"], g + 1)
                    v.tensor_tensor_scan(Bd[:, 1:1 + 2 * ROWS * TS], flat(E1[:, :, :]), flat(E2[:, :, :]), 0.0,
                                         ALU.mult, ALU.add).then_inc(s["b_scan"], 1)
                    v.wait_ge(s["ev"], g + 1)
                    v.tensor_tensor_scan(A[:, 1:1 + 2 * ROWS * TS], flat(E1[:, :, :]), flat(EV[:, :, :]), 0.0,
                                         ALU.mult, ALU.add).then_inc(s["a_scan"], 1)
                    if following:
                        second_norm(g + 1)
                    af, ab = before(A)
                    v.wait_ge(s["ex"], g + 1)
                    v.wait_ge(s["a_scan"], g + 1)
                    loop.did(v.tensor_tensor(N1[:, 0, :, :], EX[:, 0, :, :], af, ALU.mult))
                    loop.did(v.tensor_tensor(N1[:, 1, :, :], EX[:, 1, :, :], ab, ALU.mult))
                    loop.did(v.tensor_tensor(N1[:, 2, :, :], EX[:, 2, :, :], VV[:, 0:ROWS, 1:TS], ALU.mult))
                    loop.settle()
                    loop.did(v.tensor_tensor(N1[:, 0, :, :], N1[:, 0, :, :], N1[:, 1, :, :], ALU.add))
                    v.wait_ge(s["dpart"], g * 2 + 2)
                    loop.did(v.tensor_tensor(D1[:, 0, :, :], D1[:, 0, :, :], D1[:, 1, :, :], ALU.add))
                    loop.settle()
                    loop.did(v.tensor_tensor(N1[:, 0, :, :], N1[:, 0, :, :], N1[:, 2, :, :], ALU.add))
                    loop.did(v.tensor_tensor(D1[:, 0, :, :], D1[:, 0, :, :], EX[:, 2, :, :], ALU.add))
                    loop.settle()
                    if last is not None:
                        finish(last)
                    loop.did(v.reciprocal(D1[:, 1, :, :], D1[:, 0, :, :]))
                    v.wait_ge(s["r_in"], g + 1)
                    loop.did(v.scalar_tensor_tensor(N1[:, 1, :, :], SR[:, :, :], 1.0, N1[:, 0, :, :], ALU.add,
                                                    ALU.mult))
                    loop.settle()
                    for Y, t0, t1 in ((YP, 0, TP), (YX, TP, T)):
                        v.scalar_tensor_tensor(Y[:, :, :], N1[:, 1, :, t0:t1], 0.5, D1[:, 1, :, t0:t1], ALU.mult,
                                               ALU.mult).then_inc(s["y"], 1)
                    loop.end()

                def mixed(g):
                    back.turn(g)
                    v.wait_ge(s["attn"], g + 1)
                    v.wait_ge(s["kept"], g * 2 + 2)
                    v.tensor_tensor(x1[:, :, :], tiles(psT), x0k[:, :, :], ALU.add).then_inc(s["x1"], 1)
                    v.wait_ge(s["x1"], g + 1)
                    seen(v, passed)
                    norm(v, back, x1, hn2, s["var2"], s["rstd2"], g + 1, s["norm2"])
                    v.tensor_tensor(xh[:, :, :], x1[:, :, :], hck[:, :, :], ALU.add).then_inc(s["hc_free"], 1)

                def finish(g):
                    v.wait_ge(s["down"], g + 1)
                    v.wait_ge(s["gate"], g + 1)
                    v.wait_ge(s["hc_free"], g + 1)
                    back.did(v.scalar_tensor_tensor(ff[:, :, :], gate[:, :, :], 1.0, tiles(psK), ALU.add, ALU.mult))
                    back.settle()
                    v.scalar_tensor_tensor(H[:, bass.ds(g * 3, 3), :], ff[:, :, :], 0.5, xh[:, :, :], ALU.mult,
                                           ALU.add).then_inc(s["done"], 1)
                    back.end()

                v.sem_inc(s["done"], 1)
                first_norm(0)
                second_norm(0)
                front(0)
                with v.Fori(0, NG - 2) as g:
                    front(g + 1, last=g)
                    v.wait_ge(s["done"], g + 2)
                front(NG - 1, following=False, last=NG - 2)
                v.wait_ge(s["done"], NG)
                mixed(NG - 1)
                finish(NG - 1)

def _layouts(np_, i):
    t = {}
    x = i["x"].reshape(NG, GB, 3, 4, 16, 4, 16)
    x = x.transpose(0, 2, 4, 6, 1, 3, 5).reshape(NG, KC, P, P)
    t["patches"] = x.transpose(0, 2, 1, 3)
    t["text"] = i["txt"].reshape(NG, 2, P, C).transpose(0, 2, 1, 3)
    t["conv_w"] = i["L0_tok_conv_w"].reshape(C, KC, P).transpose(2, 1, 0)
    t["conv_b"] = i["L0_tok_conv_b"].reshape(1, C)
    t["pos"] = i["L0_tok_pos_table"].reshape(32, 32, C)[::8, ::8].reshape(TP, C)
    t["ln"] = np_.stack([i["L0_attn_" + n].reshape(2, HC).T for n in ("ln1_w", "ln1_b", "ln2_w", "ln2_b")], 1)

    def fold(w):
        return w.T.reshape(2, HC, w.shape[0]).transpose(1, 0, 2)

    t["w_kvr"] = np_.stack([fold(i["L0_attn_" + n]) for n in ("Wk_a", "Wv_a", "Wr_a")], 2)
    t["Wo"] = i["L0_attn_Wo_a"].T
    t["Wk_f"] = fold(i["L0_attn_Wk_f"])
    t["Wr_f"] = fold(i["L0_attn_Wr_f"])
    t["Wv_f"] = i["L0_attn_Wv_f"].T.reshape(HCH, P, C).transpose(1, 0, 2)
    t["w_fc"] = fold(i["L0_ffn_w_fc"])
    t["w_proj"] = i["L0_ffn_w_proj"].T.reshape(HCH, P, C).transpose(1, 0, 2)
    t["w_in"] = fold(i["L1_attn_w_in"])
    wo = i["L1_attn_w_out"].T.reshape(3, 2, 2, DH, C).transpose(2, 1, 0, 3, 4)
    t["w_out"] = wo.reshape(2, HC, C).transpose(1, 0, 2)
    t["alpha_e"] = i["L0_ffn_alpha_e"].reshape(1, 3)
    t["alpha_r"] = i["L0_ffn_alpha_r"].reshape(1, 3)
    t["b_fc"] = i["L0_ffn_b_fc"].reshape(HCH, P).T
    t["b_proj"] = i["L0_ffn_b_proj"].reshape(1, C)
    widths = np_.array([r * e for e in EMBEDS for r in RATIOS])
    t["hmask"] = (np_.arange(HID).reshape(HCH, P).T[:, :, None] < widths).astype(np_.float32)
    t["cut"] = (np_.arange(P)[:, None] < EMBEDS[1] - HC).astype(np_.float32)
    t["iota8"] = np_.arange(NE, dtype=np_.float32).reshape(1, NE)
    t["tri"] = np_.triu(np_.ones((P, P), np_.float32), 1)
    t["blocks"] = np_.arange(NBLK, dtype=np_.float32).reshape(1, NBLK)
    t["router"] = fold(i["L1_ffn_router_w"])
    t["w1"] = i["L1_ffn_w1"].transpose(0, 2, 1).reshape(NE * 2, HC, ID).transpose(1, 0, 2)
    t["w2"] = i["L1_ffn_w2"].transpose(0, 2, 1).reshape(NE * 4, P, C).transpose(1, 0, 2)
    df = np_.stack([i["L0_attn_decay"], i["L0_attn_first"]])
    t["decfirst"] = np_.stack([df[:, 0:P], np_.concatenate([df[:, P:C], df[:, P:C]], 1)], 2).transpose(1, 0, 2)
    return {n: np_.ascontiguousarray(v) for n, v in t.items()}


def kernel(**inputs):
    import numpy as _np
    import concourse.bacc as _bacc
    from concourse import mybir as _mybir
    from concourse.bass_utils import run_bass_kernel_spmd as _run

    nc = _bacc.Bacc("TRN2", target_bir_lowering=False, num_devices=1)
    laid = _layouts(_np, {n: _np.asarray(v) for n, v in inputs.items()})
    a = {n: nc.dram_tensor("in_" + n, v.shape, _mybir.dt.from_np(v.dtype), kind="ExternalInput").ap()
         for n, v in laid.items()}
    out = nc.dram_tensor("out_dram", (P, NT, C), F32, kind="ExternalOutput").ap()
    rows = [nc.dram_tensor(n, (NBLK * P, C), F32, kind="Internal").ap() for n in ("x_rows", "y_rows")]
    program(nc, a, out, *rows)
    r = _run(nc, [{"in_" + n: v for n, v in laid.items()}], core_ids=[0])
    o = r.results[0]["out_dram"].reshape(P, NG, 3, C).transpose(1, 2, 0, 3)
    got = _np.empty((B, T, C), _np.float32)
    got[:, 0:TP] = o[:, 0].reshape(B, TP, C)
    got[:, TP:T] = o[:, 1:3].reshape(B, TX, C)
    return got
```

```python
from contextlib import ExitStack

import numpy as np

import concourse.bass as bass
from concourse import mybir

F32 = mybir.dt.float32
BF16 = mybir.dt.bfloat16
U32 = mybir.dt.uint32
I32 = mybir.dt.int32
ALU = mybir.AluOpType
ACT = mybir.ActivationFunctionType
AX = mybir.AxisListType
RMAX = bass.bass_isa.ReduceOp.max
RADD = bass.bass_isa.ReduceOp.add

P = 128
B, T, C = 64, 48, 192
TP, TX = 16, 32
HC = C // 2
NG, GB = 8, 8
GT = GB * T
NT = 3 * NG
KC = 768 // P
HID = 768
HCH = HID // P
ROWS = GB + GB // 2
TS = T + 1
EPS = 1e-5
NEG = -1e38
NH, DH = 12, 16
MAGIC = 12582912.0
EMBEDS, RATIOS = (96, 144, 192), (2, 3, 4)
NE, ID = 8, 512
NQ = 4
QT = NT // NQ
ROOM = B * T + P
NOWHERE = float(1 << 20)
NBLK = 2 * B * T // P + NE - 1
QMAX = 127.0
NP = B // 2
PP = 112
NS = NP // 2
SETW = 2 * NH * T


class Straight:

    def __init__(self, sem):
        self.sem, self.n = sem, 0

    def on(self, eng):
        self.eng = eng
        return self

    def did(self, ins):
        self.n += 1
        ins.then_inc(self.sem, 1)

    def settle(self):
        self.eng.wait_ge(self.sem, self.n)


class Steps:

    def __init__(self, eng, sem, per=0):
        self.eng, self.sem, self.per, self.base, self.n = eng, sem, per, 0, 0

    def turn(self, i):
        assert self.n in (0, self.per)
        self.base, self.n = i * self.per, 0

    def did(self, ins):
        self.n += 1
        ins.then_inc(self.sem, 1)

    def settle(self):
        self.eng.wait_ge(self.sem, self.base + self.n)

    def end(self):
        assert self.n == self.per, (self.n, self.per)


def bcast(ap, n, at):
    v = ap.unsqueeze(at)
    shape = list(v.shape)
    shape[at] = n
    return v.broadcast_to(shape)


def program(nc, a, out, X_rows, Y_rows):
    ctx = ExitStack()
    with ctx:
        def sb(name, shape, dt=F32, scope=ctx):
            return scope.enter_context(nc.sbuf_tensor(name, shape, dt))

        def sem(name):
            return ctx.enter_context(nc.semaphore(name))

        class EarlySems:

            def __enter__(self):
                self.scope, self.all = ExitStack(), []
                return self

            def __call__(self, name):
                self.all.append(self.scope.enter_context(nc.semaphore(name)))
                return self.all[-1]

            def __exit__(self, *_):
                with nc.Block() as block:
                    @block.gpsimd
                    def _(gp):
                        for x in self.all:
                            gp.sem_clear(x)
                self.scope.close()

        PS = ctx.enter_context(nc.psum_tensor("PS", [P, 8, 512], F32))
        straight = Straight(sem("straight"))
        passed = sem("passed")
        H = sb("H", [P, NT, C])
        ident = sb("ident", [P, P])
        identb = sb("identb", [P, P], BF16)
        neghalf = sb("neghalf", [P, 16])
        stat = sb("stat", [P, 3, 6])
        mv = sb("mv", [P, 3, 2])
        varp = sb("varp", [P, 3])
        rstd = sb("rstd", [P, 3])

        def norm(v, steps, src, dst, var_ready, rstd_ready, count, ready=None, meanwhile=None):
            for j in range(3):
                steps.did(v.bn_stats(stat[:, j, :], src[:, j, :]))
            steps.settle()
            seen(v, passed)
            for j in range(3):
                steps.did(v.bn_aggr(mv[:, j, :], stat[:, j, :]))
            steps.settle()
            v.tensor_scalar(varp[:, :], mv[:, :, 1], EPS, None, ALU.add).then_inc(var_ready, 1)
            if meanwhile is not None:
                meanwhile()
            v.wait_ge(rstd_ready, count)
            for j in range(3):
                ins = v.tensor_scalar(dst[:, j, :], src[:, j, :], mv[:, j, 0:1], rstd[:, j:j + 1],
                                      ALU.subtract, ALU.mult)
                if ready is None:
                    steps.did(ins)
                else:
                    ins.then_inc(ready, 1)

        def rsqrt(g, var_ready, rstd_ready, count):
            g.wait_ge(var_ready, count)
            g.tensor_tensor(out=rstd[:, :], in0=varp[:, :], in1=neghalf[:, 0:3],
                            op=ALU.pow).then_inc(rstd_ready, 1)

        with EarlySems() as early:
            embed_and_mix(nc, straight, passed, a, early, sb, PS, H, ident, identb, neghalf, norm, rsqrt)
        att = ExitStack()
        with att:
            SC = sb("SC", [P, 24], F32, att)
            MX = sb("MX", [P, 16], F32, att)
            wout = sb("wout", [HC, 2, C], BF16, att)
            Vi = sb("Vi", [P, NP, C], BF16, att)
            stage = ExitStack()
            with stage:
                Qp = sb("Qp", [P, 3, B * T], BF16, stage)
                Kp = sb("Kp", [P, 3, B * T], BF16, stage)
                real = ExitStack()
                with real:
                    Q = sb("Qf", [HC, 2, B * T], F32, real)
                    K = sb("Kf", [HC, 2, B * T], F32, real)
                    V = sb("Vf", [P, NP, C], F32, real)
                    ffn_and_project(nc, straight, passed, a, sem, sb, PS, H, ident, norm, rsqrt, Q, K, V, MX, SC, Qp, Kp)
                    quantise_qkv(nc, straight, a, sem, sb, PS, SC, Q, K, V, Qp, Kp, Vi, wout, MX)
                Qs = sb("Qs", [P, 2, 3, GT], BF16, stage)
                Ks = sb("Ks", [P, 2, 3, GT], BF16, stage)
                E = sb("E", [P, NS, SETW], F32, stage)
                RS = sb("RS", [P, NS, 2 * NH], F32, stage)
                score_maximum(nc, straight, sem, sb, PS, SC, Qp, Kp, Qs, Ks)
                softmax_rows(nc, straight, passed, sem, sb, PS, SC, Qp, Kp, Qs, Ks, E, RS)
                CTX = sb("CTX", [P, NP, C], F32, stage)
                context(nc, straight, passed, sem, sb, PS, SC, identb, E, RS, Vi, CTX)
                Y = E[:, 0:4, :].rearrange("p a n -> p (a n)").rearrange("p (j c) -> p j c", c=C)
                R = E[:, 4:8, :].rearrange("p a n -> p (a n)").rearrange("p (j c) -> p j c", c=C)
                project_out(nc, straight, passed, sem, sb, PS, SC, H, identb, norm, rsqrt, CTX, wout, Y, R)
                batch_norm(nc, straight, sem, sb, PS, SC, H, ident, neghalf, Y, R)
        moe = ExitStack()
        with moe:
            GK = sb("GK", [P, 2, NT], F32, moe)
            blocks = {"expert": sb("block_expert", [P, NBLK], I32, moe),
                      "row": sb("block_row", [P, NBLK], I32, moe),
                      "void": sb("block_void", [P, NBLK], F32, moe)}
            PR = sb("PR", [P, NT, NE], F32, moe)
            ONE = sb("ONE", [P, 2, NT, NE], F32, moe)
            imp = sb("imp", [P, 2, NE], F32, moe)
            W1 = sb("W1", [HC, NE * 2, ID], F32, moe)
            W2 = sb("W2", [P, NE * 4, C], F32, moe)
            route(nc, straight, passed, a, sem, sb, PS, H, ident, norm, rsqrt, W1, W2, PR, ONE, imp, blocks, X_rows)
            experts(nc, straight, passed, sem, sb, PS, ident, W1, W2, PR, ONE, imp, GK, blocks, X_rows, Y_rows)
            combine(nc, sem, sb, H, GK, Y_rows, out)


def ffn_and_project(nc, straight, passed, a, sem, sb_, PS, H, ident, norm, rsqrt, Q, K, V, MX, SC, Qp, Kp):
    scope = ExitStack()
    with scope:
        def sb(name, shape, dt=F32):
            return sb_(name, shape, dt, scope)

        s = {n: sem("p2_" + n) for n in (
            "weights", "w0_ready", "w1_ready", "win_ready", "var", "rstd", "norm", "turned_f", "turned_g", "xf", "xg", "up", "gelu",
            "down", "h3", "qk", "qk_in", "v", "v_in", "f_dve", "g_dve", "m_dve", "wmaxes", "wmax_all",
            "zeros")}
        w0 = sb("w0", [HC, 2, HID])
        w1 = sb("w1", [P, HCH, C])
        win = sb("win", [HC, 2, 3 * C])
        alpha = sb("alpha", [P, 2, 3])
        aij = sb("aij", [P, 3, 3])
        hmask = sb("hmask", [P, HCH, 9])
        g0 = sb("g0", [P, 3, HID])
        gc = sb("gc", [P, 3, HCH])
        gp_ = sb("gp_", [P, HCH, 9])
        cut = sb("cut", [P, 1])
        bfc = sb("bfc", [P, HCH])
        bpr = sb("bpr", [P, C])
        hf = sb("hf", [P, 3, C])
        hg = sb("hg", [P, 3, C])
        xf = sb("xf", [HC, 2, GT])
        xg = sb("xg", [HC, 2, GB, 64])
        gl = sb("gl", [P, HCH, GT])
        x2 = sb("x2", [P, 3, C])
        x2b = sb("x2b", [P, 3, C])
        x3 = sb("x3", [P, 3, C])
        UP_BANK = (4, 5, 6, 7, 2, 3)
        F_DVE, G_DVE, M_DVE = 8, 6, 5
        wmax = sb("wmax", [P, 4])

        psF, psG = PS[:, 0:2, :], PS[:, 2:4, :]

        def tiles(ps):
            return ps.rearrange("p k (j c) -> p (k j) c", c=256)[:, 0:3, 0:C]

        def values(ps):
            return ps[0:PP].rearrange("p k (j c) -> p (k j) c", c=256)[:, :, 0:C]

        with nc.Block() as block:
            @block.sync
            def _(sp):
                def load(dst, src):
                    sp.dma_start(dst, src).then_inc(s["weights"], 16)
                load(w0[:, :, :], a["w_fc"])
                load(w1[:, :, :], a["w_proj"])
                load(win[:, :, :], a["w_in"])
                load(alpha[:, 0, :], a["alpha_e"].to_broadcast([P, 3]))
                load(alpha[:, 1, :], a["alpha_r"].to_broadcast([P, 3]))
                load(hmask[:, :, :], a["hmask"])
                load(bfc[:, :], a["b_fc"])
                load(bpr[:, :], a["b_proj"].to_broadcast([P, C]))
                load(cut[:, :], a["cut"])

            NW = 9

            @block.gpsimd
            def _(gp):
                rsqrt(gp, s["var"], s["rstd"], 1)
                for x in (Qp, Kp):
                    gp.memset(x[:, :, :].rearrange("p c n -> p (c n)").bitcast(F32), 0.0).then_inc(s["zeros"], 1)
                gp.wait_ge(s["wmaxes"], 1)
                gp.partition_all_reduce(wmax[:, 1:2], wmax[:, 0:1], P, RMAX).then_inc(s["wmax_all"], 1)
                with gp.Fori(1, 2 * NG) as n:
                    rsqrt(gp, s["var"], s["rstd"], n + 1)

            @block.vector
            def _(v):
                st = straight.on(v)
                st.did(v.memset(wmax[:, :], 0.0))
                st.did(v.memset(MX[:, :], 0.0))
                st.did(v.memset(xg[:, :, :, :], 0.0))
                ffn = Steps(v, s["f_dve"], F_DVE)
                proj = Steps(v, s["g_dve"], G_DVE)
                maxima = Steps(v, s["m_dve"], M_DVE)

                def biased():
                    ffn.did(v.tensor_tensor(x2b[:, :, :], x2[:, :, :], bcast(bpr[:, :], 3, 1), ALU.add))

                def norm_ffn(g, first=False):
                    ffn.turn(g)
                    if not first:
                        v.wait_ge(s["turned_f"], g)
                    ffn.did(v.tensor_scalar(x2[:, :, :], H[:, bass.ds(g * 3, 3), :], 1.0, None, ALU.mult))
                    ffn.settle()
                    norm(v, ffn, x2, hf, s["var"], s["rstd"], g * 2 + 1, s["norm"], None if first else biased)
                    if not first:
                        ffn.end()

                norm_ffn(0, first=True)
                v.wait_ge(s["weights"], 16 * NW)
                st.settle()
                v.tensor_reduce(wmax[0:HC, 0:1], win[:, :, :].rearrange("p c n -> p (c n)"), AX.X, ALU.max,
                                apply_absolute_value=True).then_inc(s["wmaxes"], 1)
                for i in range(3):
                    st.did(v.tensor_scalar(aij[:, i, :], alpha[:, 1, :], alpha[:, 0, i:i + 1], None, ALU.mult))
                st.did(v.memset(g0[:, :, :], 0.0))
                st.settle()
                for j, r in enumerate(RATIOS):
                    for i, e in enumerate(EMBEDS):
                        st.did(v.tensor_scalar(g0[:, i, 0:r * e], g0[:, i, 0:r * e], aij[:, i, j:j + 1], None,
                                               ALU.add))
                    st.settle()
                st.did(v.tensor_tensor(gp_[:, :, :], hmask[:, :, :],
                                       bcast(aij[:, :, :].rearrange("p i j -> p (i j)"), HCH, 1), ALU.mult))
                st.settle()
                for i in range(3):
                    st.did(v.tensor_reduce(gc[:, i, :], gp_[:, :, 3 * i:3 * i + 3], AX.X, ALU.add))
                st.settle()
                st.did(v.tensor_tensor(g0[:, 0, :], g0[:, 0, :], g0[:, 1, :], ALU.add))
                st.did(v.tensor_tensor(gc[:, 1, :], gc[:, 1, :], gc[:, 2, :], ALU.add))
                st.settle()
                st.did(v.tensor_tensor(g0[:, 0, :], g0[:, 0, :], g0[:, 2, :], ALU.add))
                st.did(v.scalar_tensor_tensor(g0[:, 1, :], g0[:, 1, :], cut[:, 0:1], g0[:, 2, :], ALU.mult,
                                              ALU.add))
                st.did(v.tensor_tensor(gc[:, 0, :], gc[:, 0, :], gc[:, 1, :], ALU.add))
                st.settle()
                for c in range(2):
                    v.tensor_tensor(w0[:, c, :], w0[:, c, :], g0[0:HC, c, :], ALU.mult).then_inc(s["w0_ready"], 1)
                v.tensor_tensor(bfc[:, :], bfc[:, :], gc[:, 0, :], ALU.mult).then_inc(s["w0_ready"], 1)
                for i, (e0, e1) in enumerate(((0, 96), (96, 144), (144, 192))):
                    for m in range(HCH):
                        v.tensor_scalar(w1[:, m, e0:e1], w1[:, m, e0:e1], gc[:, i, m:m + 1], None,
                                        ALU.mult).then_inc(s["w1_ready"], 1)
                st.did(v.tensor_reduce(alpha[:, 0, :], aij[:, :, :], AX.X, ALU.add))
                st.settle()
                st.did(v.tensor_scalar(alpha[:, 1, 1:2], alpha[:, 0, 1:2], alpha[:, 0, 2:3], None, ALU.add))
                st.settle()
                st.did(v.tensor_scalar(alpha[:, 1, 0:1], alpha[:, 0, 0:1], alpha[:, 1, 1:2], None, ALU.add))
                st.settle()
                for e0, e1, k in ((0, 96, alpha[:, 1, 0:1]), (96, 144, alpha[:, 1, 1:2]),
                                  (144, 192, alpha[:, 0, 2:3])):
                    st.did(v.tensor_scalar(bpr[:, e0:e1], bpr[:, e0:e1], k, None, ALU.mult))
                v.wait_ge(s["wmax_all"], 1)
                st.did(v.tensor_scalar(wmax[:, 2:3], wmax[:, 1:2], 1e-8, 1.0 / QMAX, ALU.max, ALU.mult))
                st.settle()
                st.did(v.reciprocal(wmax[:, 3:4], wmax[:, 2:3]))
                st.settle()
                st.did(v.tensor_copy(SC[:, S_WIN:S_WIN + 1], wmax[:, 2:3]))
                st.did(v.tensor_scalar(win[:, :, :], win[:, :, :], wmax[0:HC, 3:4], MAGIC, ALU.mult, ALU.add))
                st.settle()
                v.tensor_scalar(win[:, :, :], win[:, :, :], -MAGIC, None, ALU.add).then_inc(s["win_ready"], 1)

                def norm_project(g, first=False):
                    proj.turn(g)
                    v.wait_ge(s["down"], g + 1)
                    ffn.settle()
                    v.tensor_tensor(x3[:, :, :], x2b[:, :, :], tiles(psF), ALU.add).then_inc(s["h3"], 1)
                    v.tensor_tensor(H[:, bass.ds(g * 3, 3), :], x2b[:, :, :], tiles(psF), ALU.add
                                    ).then_inc(s["h3"], 1)
                    v.wait_ge(s["h3"], g * 2 + 2)
                    if not first:
                        v.wait_ge(s["turned_g"], g)
                    seen(v, passed)
                    norm(v, proj, x3, hg, s["var"], s["rstd"], g * 2 + 2, s["norm"])
                    proj.end()

                def largest(g, behind):
                    maxima.turn(g)
                    for k in range(2):
                        v.wait_ge(s["qk_in"], g * 4 + 2 * k + 2)
                        maxima.did(v.tensor_reduce(MX[0:HC, 4 + k:5 + k], PS[0:HC, 4 + 2 * k:6 + 2 * k, 0:GT],
                                                   AX.XY, ALU.max, apply_absolute_value=True))
                    v.wait_ge(s["v_in"], g + 1)
                    maxima.did(v.tensor_reduce(MX[0:PP, 6:7], values(psG), AX.XY, ALU.max,
                                               apply_absolute_value=True))
                    v.wait_ge(s["norm"], (g + behind) * 6 + 6)
                    maxima.did(v.tensor_reduce(MX[:, 7:8], hg[:, :, :].rearrange("p j c -> p (j c)"), AX.X,
                                               ALU.max, apply_absolute_value=True))
                    maxima.settle()
                    maxima.did(v.tensor_tensor(MX[:, 0:4], MX[:, 0:4], MX[:, 4:8], ALU.max))
                    maxima.settle()
                    maxima.end()

                biased()
                norm_project(0, first=True)
                st.did(v.memset(MX[:, 14:15], 0.0))
                v.wait_ge(s["norm"], 6)
                st.did(v.tensor_reduce(MX[:, 3:4], hg[:, :, :].rearrange("p j c -> p (j c)"), AX.X, ALU.max,
                                       apply_absolute_value=True))
                norm_ffn(1)
                with v.Fori(0, NG - 2) as g:
                    norm_project(g + 1)
                    norm_ffn(g + 2)
                    largest(g, 1)
                norm_project(NG - 1)
                largest(NG - 2, 1)
                largest(NG - 1, 0)

            @block.tensor
            def _(pe):
                def turn(src, dst, turned):
                    for c in range(2):
                        for j in range(3):
                            mm = pe.transpose(dst[0:HC, c, j * P:(j + 1) * P], src[:, j, c * HC:(c + 1) * HC],
                                              ident[:, :])
                    mm.then_inc(turned, 1)

                def dense(g, first=False):
                    pe.wait_ge(s["norm"], g * 6 + 3)
                    turn(hf, psF, s["turned_f"])
                    pe.wait_ge(s["xf"], g * 2 + 1)
                    if first:
                        pe.wait_ge(s["w0_ready"], 3)
                    for m in range(HCH):
                        if m % 2 == 0 and not first:
                            pe.wait_ge(s["m_dve"], (g - 2) * M_DVE + m // 2 + 1)
                        for c in range(2):
                            if m == 0 and c == 1:
                                pe.wait_ge(s["xf"], g * 2 + 2)
                            mm = pe.matmul(PS[:, UP_BANK[m], 0:GT], w0[:, c, m * P:(m + 1) * P], xf[:, c, :],
                                           start=c == 0, stop=c == 1)
                        mm.then_inc(s["up"], 1)
                    pe.wait_ge(s["gelu"], g * HCH + HCH)
                    if first:
                        pe.wait_ge(s["w1_ready"], 3 * HCH)
                    for j in range(3):
                        for m in range(HCH):
                            mm = pe.matmul(psF[:, j // 2, (j % 2) * 256:(j % 2) * 256 + C],
                                           gl[:, m, j * P:(j + 1) * P], w1[:, m, :],
                                           start=m == 0, stop=m == HCH - 1)
                    mm.then_inc(s["down"], 1)

                def project(g):
                    pe.wait_ge(s["norm"], g * 6 + 6)
                    turn(hg, psG, s["turned_g"])
                    pe.wait_ge(s["xg"], g * 4 + 2)
                    for m in range(4):
                        for c in range(2):
                            if m == 0 and c == 1:
                                pe.wait_ge(s["xg"], g * 4 + 4)
                            mm = pe.matmul(PS[0:HC, 4 + m, 0:GT].rearrange("p (b t) -> p b t", t=T),
                                           win[:, c, m * HC:(m + 1) * HC], xg[:, c, :, 0:T],
                                           start=c == 0, stop=c == 1)
                        mm.then_inc(s["qk"], 1)
                    for q in range(4):
                        for c in range(2):
                            mm = pe.matmul(psG[0:PP, q // 2, (q % 2) * 256:(q % 2) * 256 + C],
                                           xg[:, c, 2 * q:2 * q + 2, :].rearrange("p b t -> p (b t)")[:, 0:PP],
                                           win[:, c, 2 * C:3 * C], start=c == 0, stop=c == 1)
                    mm.then_inc(s["v"], 1)

                dense(0, first=True)
                pe.wait_ge(s["h3"], 2)
                dense(1, first=True)
                pe.wait_ge(s["win_ready"], 1)
                project(0)
                with pe.Fori(1, NG - 1) as g:
                    pe.wait_ge(s["h3"], g * 2 + 2)
                    dense(g + 1)
                    project(g)
                pe.wait_ge(s["m_dve"], (NG - 1) * M_DVE)
                project(NG - 1)

            @block.scalar
            def _(act):
                def dense(g):
                    act.wait_ge(s["turned_f"], g + 1)
                    for c in range(2):
                        act.activation(xf[:, c, :], psF[0:HC, c, 0:GT], ACT.Copy).then_inc(s["xf"], 1)
                    for m in range(HCH):
                        act.wait_ge(s["up"], g * HCH + m + 1)
                        act.activation(gl[:, m, :], PS[:, UP_BANK[m], 0:GT], ACT.Gelu_apprx_tanh, bias=bfc[:, m:m + 1]
                                       ).then_inc(s["gelu"], 1)

                def project(g):
                    act.wait_ge(s["turned_g"], g + 1)
                    for c in range(2):
                        for j0, j1, t0, t1 in ((0, P, 0, TP), (P, GT, TP, T)):
                            act.activation(xg[:, c, :, t0:t1],
                                           psG[0:HC, c, j0:j1].rearrange("p (b t) -> p b t", t=t1 - t0),
                                           ACT.Copy).then_inc(s["xg"], 1)
                    for m in range(4):
                        act.wait_ge(s["qk"], g * 4 + m + 1)
                        dst = (Q, K)[m // 2]
                        act.activation(dst[:, m % 2, bass.ds(g * GT, GT)], PS[0:HC, 4 + m, 0:GT], ACT.Copy,
                                       scale=wmax[0:HC, 2:3]).then_inc(s["qk_in"], 1)
                    act.wait_ge(s["v"], g + 1)
                    act.activation(V[0:PP, bass.ds(g * 4, 4), :], values(psG), ACT.Copy, scale=wmax[0:PP, 2:3]
                                   ).then_inc(s["v_in"], 1)

                dense(0)
                act.wait_ge(s["win_ready"], 1)
                with act.Fori(0, NG - 1) as g:
                    dense(g + 1)
                    project(g)
                project(NG - 1)


def seen(eng, held):
    eng.sem_inc(held, 1)


(S_WIN, S_WOUT, S_Q, S_K, S_V, S_X, S_SCORE, S_ATT, S_CTX, S_Y, S_RN) = range(11)


class Scales:

    def __init__(self, v, steps, table):
        self.v, self.st, self.t = v, steps, table

    def col(self, k):
        return self.t[:, k:k + 1]

    def op(self, dst, src, s1, s2, op0, op1=None):
        if op1 is None:
            ins = self.v.tensor_scalar(self.col(dst), self.col(src), s1, None, op0)
        else:
            ins = self.v.tensor_scalar(self.col(dst), self.col(src), s1, s2, op0, op1)
        self.st.did(ins)
        self.st.settle()

    def inverse(self, dst, src):
        self.st.did(self.v.reciprocal(self.col(dst), self.col(src)))
        self.st.settle()


def quantise_qkv(nc, straight, a, sem, sb_, PS, SC, Q, K, V, Qp, Kp, Vi, wout, MX):
    scope = ExitStack()
    with scope:
        def sb(name, shape, dt=F32):
            return sb_(name, shape, dt, scope)

        s = {n: sem("p3_" + n) for n in ("wout", "maxes", "all", "q", "k", "v", "padded",
                                         "scales", "steps")}
        Qi = sb("Qi", [HC, 2, B * T], BF16)
        Ki = sb("Ki", [HC, 2, B * T], BF16)
        wf = sb("wf", [HC, 2, C])
        F_Q, F_K, F_V, F_W, M_ = 11, 12, 13, 14, 16
        with nc.Block() as block:
            @block.sync
            def _(sp):
                sp.dma_start(wf[:, :, :], a["w_out"]).then_inc(s["wout"], 16)
                n = 0
                for src, dst, ready in ((Qi, Qp, "q"), (Ki, Kp, "k")):
                    sp.wait_ge(s[ready], 1)
                    for h in range(NH):
                        c, r = divmod(h, 6)
                        sp.dma_start(dst[32 * (h % 4):32 * (h % 4) + DH, h // 4, :],
                                     src[DH * r:DH * r + DH, c, :]).then_inc(s["padded"], 16)
                        n += 16
                sp.wait_ge(s["padded"], n)

            @block.gpsimd
            def _(gp):
                gp.wait_ge(s["maxes"], 1)
                gp.partition_all_reduce(MX[:, 8:13], MX[:, 0:5], P, RMAX).then_inc(s["all"], 1)

            @block.scalar
            def _(act):
                act.wait_ge(s["scales"], 1)
                for n, X, f in ((HC, K, F_K), (PP, V, F_V)):
                    act.activation(X[0:n, :, :], X[0:n, :, :], ACT.Identity, scale=SC[0:n, f:f + 1],
                                   bias=SC[0:n, 17:18]).then_inc(s["steps"], 1)

            @block.vector
            def _(v):
                st = straight.on(v)
                sc = Scales(v, st, SC)
                st.did(v.memset(MX[:, 4:5], 0.0))
                st.did(v.memset(PS[:, :, :], 0.0))
                v.wait_ge(s["wout"], 16)
                st.settle()
                v.tensor_reduce(MX[0:HC, 4:5], wf[:, :, :].rearrange("p c n -> p (c n)"), AX.X, ALU.max,
                                apply_absolute_value=True).then_inc(s["maxes"], 1)
                v.wait_ge(s["all"], 1)
                st.did(v.tensor_scalar(MX[:, 8:11], MX[:, 8:11], SC[:, S_WIN:S_WIN + 1], None, ALU.mult))
                st.settle()
                st.did(v.tensor_scalar(SC[:, S_Q:S_Q + 4], MX[:, 8:12], 1e-8, 1.0 / QMAX, ALU.max, ALU.mult))
                st.did(v.tensor_scalar(SC[:, S_WOUT:S_WOUT + 1], MX[:, 12:13], 1e-8, 1.0 / QMAX, ALU.max,
                                       ALU.mult))
                st.settle()
                st.did(v.reciprocal(SC[:, F_Q:F_Q + 3], SC[:, S_Q:S_Q + 3]))
                st.did(v.reciprocal(SC[:, F_W:F_W + 1], SC[:, S_WOUT:S_WOUT + 1]))
                st.settle()
                v.memset(SC[:, 17:18], MAGIC).then_inc(s["scales"], 1)
                st.did(v.tensor_scalar(wf[:, :, :], wf[:, :, :], SC[0:HC, F_W:F_W + 1], MAGIC, ALU.mult,
                                       ALU.add))
                st.settle()
                st.did(v.tensor_scalar(wout[:, :, :], wf[:, :, :], -MAGIC, None, ALU.add))
                for n, (X, Xi, f, ready) in enumerate(((Q, Qi, F_Q, "q"), (K, Ki, F_K, "k"), (V, Vi, F_V, "v"))):
                    r = X.shape[0] if X is not V else PP
                    if n:
                        v.wait_ge(s["steps"], n)
                    else:
                        st.did(v.tensor_scalar(X[0:r, :, :], X[0:r, :, :], SC[0:r, f:f + 1], MAGIC, ALU.mult,
                                               ALU.add))
                        st.settle()
                    v.tensor_scalar(Xi[0:r, :, :], X[0:r, :, :], -MAGIC, None, ALU.add).then_inc(s[ready], 1)
                st.settle()


def score_matmuls(pe, PS, Qs, Ks, buf, half):
    for slot in range(2):
        for e in range(2):
            tok = slice(((half * 2 + slot) * 2 + e) * T, ((half * 2 + slot) * 2 + e + 1) * T)
            for c in range(3):
                for j in range(4):
                    col = slot * 3 * T + c * T
                    mm = pe.matmul(PS[64 * e:64 * e + T, 4 * half + j, col:col + T],
                                   Qs[32 * j:32 * j + DH, buf, c, tok], Ks[32 * j:32 * j + DH, buf, c, tok],
                                   start=True, stop=True, skip_group_check=True)
    return mm


def turns(eng, turn):
    turn(0)
    with eng.Fori(1, NG // 2 - 1) as i:
        turn(i)
    turn(NG // 2 - 1)


def is_first(i):
    return isinstance(i, int) and i == 0


def is_last(i):
    return isinstance(i, int) and i == NG // 2 - 1


def all_scores(pe, PS, Qs, Ks, s):
    def turn(i):
        for k in range(4):
            if k % 2 == 0:
                pe.wait_ge(s["staged%d" % (k // 2)], i * 32 + 32)
            if not is_first(i) or k >= 2:
                pe.wait_ge(s["free"], i * 4 + k - 1)
            score_matmuls(pe, PS, Qs, Ks, k // 2, k % 2).then_inc(s["scores"], 1)
    turns(pe, turn)


def stage_all(sp, Qp, Kp, Qs, Ks, s):
    for buf in range(2):
        stage_qk(sp, Qp, Kp, Qs, Ks, buf, buf, s)
    with sp.Fori(1, NG // 2) as i:
        for buf in range(2):
            sp.wait_ge(s["scores"], (i * 2 + buf - 1) * 2)
            stage_qk(sp, Qp, Kp, Qs, Ks, i * 2 + buf, buf, s)


def stage_qk(sp, Qp, Kp, Qs, Ks, g, buf, s):
    for src, dst in ((Qp, Qs), (Kp, Ks)):
        sp.dma_start(dst[:, buf, :, :], src[:, :, bass.ds(g * GT, GT)]).then_inc(s["staged%d" % buf], 16)


def score_maximum(nc, straight, sem, sb_, PS, SC, Qp, Kp, Qs, Ks):
    scope = ExitStack()
    with scope:
        s = {n: sem("p4_" + n) for n in ("staged0", "staged1", "scores", "free", "loop_dve", "maxes",
                                         "all")}
        m = sb_("m4", [P, 4], F32, scope)
        with nc.Block() as block:
            @block.sync
            def _(sp):
                stage_all(sp, Qp, Kp, Qs, Ks, s)

            @block.tensor
            def _(pe):
                all_scores(pe, PS, Qs, Ks, s)

            @block.gpsimd
            def _(gp):
                gp.wait_ge(s["maxes"], 1)
                gp.partition_all_reduce(m[:, 3:4], m[:, 0:1], P, RMAX).then_inc(s["all"], 1)

            @block.vector
            def _(v):
                st = straight.on(v)
                st.did(v.memset(m[:, :], 0.0))
                st.settle()
                loop = Steps(v, s["loop_dve"], 4)
                with v.Fori(0, NG // 2) as i:
                    loop.turn(i)
                    for k in range(4):
                        v.wait_ge(s["scores"], i * 4 + k + 1)
                        h = k % 2
                        v.tensor_reduce(m[0:PP, 1 + h:2 + h], PS[0:PP, 4 * h:4 * h + 4, 0:6 * T], AX.XY, ALU.max,
                                        apply_absolute_value=True).then_inc(s["free"], 1)
                        v.wait_ge(s["free"], i * 4 + k + 1)
                        loop.did(v.tensor_tensor(m[:, 0:1], m[:, 0:1], m[:, 1 + h:2 + h], ALU.max))
                        loop.settle()
                    loop.end()
                v.memset(m[:, 1:2], 0.0).then_inc(s["maxes"], 1)
                v.wait_ge(s["all"], 1)
                sc = Scales(v, st, SC)
                sc.op(15, S_Q, SC[:, S_K:S_K + 1], 0.25, ALU.mult, ALU.mult)
                st.did(v.tensor_scalar(SC[:, S_SCORE:S_SCORE + 1], m[:, 3:4], SC[:, 15:16], 1e-8, ALU.mult,
                                       ALU.max))
                st.settle()
                sc.op(S_SCORE, S_SCORE, 1.0 / QMAX, None, ALU.mult)
                sc.inverse(16, S_SCORE)
                sc.op(16, 16, SC[:, 15:16], None, ALU.mult)
                st.did(v.memset(SC[:, 17:18], MAGIC))
                st.settle()


def softmax_rows(nc, straight, passed, sem, sb_, PS, SC, Qp, Kp, Qs, Ks, E, RS):
    scope = ExitStack()
    with scope:
        def sb(name, shape, dt=F32):
            return sb_(name, shape, dt, scope)

        s = {n: sem("p5_" + n) for n in ("staged0", "staged1", "scores", "free", "rowmax", "less",
                                         "exp", "sums", "maxes", "all")}
        W = sb("W5", [P, 4, SETW])
        rm = sb("rm5", [P, 4, 2 * NH])
        m = sb("m5", [P, 2])
        with nc.Block() as block:
            @block.sync
            def _(sp):
                stage_all(sp, Qp, Kp, Qs, Ks, s)

            @block.tensor
            def _(pe):
                all_scores(pe, PS, Qs, Ks, s)

            @block.scalar
            def _(act):
                def steps(n, k):
                    act.wait_ge(s["scores"], n + 1)
                    if not isinstance(n, int) or n >= 4:
                        act.wait_ge(s["exp"], n - 3)
                    act.activation(W[0:PP, k, :].rearrange("p (k n) -> p k n", k=4),
                                   PS[0:PP, 4 * (k % 2):4 * (k % 2) + 4, 0:6 * T], ACT.Identity,
                                   scale=SC[0:PP, 16:17], bias=SC[0:PP, 17:18]).then_inc(s["free"], 1)

                def turn(i):
                    for k in range(4):
                        if not is_last(i) or k < 2:
                            steps(i * 4 + k + 2, (k + 2) % 4)
                        act.wait_ge(s["less"], i * 4 + k + 1)
                        act.activation(E[0:PP, bass.ds(i * 4 + k, 1), :], W[0:PP, k:k + 1, :], ACT.Exp,
                                       scale=SC[0:PP, S_SCORE:S_SCORE + 1]).then_inc(s["exp"], 1)
                steps(0, 0)
                steps(1, 1)
                turns(act, turn)

            @block.gpsimd
            def _(gp):
                with gp.Fori(0, NG // 2) as i:
                    for k in range(4):
                        gp.wait_ge(s["rowmax"], i * 4 + k + 1)
                        w = W[0:PP, k, :].rearrange("p (r n) -> p r n", n=T)
                        gp.tensor_tensor(out=w, in0=w, in1=bcast(rm[0:PP, k, :], T, 2), op=ALU.subtract
                                         ).then_inc(s["less"], 1)
                gp.wait_ge(s["maxes"], 1)
                gp.partition_all_reduce(m[:, 1:2], m[:, 0:1], P, RMAX).then_inc(s["all"], 1)

            @block.vector
            def _(v):
                def row_maxima(n, k):
                    v.wait_ge(s["free"], n + 1)
                    v.tensor_reduce(rm[0:PP, k, :], W[0:PP, k, :].rearrange("p (r n) -> p r n", n=T), AX.X,
                                    ALU.max).then_inc(s["rowmax"], 1)

                def turn(i):
                    for k in range(4):
                        if not is_last(i) or k < 2:
                            row_maxima(i * 4 + k + 2, (k + 2) % 4)
                        v.wait_ge(s["exp"], i * 4 + k + 1)
                        seen(v, passed)
                        v.tensor_reduce(RS[0:PP, bass.ds(i * 4 + k, 1), :].rearrange("p a r -> p (a r)"),
                                        E[0:PP, bass.ds(i * 4 + k, 1), :].rearrange(
                                            "p a (r n) -> p (a r) n", n=T), AX.X, ALU.add).then_inc(s["sums"], 1)
                row_maxima(0, 0)
                row_maxima(1, 1)
                turns(v, turn)
                st = straight.on(v)
                sc = Scales(v, st, SC)
                st.did(v.memset(m[:, :], 0.0))
                v.wait_ge(s["sums"], 2 * NG)
                r = RS[0:PP, :, :].rearrange("p a r -> p (a r)")
                st.did(v.reciprocal(r, r))
                st.settle()
                v.tensor_reduce(m[0:PP, 0:1], r, AX.X, ALU.max).then_inc(s["maxes"], 1)
                v.wait_ge(s["all"], 1)
                st.did(v.tensor_scalar(SC[:, S_ATT:S_ATT + 1], m[:, 1:2], 1e-8, 1.0 / QMAX, ALU.max, ALU.mult))
                st.settle()
                sc.inverse(18, S_ATT)
                st.did(v.tensor_scalar(r, r, SC[0:PP, 18:19], None, ALU.mult))
                st.settle()


def context(nc, straight, passed, sem, sb_, PS, SC, identb, E, RS, Vi, CTX):
    scope = ExitStack()
    with scope:
        def sb(name, shape, dt=F32):
            return sb_(name, shape, dt, scope)

        s = {n: sem("p6_" + n) for n in ("staged0", "staged1", "prod", "ai", "turned", "at", "ctx",
                                         "ctx_in", "max", "maxes", "all", "loop_dve")}
        W = sb("W6", [P, 2, SETW])
        Ai = sb("Ai", [P, 2, SETW], BF16)
        AT = sb("AT", [P, 4, 6 * PP], BF16)
        Vs = sb("Vs", [P, 2, 2, 4, C], BF16)
        m = sb("m6", [P, 4])
        with nc.Block() as block:
            @block.sync
            def _(sp):
                def stage(g, par):
                    for r0, r1, q0, w in ((0, PP, 0, 0), (0, T, 64, 1), (64, PP, 0, 1)):
                        sp.dma_start(Vs[r0:r1, par, w, :, :], Vi[q0:q0 + r1 - r0, bass.ds(g * 4, 4), :]
                                     ).then_inc(s["staged%d" % par], 16)
                stage(0, 0)
                stage(1, 1)
                with sp.Fori(1, NG // 2) as i:
                    for par in range(2):
                        sp.wait_ge(s["ctx"], i * 2 + par - 1)
                        stage(i * 2 + par, par)

            @block.gpsimd
            def _(gp):
                gp.wait_ge(s["maxes"], 1)
                gp.partition_all_reduce(m[:, 2:3], m[:, 0:1], P, RMAX).then_inc(s["all"], 1)

            @block.tensor
            def _(pe):
                def turn_round(g):
                    for q in range(4):
                        h, slot = divmod(q, 2)
                        pe.wait_ge(s["ai"], g * 2 + h + 1)
                        seen(pe, passed)
                        pt = PS[:, q, :].bitcast(BF16)
                        for j in range(4):
                            for c in range(3):
                                o, k = 64 * (j % 2), (j // 2) * 3 + c
                                col = ((j * 2 + slot) * 3 + c) * T
                                mm = pe.transpose(pt[o:o + T, k * PP:(k + 1) * PP], Ai[0:PP, h, col:col + T],
                                                  identb[0:PP, 0:PP])
                        mm.then_inc(s["turned"], 1)

                def products(g, par, n):
                    pe.wait_ge(s["staged%d" % par], n * 48 + 48)
                    for q in range(4):
                        pe.wait_ge(s["at"], g * 4 + q + 1)
                        seen(pe, passed)
                        for j in range(4):
                            for c in range(3):
                                for e in range(2):
                                    o, k, odd = 64 * (j % 2), (j // 2) * 3 + c, j % 2
                                    hd = 4 * c + j
                                    mm = pe.matmul(
                                        PS[64 * e:64 * e + T, 4 + odd, q * HC + k * DH:q * HC + (k + 1) * DH],
                                        AT[o:o + T, q, k * PP + 64 * e:k * PP + 64 * e + T],
                                        Vs[o:o + T, par, int(e != odd), q, hd * DH:(hd + 1) * DH],
                                        start=True, stop=True, skip_group_check=True)
                    mm.then_inc(s["ctx"], 1)

                def turn(i):
                    for par in range(2):
                        g = i * 2 + par
                        products(g, par, i)
                        if not is_last(i) or par == 0:
                            turn_round(g + 1)
                            pe.wait_ge(s["ctx_in"], g * 2 + 2)
                            pe.wait_ge(s["max"], g + 1)
                turn_round(0)
                turns(pe, turn)

            @block.scalar
            def _(act):
                def turned(g):
                    for q in range(4):
                        act.wait_ge(s["turned"], g * 4 + q + 1)
                        act.activation(AT[0:PP, q, :], PS[0:PP, q, :].bitcast(BF16)[:, 0:6 * PP], ACT.Identity
                                       ).then_inc(s["at"], 1)

                def contexts(g):
                    act.wait_ge(s["ctx"], g + 1)
                    for odd in range(2):
                        act.activation(CTX[0:PP, bass.ds(g * 4, 4), odd * HC:(odd + 1) * HC],
                                       PS[0:PP, 4 + odd, 0:4 * HC].rearrange("p (q n) -> p q n", q=4),
                                       ACT.Identity).then_inc(s["ctx_in"], 1)
                turned(0)
                with act.Fori(0, NG - 1) as g:
                    contexts(g)
                    turned(g + 1)
                contexts(NG - 1)

            @block.vector
            def _(v):
                st = straight.on(v)
                st.did(v.memset(m[:, :], 0.0))
                st.settle()
                loop = Steps(v, s["loop_dve"], 1)

                def quantise(g):
                    for h in range(2):
                        e = E[0:PP, bass.ds(g * 2 + h, 1), :].rearrange("p a (r n) -> p (a r) n", n=T)
                        r = RS[0:PP, bass.ds(g * 2 + h, 1), :].rearrange("p a r -> p (a r)")
                        v.tensor_tensor(W[0:PP, h, :].rearrange("p (r n) -> p r n", n=T), e, bcast(r, T, 2),
                                        ALU.mult).then_inc(s["prod"], 1)
                        v.wait_ge(s["prod"], g * 2 + h + 1)
                        if not isinstance(g, int):
                            v.wait_ge(s["turned"], g * 4 + 2 * h - 2)
                        v.tensor_scalar(Ai[0:PP, h, :], W[0:PP, h, :], MAGIC, -MAGIC, ALU.add, ALU.add
                                        ).then_inc(s["ai"], 1)

                def largest(g):
                    loop.turn(g)
                    v.wait_ge(s["ctx_in"], g * 2 + 2)
                    v.tensor_reduce(m[0:PP, 1:2], PS[0:PP, 4:6, 0:4 * HC], AX.XY, ALU.max,
                                    apply_absolute_value=True).then_inc(s["max"], 1)
                    v.wait_ge(s["max"], g + 1)
                    loop.did(v.tensor_tensor(m[:, 0:1], m[:, 0:1], m[:, 1:2], ALU.max))
                    loop.settle()
                    loop.end()
                quantise(0)
                with v.Fori(0, NG - 1) as g:
                    quantise(g + 1)
                    v.wait_ge(s["ai"], g * 2 + 4)
                    largest(g)
                largest(NG - 1)
                v.memset(m[:, 1:2], 0.0).then_inc(s["maxes"], 1)
                v.wait_ge(s["all"], 1)
                sc = Scales(v, st, SC)
                sc.op(15, S_ATT, SC[:, S_V:S_V + 1], None, ALU.mult)
                st.did(v.tensor_scalar(SC[:, S_CTX:S_CTX + 1], m[:, 2:3], SC[:, 15:16], 1e-8, ALU.mult, ALU.max))
                st.settle()
                sc.op(S_CTX, S_CTX, 1.0 / QMAX, None, ALU.mult)
                sc.inverse(16, S_CTX)
                sc.op(16, 16, SC[:, 15:16], None, ALU.mult)


def project_out(nc, straight, passed, sem, sb_, PS, SC, H, identb, norm, rsqrt, CTX, wout, Y, R):
    scope = ExitStack()
    with scope:
        def sb(name, shape, dt=F32):
            return sb_(name, shape, dt, scope)

        s = {n: sem("p7_" + n) for n in ("loop_dve", "cf", "ci", "turned", "cT", "y", "y_in", "max", "var",
                                         "rstd", "norm", "maxes", "all")}
        cf = sb("cf", [P, 4, C])
        Ci = sb("Ci", [P, 4, C], BF16)
        cT = sb("cT", [HC, 2, GT], BF16)
        hx = sb("hx", [P, 3, C])
        hn = sb("hn7", [P, 3, C])
        m = sb("m7", [P, 4])
        LOOP = 10
        with nc.Block() as block:
            @block.gpsimd
            def _(gp):
                with gp.Fori(0, NG) as g:
                    rsqrt(gp, s["var"], s["rstd"], g + 1)
                gp.wait_ge(s["maxes"], 1)
                gp.partition_all_reduce(m[:, 2:3], m[:, 0:1], P, RMAX).then_inc(s["all"], 1)

            @block.scalar
            def _(act):
                def steps(g):
                    if not (isinstance(g, int) and g == 0):
                        act.wait_ge(s["ci"], g)
                    act.activation(cf[0:PP, :, :], CTX[0:PP, bass.ds(g * 4, 4), :], ACT.Identity,
                                   scale=SC[0:PP, 16:17], bias=SC[0:PP, 17:18]).then_inc(s["cf"], 1)

                def turn(g, last=False):
                    if not last:
                        steps(g + 1)
                    act.wait_ge(s["turned"], g + 1)
                    pt = PS[0:HC, 0, :].bitcast(BF16)[:, 0:8 * PP].rearrange("p (c q n) -> p c q n", c=2, q=4)
                    for c in range(2):
                        for t0, t1, d0 in ((0, TP, 0), (TP, T, P)):
                            for e in range(2):
                                n = t1 - t0
                                dst = cT[:, c, d0:d0 + GB * n].rearrange("p (q e t) -> p q e t", q=4, e=2)
                                act.activation(dst[:, :, e, :], pt[:, c, :, 64 * e + t0:64 * e + t1], ACT.Identity
                                               ).then_inc(s["cT"], 1)
                    act.wait_ge(s["y"], g + 1)
                    act.activation(Y[:, bass.ds(g * 3, 3), :],
                                   PS[:, 2:4, :].rearrange("p k (j c) -> p (k j) c", c=256)[:, 0:3, 0:C],
                                   ACT.Identity).then_inc(s["y_in"], 1)

                steps(0)
                with act.Fori(0, NG - 1) as g:
                    turn(g)
                turn(NG - 1, last=True)

            @block.tensor
            def _(pe):
                def turn(g):
                    pe.wait_ge(s["ci"], g + 1)
                    pt = PS[0:HC, 0, :].bitcast(BF16)
                    for c in range(2):
                        for q in range(4):
                            k = c * 4 + q
                            mm = pe.transpose(pt[:, k * PP:(k + 1) * PP], Ci[0:PP, q, c * HC:(c + 1) * HC],
                                              identb[0:PP, 0:PP])
                    mm.then_inc(s["turned"], 1)

                def product(g):
                    pe.wait_ge(s["cT"], g * 8 + 8)
                    for j in range(3):
                        for c in range(2):
                            mm = pe.matmul(PS[:, 2 + j // 2, (j % 2) * 256:(j % 2) * 256 + C],
                                           cT[:, c, j * P:(j + 1) * P], wout[:, c, :], start=c == 0, stop=c == 1)
                    mm.then_inc(s["y"], 1)

                turn(0)
                with pe.Fori(0, NG - 1) as g:
                    product(g)
                    turn(g + 1)
                    pe.wait_ge(s["y_in"], g + 1)
                product(NG - 1)

            @block.vector
            def _(v):
                st = straight.on(v)
                sc = Scales(v, st, SC)
                st.did(v.memset(m[:, :], 0.0))
                st.did(v.reciprocal(SC[:, 19:20], SC[:, S_X:S_X + 1]))
                st.settle()
                loop = Steps(v, s["loop_dve"], LOOP)
                def integers(g):
                    v.wait_ge(s["cf"], g + 1)
                    if not (isinstance(g, int) and g == 0):
                        v.wait_ge(s["turned"], g)
                    v.tensor_scalar(Ci[0:PP, :, :], cf[0:PP, :, :], -MAGIC, None, ALU.add).then_inc(s["ci"], 1)

                def turn(g, last=False):
                    loop.turn(g)

                    def meanwhile():
                        if not last:
                            integers(g + 1)
                        v.wait_ge(s["y_in"], g + 1)
                        seen(v, passed)
                        v.tensor_reduce(m[:, 1:2], Y[:, bass.ds(g * 3, 3), :], AX.XY, ALU.max,
                                        apply_absolute_value=True).then_inc(s["max"], 1)
                        v.wait_ge(s["max"], g + 1)
                        loop.did(v.tensor_tensor(m[:, 0:1], m[:, 0:1], m[:, 1:2], ALU.max))

                    loop.did(v.tensor_scalar(hx[:, :, :], H[:, bass.ds(g * 3, 3), :], 1.0, None, ALU.mult))
                    loop.settle()
                    norm(v, loop, hx, hn, s["var"], s["rstd"], g + 1, s["norm"], meanwhile)
                    v.wait_ge(s["norm"], g * 3 + 3)
                    loop.did(v.tensor_scalar(hn[:, :, :], hn[:, :, :], SC[:, 19:20], MAGIC, ALU.mult, ALU.add))
                    loop.settle()
                    loop.did(v.tensor_scalar(R[:, bass.ds(g * 3, 3), :], hn[:, :, :], -MAGIC,
                                             SC[:, S_X:S_X + 1], ALU.add, ALU.mult))
                    loop.settle()
                    loop.end()

                integers(0)
                with v.Fori(0, NG - 1) as g:
                    turn(g)
                turn(NG - 1, last=True)
                v.memset(m[:, 1:2], 0.0).then_inc(s["maxes"], 1)
                v.wait_ge(s["all"], 1)
                sc.op(15, S_CTX, SC[:, S_WOUT:S_WOUT + 1], None, ALU.mult)
                st.did(v.tensor_scalar(SC[:, S_Y:S_Y + 1], m[:, 2:3], SC[:, 15:16], 1e-8, ALU.mult, ALU.max))
                st.settle()
                sc.op(S_Y, S_Y, 1.0 / QMAX, None, ALU.mult)
                sc.inverse(16, S_Y)
                sc.op(16, 16, SC[:, 15:16], None, ALU.mult)


def batch_norm(nc, straight, sem, sb_, PS, SC, H, ident, neghalf, Y, R):
    scope = ExitStack()
    with scope:
        def sb(name, shape, dt=F32):
            return sb_(name, shape, dt, scope)

        s = {n: sem("p8_" + n) for n in ("ones", "r", "mean", "centred", "square", "var", "vard", "column",
                                         "columns_in", "pow", "diag", "spread", "maxes", "all")}
        ones = sb("ones8", [P, P])
        SQ = sb("SQ", [P, NT, C])
        vr = sb("vr", [P, C])
        one = sb("one8", [HC, P])
        vc = sb("vc", [HC, 2])
        diag = sb("diag", [HC, 2, HC])
        m = sb("m8", [P, 2])
        with nc.Block() as block:
            @block.gpsimd
            def _(gp):
                gp.memset(ones[:, :], 1.0 / (B * T)).then_inc(s["ones"], 1)
                gp.memset(one[:, :], 1.0).then_inc(s["ones"], 1)
                gp.wait_ge(s["columns_in"], 1)
                gp.tensor_tensor(out=vc[:, :], in0=vc[:, :], in1=neghalf[0:HC, 0:2], op=ALU.pow
                                 ).then_inc(s["pow"], 1)
                gp.wait_ge(s["maxes"], 1)
                gp.partition_all_reduce(m[:, 1:2], m[:, 0:1], P, RMAX).then_inc(s["all"], 1)

            @block.scalar
            def _(act):
                for k in range(NQ):
                    act.wait_ge(s["centred"], k + 1)
                    act.activation(SQ[:, k * QT:(k + 1) * QT, :], R[:, k * QT:(k + 1) * QT, :], ACT.Square
                                   ).then_inc(s["square"], 1)

            @block.tensor
            def _(pe):
                pe.wait_ge(s["ones"], 2)
                for n, (src, ready, done) in enumerate(((R, "r", "mean"), (SQ, "square", "var"))):
                    for k in range(NT):
                        if k % QT == 0:
                            pe.wait_ge(s[ready], k // QT + 1)
                        mm = pe.matmul(PS[:, n, 0:C], ones[:, :], src[:, k, :], start=k == 0, stop=k == NT - 1)
                    mm.then_inc(s[done], 1)
                pe.wait_ge(s["vard"], 1)
                for c in range(2):
                    mm = pe.matmul(PS[0:HC, 2, c:c + 1], vr[0:1, c * HC:(c + 1) * HC], one[0:1, 0:1],
                                   start=True, stop=True)
                mm.then_inc(s["column"], 1)
                pe.wait_ge(s["diag"], 2)
                for c in range(2):
                    mm = pe.matmul(PS[:, 3, c * HC:(c + 1) * HC], one[:, :], diag[:, c, :], start=True, stop=True)
                mm.then_inc(s["spread"], 1)

            @block.vector
            def _(v):
                st = straight.on(v)
                sc = Scales(v, st, SC)
                quarters = [slice(k * QT, (k + 1) * QT) for k in range(NQ)]
                for q in quarters:
                    st.did(v.tensor_scalar(Y[:, q, :], Y[:, q, :], SC[:, 16:17], MAGIC, ALU.mult, ALU.add))
                    st.settle()
                    st.did(v.tensor_scalar(Y[:, q, :], Y[:, q, :], -MAGIC, SC[:, S_Y:S_Y + 1], ALU.add, ALU.mult))
                    st.settle()
                    v.tensor_tensor(R[:, q, :], R[:, q, :], Y[:, q, :], ALU.add).then_inc(s["r"], 1)
                v.wait_ge(s["mean"], 1)
                v.wait_ge(s["r"], NQ)
                for q in quarters:
                    v.tensor_tensor(R[:, q, :], R[:, q, :], bcast(PS[:, 0, 0:C], QT, 1), ALU.subtract
                                    ).then_inc(s["centred"], 1)
                v.wait_ge(s["var"], 1)
                v.tensor_scalar(vr[:, :], PS[:, 1, 0:C], EPS, None, ALU.add).then_inc(s["vard"], 1)
                v.wait_ge(s["column"], 1)
                v.tensor_copy(vc[:, :], PS[0:HC, 2, 0:2]).then_inc(s["columns_in"], 1)
                v.wait_ge(s["pow"], 1)
                for c in range(2):
                    v.tensor_scalar(diag[:, c, :], ident[0:HC, 0:HC], vc[:, c:c + 1], None, ALU.mult
                                    ).then_inc(s["diag"], 1)
                v.wait_ge(s["spread"], 1)
                v.wait_ge(s["centred"], NQ)
                for q in quarters:
                    st.did(v.tensor_tensor(R[:, q, :], R[:, q, :], bcast(PS[:, 3, 0:C], QT, 1), ALU.mult))
                st.settle()
                v.tensor_reduce(m[:, 0:1], R[:, :, :], AX.XY, ALU.max, apply_absolute_value=True
                                ).then_inc(s["maxes"], 1)
                v.wait_ge(s["all"], 1)
                st.did(v.tensor_scalar(SC[:, S_RN:S_RN + 1], m[:, 1:2], 1e-8, 1.0 / QMAX, ALU.max, ALU.mult))
                st.settle()
                sc.inverse(16, S_RN)
                st.did(v.tensor_scalar(R[:, :, :], R[:, :, :], SC[:, 16:17], MAGIC, ALU.mult, ALU.add))
                st.settle()
                st.did(v.tensor_scalar(R[:, :, :], R[:, :, :], -MAGIC, SC[:, S_RN:S_RN + 1], ALU.add, ALU.mult))
                st.settle()
                st.did(v.tensor_tensor(H[:, :, :], H[:, :, :], R[:, :, :], ALU.add))
                st.settle()


def route(nc, straight, passed, a, sem, sb_, PS, H, ident, norm, rsqrt, W1, W2, PR, ONE, imp, blocks, X_rows):
    scope = ExitStack()
    with scope:
        def sb(name, shape, dt=F32):
            return sb_(name, shape, dt, scope)

        s = {n: sem("p9_" + n) for n in ("weights", "var", "rstd", "norm", "turned", "xs", "kept", "logits",
                                         "shifted", "exp", "norm_dve", "loop_dve", "part", "importance",
                                         "experts", "ids", "chosen", "ranks", "slots", "pads", "sent")}
        rw = sb("rw", [HC, 2, NE])
        iota8 = sb("iota8", [P, NE])
        tri = sb("tri", [P, P])
        ones = sb("ones9", [P, P])
        number = sb("number", [P, NBLK])
        lane = sb("lane", [P, 1])
        home = sb("home", [P, 2, NT])
        hx = sb("hx9", [P, 3, C])
        hn = sb("hn9", [P, 3, C])
        xs = sb("xs9", [HC, 2, GT])
        lg = sb("lg", [P, 3, NE])
        ex = sb("ex9", [P, 3, NE])
        pg = sb("pg", [P, 3, NE])
        t3 = sb("t3", [P, 3, 3])
        top = sb("top", [P, 3, 8])
        idx = sb("idx", [P, 3, 8], U32)
        idf = sb("idf", [P, 3, 2])
        one = sb("one9", [P, 2, 3, NE])
        sel = sb("sel", [P, 3, NE])
        end = sb("end", [P, 4, NE])
        off = sb("off", [P, 3, NE])
        pick = sb("pick", [P, 2, 3, NE])
        slf = sb("slf", [P, 2, 3])
        slots = sb("slots", [P, 2, NT], U32)
        XR = sb("XR", [P, 2, NT, C + 1])
        pad = sb("pad", [P, C + 1])
        padf = sb("padf", [P, NE])
        pads = sb("pads", [P, NE], U32)
        nb = sb("nb", [P, 4, NE])
        own = sb("own", [P, NBLK, NE])
        bt = sb("bt", [P, 4, NBLK])
        NORM, LOOP = 7, 23
        NW = 6
        with nc.Block() as block:
            @block.sync
            def _(sp):
                def load(dst, src):
                    sp.dma_start(dst, src).then_inc(s["weights"], 16)
                load(rw[:, :, :], a["router"])
                load(iota8[:, :], a["iota8"].to_broadcast([P, NE]))
                load(tri[:, :], a["tri"])
                load(number[:, :], a["blocks"].to_broadcast([P, NBLK]))
                load(home[:, :, :], a["home"])
                load(lane[:, :], a["lane"])
                sp.dma_start(W1[:, :, :], a["w1"]).then_inc(s["experts"], 16)
                sp.dma_start(W2[:, :, :], a["w2"]).then_inc(s["experts"], 16)
                sp.wait_ge(s["experts"], 32)

            @block.gpsimd
            def _(gp):
                rsqrt(gp, s["var"], s["rstd"], 1)
                rsqrt(gp, s["var"], s["rstd"], 2)
                gp.wait_ge(s["ids"], 1)
                for g in range(NG):
                    if g == NG - 1:
                        gp.wait_ge(s["part"], 1)
                        gp.partition_all_reduce(imp[:, 1, :], imp[:, 0, :], P, RADD).then_inc(s["importance"], 1)
                    gp.wait_ge(s["kept"], g * 2 + 2)
                    gp.wait_ge(s["slots"], g + 1)
                    for t in range(g * 3, g * 3 + 3):
                        for k in range(2):
                            gp.indirect_dma_start(X_rows, bass.IndirectOffsetOnAxis(slots[:, k, t:t + 1], 0),
                                                  XR[:, k, t, :], None).then_inc(s["sent"], 16)
                        if t == g * 3 and g + 2 < NG:
                            rsqrt(gp, s["var"], s["rstd"], g + 3)
                gp.wait_ge(s["pads"], 1)
                for e in range(NE):
                    gp.indirect_dma_start(X_rows, bass.IndirectOffsetOnAxis(pads[:, e:e + 1], 0), pad[:, :],
                                          None).then_inc(s["sent"], 16)
                gp.wait_ge(s["sent"], 16 * (2 * NT + NE))

            @block.tensor
            def _(pe):
                def turn(g):
                    pe.wait_ge(s["norm"], g * 3 + 3)
                    for c in range(2):
                        for j in range(3):
                            mm = pe.transpose(PS[0:HC, c, j * P:(j + 1) * P], hn[:, j, c * HC:(c + 1) * HC],
                                              ident[:, :])
                    mm.then_inc(s["turned"], 1)

                def logits(g):
                    pe.wait_ge(s["xs"], g * 2 + 2)
                    if not (isinstance(g, int) and g == 0):
                        pe.wait_ge(s["shifted"], g)
                    for j in range(3):
                        for c in range(2):
                            mm = pe.matmul(PS[:, 2, j * NE:(j + 1) * NE], xs[:, c, j * P:(j + 1) * P], rw[:, c, :],
                                           start=c == 0, stop=c == 1)
                    mm.then_inc(s["logits"], 1)

                def ranks(g):
                    pe.wait_ge(s["chosen"], g + 1)
                    for n, w in enumerate((tri, ones)):
                        mm = pe.matmul(PS[:, 3 + n, 0:3 * NE], w[:, :], sel[:, :, :].rearrange("p j e -> p (j e)"),
                                       start=True, stop=True)
                    mm.then_inc(s["ranks"], 1)

                pe.wait_ge(s["weights"], 16 * NW)
                pe.wait_ge(s["ids"], 1)
                turn(0)
                logits(0)
                with pe.Fori(0, NG - 1) as g:
                    turn(g + 1)
                    ranks(g)
                    logits(g + 1)
                ranks(NG - 1)

            @block.scalar
            def _(act):
                def turned(g):
                    act.wait_ge(s["turned"], g + 1)
                    for c in range(2):
                        act.activation(xs[:, c, :], PS[0:HC, c, 0:GT], ACT.Copy).then_inc(s["xs"], 1)

                def keep(g):
                    for k in range(2):
                        act.activation(XR[:, k, bass.ds(g * 3, 3), 0:C], hn[:, :, :], ACT.Copy
                                       ).then_inc(s["kept"], 1)

                def exponentials(g):
                    act.wait_ge(s["shifted"], g + 1)
                    act.activation(ex[:, :, :], lg[:, :, :], ACT.Exp).then_inc(s["exp"], 1)

                turned(0)
                keep(0)
                with act.Fori(0, NG - 1) as g:
                    exponentials(g)
                    turned(g + 1)
                    keep(g + 1)
                exponentials(NG - 1)

            @block.vector
            def _(v):
                st = straight.on(v)
                st.did(v.memset(pad[:, 0:C], 0.0))
                st.did(v.memset(pad[:, C:C + 1], NOWHERE))
                st.did(v.memset(ones[:, :], 1.0))
                v.wait_ge(s["weights"], 16 * NW)
                st.did(v.tensor_scalar(end[:, 0, :], iota8[:, :], float(ROOM), None, ALU.mult))
                st.settle()
                v.tensor_copy(XR[:, :, :, C], home[:, :, :]).then_inc(s["ids"], 1)
                norms = Steps(v, s["norm_dve"], NORM)
                loop = Steps(v, s["loop_dve"], LOOP)

                def rows(g):
                    norms.turn(g)
                    if not (isinstance(g, int) and g == 0):
                        v.wait_ge(s["turned"], g)
                        v.wait_ge(s["kept"], g * 2)
                        seen(v, passed)
                    norms.did(v.tensor_scalar(hx[:, :, :], H[:, bass.ds(g * 3, 3), :], 1.0, None, ALU.mult))
                    norms.settle()
                    norm(v, norms, hx, hn, s["var"], s["rstd"], g + 1, s["norm"])
                    norms.end()

                def choose(g, last=False):
                    loop.turn(g)
                    v.wait_ge(s["logits"], g + 1)
                    z = PS[:, 2, 0:3 * NE].rearrange("p (j e) -> p j e", e=NE)
                    loop.did(v.tensor_reduce(t3[:, 0, :], z, AX.X, ALU.max))
                    loop.settle()
                    v.tensor_tensor(lg[:, :, :], z, bcast(t3[:, 0, :], NE, 2), ALU.subtract
                                    ).then_inc(s["shifted"], 1)
                    v.wait_ge(s["exp"], g + 1)
                    loop.did(v.tensor_reduce(t3[:, 1, :], ex[:, :, :], AX.X, ALU.add))
                    loop.settle()
                    loop.did(v.reciprocal(t3[:, 2, :], t3[:, 1, :]))
                    loop.settle()
                    loop.did(v.tensor_tensor(pg[:, :, :], ex[:, :, :], bcast(t3[:, 2, :], NE, 2), ALU.mult))
                    loop.settle()
                    seen(v, passed)
                    for j in range(3):
                        loop.did(v.max(top[:, j, :], pg[:, j, :]))
                    loop.did(v.tensor_scalar(PR[:, bass.ds(g * 3, 3), :], pg[:, :, :], 1.0, None, ALU.mult))
                    loop.settle()
                    if last:
                        v.tensor_reduce(imp[:, 0, :], PR[:, :, :].rearrange("p t e -> p e t"), AX.X, ALU.add
                                        ).then_inc(s["part"], 1)
                    seen(v, passed)
                    for j in range(3):
                        loop.did(v.max_index(idx[:, j, :], top[:, j, :], pg[:, j, :]))
                    loop.settle()
                    loop.did(v.tensor_copy(idf[:, :, :], idx[:, :, 0:2]))
                    loop.settle()
                    for k in range(2):
                        loop.did(v.tensor_tensor(one[:, k, :, :], bcast(iota8[:, :], 3, 1),
                                                 idf[:, :, k:k + 1].broadcast_to([P, 3, NE]), ALU.is_equal))
                    loop.settle()
                    v.tensor_tensor(sel[:, :, :], one[:, 0, :, :], one[:, 1, :, :], ALU.add
                                    ).then_inc(s["chosen"], 1)
                    loop.did(v.tensor_scalar(ONE[:, :, bass.ds(g * 3, 3), :], one[:, :, :, :], 1.0, None, ALU.mult))
                    v.wait_ge(s["ranks"], g + 1)
                    for j in range(3):
                        loop.did(v.tensor_tensor(end[:, j + 1, :], end[:, j, :], PS[:, 4, j * NE:(j + 1) * NE],
                                                 ALU.add))
                        loop.settle()
                    loop.did(v.tensor_tensor(off[:, :, :], end[:, 0:3, :],
                                             PS[:, 3, 0:3 * NE].rearrange("p (j e) -> p j e", e=NE), ALU.add))
                    loop.settle()
                    loop.did(v.tensor_copy(end[:, 0, :], end[:, 3, :]))
                    for k in range(2):
                        loop.did(v.tensor_tensor(pick[:, k, :, :], one[:, k, :, :], off[:, :, :], ALU.mult))
                    loop.settle()
                    loop.did(v.tensor_reduce(slf[:, :, :], pick[:, :, :, :], AX.X, ALU.add))
                    loop.settle()
                    v.tensor_scalar(slots[:, :, bass.ds(g * 3, 3)], slf[:, :, :], 1.0, None, ALU.mult
                                    ).then_inc(s["slots"], 1)
                    loop.end()

                rows(0)
                with v.Fori(0, NG - 1) as g:
                    rows(g + 1)
                    choose(g)
                choose(NG - 1, last=True)
                st.did(v.scalar_tensor_tensor(padf[:, :], lane[:, 0:1].broadcast_to([P, NE]), 1.0, end[:, 0, :],
                                              ALU.mult, ALU.add))
                st.settle()
                v.tensor_copy(pads[:, :], padf[:, :]).then_inc(s["pads"], 1)
                st.did(v.scalar_tensor_tensor(nb[:, 1, :], iota8[:, :], -float(ROOM), end[:, 0, :], ALU.mult,
                                              ALU.add))
                st.settle()
                st.did(v.tensor_scalar(nb[:, 0, :], nb[:, 1, :], 1.0 / P, (P - 1) / P - 0.5 + 0.5 / P, ALU.mult,
                                       ALU.add))
                st.settle()
                st.did(v.tensor_scalar(nb[:, 1, :], nb[:, 0, :], MAGIC, None, ALU.add))
                st.settle()
                st.did(v.tensor_scalar(nb[:, 0, :], nb[:, 1, :], -MAGIC, None, ALU.add))
                st.settle()
                st.did(v.tensor_tensor_scan(nb[:, 2, :], ones[:, 0:NE], nb[:, 0, :], 0.0, ALU.mult, ALU.add))
                st.settle()
                st.did(v.tensor_tensor(nb[:, 3, :], nb[:, 2, :], nb[:, 0, :], ALU.subtract))
                st.did(v.tensor_tensor(own[:, :, :], bcast(number[:, :], NE, 2), bcast(nb[:, 2, :], NBLK, 1),
                                       ALU.is_ge))
                st.settle()
                st.did(v.tensor_reduce(bt[:, 0, :], own[:, :, :], AX.X, ALU.add))
                st.settle()
                st.did(v.tensor_scalar(bt[:, 3, :], bt[:, 0, :], float(NE), None, ALU.is_equal))
                st.did(v.tensor_scalar(bt[:, 1, :], bt[:, 0, :], float(NE - 1), None, ALU.min))
                st.settle()
                st.did(v.tensor_copy(blocks["expert"][:, :], bt[:, 1, :]))
                st.did(v.tensor_scalar(blocks["void"][:, :], bt[:, 3, :], NOWHERE, None, ALU.mult))
                st.did(v.tensor_tensor(own[:, :, :], bcast(iota8[:, :], NBLK, 1), bcast(bt[:, 1, :], NE, 2),
                                       ALU.is_equal))
                st.settle()
                st.did(v.tensor_tensor(own[:, :, :], own[:, :, :], bcast(nb[:, 3, :], NBLK, 1), ALU.mult))
                st.settle()
                st.did(v.tensor_reduce(bt[:, 2, :], own[:, :, :], AX.X, ALU.add))
                st.did(v.tensor_scalar(bt[:, 3, :], bt[:, 3, :], -float(P), float(P), ALU.mult, ALU.add))
                st.settle()
                st.did(v.tensor_tensor(bt[:, 2, :], number[:, :], bt[:, 2, :], ALU.subtract))
                st.settle()
                st.did(v.tensor_tensor(bt[:, 2, :], bt[:, 2, :], bt[:, 3, :], ALU.mult))
                st.settle()
                st.did(v.scalar_tensor_tensor(bt[:, 2, :], bt[:, 1, :], float(ROOM), bt[:, 2, :], ALU.mult,
                                              ALU.add))
                st.settle()
                st.did(v.tensor_copy(blocks["row"][:, :], bt[:, 2, :]))
                v.wait_ge(s["importance"], 1)


def choice_weights(v, st, imp, PR, ONE, GK, tmp):
    SEL, G, den, PK = tmp
    st.did(v.tensor_scalar(imp[:, 0, :], imp[:, 1, :], -1.0, 1.0 - 0.9, ALU.add, ALU.mult))
    st.did(v.tensor_tensor(SEL[:, :, :], ONE[:, 0, :, :], ONE[:, 1, :, :], ALU.add))
    st.settle()
    st.did(v.tensor_scalar(imp[:, 0, :], imp[:, 0, :], 1.0, 0.01, ALU.add, ALU.add))
    st.settle()
    st.did(v.reciprocal(imp[:, 1, :], imp[:, 0, :]))
    st.settle()
    st.did(v.tensor_tensor(PR[:, :, :], PR[:, :, :], bcast(imp[:, 1, :], NT, 1), ALU.mult))
    st.settle()
    st.did(v.tensor_tensor(PR[:, :, :], PR[:, :, :], SEL[:, :, :], ALU.mult))
    st.settle()
    st.did(v.tensor_reduce(den[:, :], PR[:, :, :], AX.X, ALU.add))
    st.settle()
    st.did(v.reciprocal(den[:, :], den[:, :]))
    st.settle()
    st.did(v.tensor_tensor(G[:, :, :], PR[:, :, :], bcast(den[:, :], NE, 2), ALU.mult))
    st.settle()
    for k in range(2):
        st.did(v.tensor_tensor(PK[:, k, :, :], ONE[:, k, :, :], G[:, :, :], ALU.mult))
    st.settle()
    for k in range(2):
        st.did(v.tensor_reduce(GK[:, k, :], PK[:, k, :, :], AX.X, ALU.add))
    st.settle()


def experts(nc, straight, passed, sem, sb_, PS, ident, W1, W2, PR, ONE, imp, GK, blocks, X_rows, Y_rows):
    scope = ExitStack()
    with scope:
        def sb(name, shape, dt=F32):
            return sb_(name, shape, dt, scope)

        s = {n: sem("p10_" + n) for n in ("x0", "x1", "turned", "xT", "up", "silu", "h_turned", "hT", "down", "y",
                                          "place", "y_out0", "y_out1")}
        xb = sb("xb", [P, 2, C + 1])
        weighing = (sb("SEL", [P, NT, NE]), sb("G", [P, NT, NE]), sb("den", [P, NT]), sb("PK", [P, 2, NT, NE]))
        placef = sb("placef", [P, 2])
        place = sb("place", [P, 2], U32)
        xT = sb("xT10", [HC, 2, 2, P])
        h = sb("h10", [P, 2, ID])
        hT = sb("hT10", [P, 2, ID])
        yb = sb("yb", [P, 2, C])

        def steps(eng, step, first, last):
            for b in range(first):
                step(b, b % 2, b // 2)
            with eng.Fori(first // 2, last // 2) as i:
                for par in range(2):
                    step(i * 2 + par, par, i)
            for b in range(last, NBLK):
                step(b, b % 2, b // 2)

        def static(b):
            return isinstance(b, int)

        with nc.Block() as block:
            @block.sync
            def _(sp):
                def load(b, par, n):
                    if not static(b) or b >= 2:
                        sp.wait_ge(s["turned"], b - 1)
                        sp.wait_ge(s["place"], b - 1)
                    row = sp.value_load(blocks["row"][0:1, bass.ds(b, 1)], min_val=0, max_val=NE * ROOM - P)
                    sp.dma_start(xb[:, par, :], X_rows[bass.ds(row, P), :]).then_inc(s["x%d" % par], 16)
                steps(sp, load, 2, NBLK - 1)

            @block.gpsimd
            def _(gp):
                def store(b, par, n):
                    gp.wait_ge(s["y"], b * 2 + 2)
                    seen(gp, passed)
                    gp.indirect_dma_start(Y_rows, bass.IndirectOffsetOnAxis(place[:, par:par + 1], 0),
                                          yb[:, par, :], None, bounds_check=2 * B * T - 1, oob_is_err=False
                                          ).then_inc(s["y_out%d" % par], 16)
                steps(gp, store, 2, NBLK - 1)
                for par in range(2):
                    gp.wait_ge(s["y_out%d" % par], 16 * ((NBLK + 1 - par) // 2))

            @block.tensor
            def _(pe):
                def turn(b, par, n):
                    pe.wait_ge(s["x%d" % par], n * 16 + 16)
                    for c in range(2):
                        mm = pe.transpose(PS[0:HC, par, c * P:(c + 1) * P], xb[:, par, c * HC:(c + 1) * HC],
                                          ident[:, :])
                    mm.then_inc(s["turned"], 1)

                def up(b, par, e):
                    pe.wait_ge(s["xT"], b + 1)
                    for c in range(2):
                        mm = pe.matmul(PS[:, 2 + par, :], xT[:, par, c, :],
                                       W1[:, bass.ds(e * 2 + c, 1), :].rearrange("p a n -> p (a n)"),
                                       start=c == 0, stop=c == 1)
                    mm.then_inc(s["up"], 1)

                def turn_hidden(b, par):
                    pe.wait_ge(s["silu"], b + 1)
                    for m in range(4):
                        mm = pe.transpose(PS[:, 4 + par, m * P:(m + 1) * P], h[:, par, m * P:(m + 1) * P],
                                          ident[:, :])
                    mm.then_inc(s["h_turned"], 1)

                def down(b, par, e):
                    pe.wait_ge(s["hT"], b + 1)
                    if not static(b) or b >= 2:
                        pe.wait_ge(s["y"], b * 2 - 2)
                    for m in range(4):
                        mm = pe.matmul(PS[:, 6 + par, 0:C], hT[:, par, m * P:(m + 1) * P],
                                       W2[:, bass.ds(e * 4 + m, 1), :].rearrange("p a n -> p (a n)"),
                                       start=m == 0, stop=m == 3)
                    mm.then_inc(s["down"], 1)

                def expert(b):
                    return pe.value_load(blocks["expert"][0:1, bass.ds(b, 1)], min_val=0, max_val=NE - 1)

                def step(b, par, n):
                    following = expert(b + 1) if not static(b) or b + 1 < NBLK else None
                    turn_hidden(b, par)
                    if following is not None:
                        up(b + 1, 1 - par, following)
                    if not static(b) or b + 2 < NBLK:
                        turn(b + 2, par, n + 1)
                    down(b, par, expert(b))

                turn(0, 0, 0)
                turn(1, 1, 0)
                up(0, 0, expert(0))
                steps(pe, step, 2, NBLK - 3)

            @block.scalar
            def _(act):
                def taken(b, par, n):
                    act.wait_ge(s["turned"], b + 1)
                    if not static(b) or b >= 2:
                        act.wait_ge(s["up"], b - 1)
                    act.activation(xT[:, par, :, :], PS[0:HC, par, 0:2 * P].rearrange("p (c n) -> p c n", c=2),
                                   ACT.Copy).then_inc(s["xT"], 1)

                def silu(b, par, n):
                    act.wait_ge(s["up"], b + 1)
                    if not static(b) or b >= 2:
                        act.wait_ge(s["h_turned"], b - 1)
                    act.activation(h[:, par, :], PS[:, 2 + par, :], ACT.Silu).then_inc(s["silu"], 1)

                def step(b, par, n):
                    silu(b - 1, 1 - par, n)
                    taken(b, par, n)

                taken(0, 0, 0)
                taken(1, 1, 0)
                silu(0, 0, 0)
                silu(1, 1, 0)
                taken(2, 0, 1)
                silu(2, 0, 1)
                taken(3, 1, 1)
                with act.Fori(2, (NBLK - 1) // 2) as i:
                    for par in range(2):
                        step(i * 2 + par, par, i)
                step(NBLK - 1, 0, NBLK // 2)
                silu(NBLK - 1, 0, NBLK // 2)

            @block.vector
            def _(v):
                def places(b, par, n):
                    v.wait_ge(s["x%d" % par], n * 16 + 16)
                    if not static(b) or b >= 2:
                        v.wait_ge(s["y"], b * 2 - 2)
                    v.tensor_tensor(placef[:, par:par + 1], xb[:, par, C:C + 1], blocks["void"][:, bass.ds(b, 1)],
                                    ALU.add).then_inc(s["place"], 1)

                def step(b, par, n):
                    v.wait_ge(s["h_turned"], b + 1)
                    if not static(b) or b >= 2:
                        v.wait_ge(s["down"], b - 1)
                    v.tensor_copy(hT[:, par, :], PS[:, 4 + par, :]).then_inc(s["hT"], 1)
                    if not static(b) or b + 1 < NBLK:
                        places(b + 1, 1 - par, n + par)
                    v.wait_ge(s["down"], b + 1)
                    if not static(b) or b >= 2:
                        v.wait_ge(s["y_out%d" % par], n * 16)
                    v.tensor_copy(yb[:, par, :], PS[:, 6 + par, 0:C]).then_inc(s["y"], 1)
                    v.wait_ge(s["place"], b + 1)
                    v.tensor_copy(place[:, par:par + 1], placef[:, par:par + 1]).then_inc(s["y"], 1)
                places(0, 0, 0)
                choice_weights(v, straight.on(v), imp, PR, ONE, GK, weighing)
                steps(v, step, 2, NBLK - 1)


def combine(nc, sem, sb_, H, GK, Y_rows, out):
    scope = ExitStack()
    with scope:
        s = {n: sem("p11_" + n) for n in ["rows%d" % q for q in range(NQ)] + ["added", "stored"]}
        yk = sb_("yk", [P, 2, NT, C], F32, scope)
        with nc.Block() as block:
            @block.sync
            def _(sp):
                for q in range(NQ):
                    for k in range(2):
                        r = slice(q * QT, (q + 1) * QT)
                        sp.dma_start(yk[:, k, r, :], Y_rows[k * B * T:(k + 1) * B * T, :].rearrange(
                            "(p t) c -> p t c", p=P)[:, r, :]).then_inc(s["rows%d" % q], 16)
                for q in range(NQ):
                    sp.wait_ge(s["added"], 2 * q + 2)
                    sp.dma_start(out[:, q * QT:(q + 1) * QT, :], H[:, q * QT:(q + 1) * QT, :]
                                 ).then_inc(s["stored"], 16)
                sp.wait_ge(s["stored"], 16 * NQ)

            @block.vector
            def _(v):
                for q in range(NQ):
                    v.wait_ge(s["rows%d" % q], 32)
                    for k in range(2):
                        for t in range(q * QT, (q + 1) * QT):
                            ins = v.scalar_tensor_tensor(H[:, t, :], yk[:, k, t, :], GK[:, k, t:t + 1], H[:, t, :],
                                                         ALU.mult, ALU.add)
                        ins.then_inc(s["added"], 1)
                        v.wait_ge(s["added"], 2 * q + k + 1)


def embed_and_mix(nc, straight, passed, a, sem, sb_, PS, H, ident, identb, neghalf, norm, rsqrt):
    scope = ExitStack()
    with scope:
        def sb(name, shape, dt=F32):
            return sb_(name, shape, dt, scope)

        px = sb("px", [P, KC, P])
        tb = sb("tb", [P, 2, C])
        cw = sb("cw", [P, KC, C])
        pos = sb("pos", [P, C])
        cb = sb("cb", [P, C])
        lnv = sb("lnv", [HC, 4, 2])
        wkvr = sb("wkvr", [HC, 2, 3, C])
        wo = sb("wo", [P, 2, C])
        wkf = sb("wkf", [HC, 2, HID])
        wrf = sb("wrf", [HC, 2, C])
        wvf = sb("wvf", [P, HCH, C])
        dec = sb("dec", [P, 2, 2])
        Wf = sb("Wf", [P, 2 * ROWS, TS])
        Uf = sb("Uf", [P, ROWS, T])
        em = sb("em", [P, C])
        hc = sb("hc", [P, 3, C])
        x0 = sb("x0", [P, 3, C])
        hck = sb("hck", [P, 3, C])
        x0k = sb("x0k", [P, 3, C])
        hn = sb("hn", [P, 3, C])
        hT = sb("hT", [HC, 2, GT])
        KK = sb("KK", [P, 2 * ROWS, TS])
        VV = sb("VV", [P, 2 * ROWS, TS])
        SR = sb("SR", [P, ROWS, T])
        M = sb("M", [P, 1 + 2 * ROWS * TS])
        A = sb("A", [P, 1 + 2 * ROWS * TS])
        Bd = sb("Bd", [P, 1 + 2 * ROWS * TS])
        E1 = sb("E1", [P, 2 * ROWS, TS])
        E2 = sb("E2", [P, 2 * ROWS, TS])
        EV = sb("EV", [P, 2 * ROWS, TS])
        EX = sb("EX", [P, 3, ROWS, T])
        MM = sb("MM", [P, ROWS, T])
        N1 = sb("N1", [P, 3, ROWS, T])
        D1 = sb("D1", [P, 2, ROWS, T])
        YP = sb("YP", [P, ROWS, TP])
        YX = sb("YX", [P, ROWS, TX])
        kf = sb("kf", [P, HCH, GT])
        hn2 = sb("hn2a", [P, 3, C])
        hT2 = sb("hT2", [HC, 2, GT])
        xh = sb("xh", [P, 3, C])
        x1 = sb("x1", [P, 3, C])
        gate = sb("gate1", [P, 3, C])
        ff = sb("ff1", [P, 3, C])

        psT = PS[:, 0:2, :]
        psK, psV, psR = PS[:, 2:4, :], PS[:, 4:6, :], PS[:, 6:8, :]

        def rows(ps):
            return ps.rearrange("p k (r t) -> p (k r) t", t=64)

        def flat(ap):
            return ap.rearrange("p r t -> p (r t)")

        def before(buf):
            v = buf[:, 1:1 + 2 * ROWS * TS].rearrange("p (r t) -> p r t", t=TS)
            return v[:, 0:ROWS, 0:T], v[:, ROWS:2 * ROWS, T - 1::-1]

        s = {n: sem("p1_" + n) for n in (
            "weights", "consts", "setup", "inputs", "embedded", "text_taken", "var", "rstd",
            "norm1", "turned1", "hT", "kvr", "k_in", "v_in", "r_in", "m", "d2", "e1", "e2", "ev", "ku", "mm",
            "ex", "dpart", "y", "attn", "norm2", "turned2", "hT2", "up", "relu", "gatemm", "gate", "down",
            "pool", "relu0", "done", "loop_dve", "back_dve", "norm_dve", "var2", "rstd2", "hc_free", "b_scan",
            "a_scan", "patches_out", "patches_in", "kept", "x1", "conv_w", "positions")}
        NW = 9
        NORM_DVE, FRONT_DVE, BACK_DVE = 15, 14, 7

        with nc.Block() as block:
            @block.sync
            def _(sp):
                def load(dst, src):
                    sp.dma_start(dst, src).then_inc(s["weights"], 16)
                sp.dma_start(px[:, :, :], a["patches"][0]).then_inc(s["inputs"], 16)
                sp.dma_start(cw[:, :, :], a["conv_w"]).then_inc(s["conv_w"], 16)
                sp.dma_start(tb[:, :, :], a["text"][0]).then_inc(s["inputs"], 16)
                sp.dma_start(cb[:, :], a["conv_b"].to_broadcast([P, C])).then_inc(s["positions"], 16)
                for k in range(GB):
                    sp.dma_start(pos[TP * k:TP * (k + 1), :], a["pos"]).then_inc(s["positions"], 16)
                load(lnv[:, :, :], a["ln"])
                load(wkvr[:, :, :, :], a["w_kvr"])
                load(dec[:, :, :], a["decfirst"])
                load(wo[:, 0, :], a["Wo"][0:P, :])
                load(wo[0:64, 1, :], a["Wo"][P:C, :])
                load(wo[64:P, 1, :], a["Wo"][P:C, :])
                with sp.Fori(1, NG) as g:
                    sp.wait_ge(s["embedded"], g)
                    sp.wait_ge(s["text_taken"], g)
                    sp.dma_start(px[:, :, :], a["patches"][bass.ds(g, 1)].rearrange("g p k m -> p (g k) m")
                                 ).then_inc(s["inputs"], 16)
                    sp.dma_start(tb[:, :, :], a["text"][bass.ds(g, 1)].rearrange("g p j c -> p (g j) c")
                                 ).then_inc(s["inputs"], 16)

            @block.gpsimd
            def _(gp):
                st = Steps(gp, s["pool"])
                st.did(gp.memset(ident[:, :], 0.0))
                st.did(gp.memset(identb[:, :], 0.0))
                st.did(gp.memset(neghalf[:, :], -0.5))
                st.did(gp.memset(KK[:, :, 0:1], NEG))
                st.did(gp.memset(VV[:, :, 0:1], 0.0))
                st.settle()
                for m in (ident, identb):
                    st.did(gp.affine_select(out=m[:, :], in_=m[:, :], compare_op=ALU.not_equal, fill=1.0,
                                            base=0, pattern=[[-1, P]], channel_multiplier=1))
                st.settle()
                st.did(gp.memset(A[:, 0:1], 0.0))
                st.did(gp.memset(Bd[:, 0:1], 0.0))
                st.settle()
                gp.memset(M[:, 0:1], 0.0).then_inc(s["consts"], 1)

                def front(g, norms=True, last=None):
                    gp.wait_ge(s["m"], g + 1)
                    gp.wait_ge(s["setup"], 1)
                    gp.tensor_tensor(out=flat(E2[:, :, :]), in0=flat(KK[:, :, :]),
                                     in1=M[:, 1:1 + 2 * ROWS * TS], op=ALU.subtract).then_inc(s["d2"], 1)
                    gp.tensor_tensor(out=EX[:, 2, :, :], in0=KK[:, 0:ROWS, 1:TS], in1=Uf[:, :, :],
                                     op=ALU.add).then_inc(s["ku"], 1)
                    if last is not None:
                        rsqrt(gp, s["var2"], s["rstd2"], last + 1)
                    gp.wait_ge(s["e2"], g + 1)
                    gp.wait_ge(s["v_in"], g * 2 + 2)
                    gp.tensor_tensor(out=flat(EV[:, :, :]), in0=flat(E2[:, :, :]), in1=flat(VV[:, :, :]),
                                     op=ALU.mult).then_inc(s["ev"], 1)
                    if norms:
                        rsqrt(gp, s["var"], s["rstd"], g * 2 + 3)
                        rsqrt(gp, s["var"], s["rstd"], g * 2 + 4)
                    gp.wait_ge(s["ex"], g + 1)
                    gp.wait_ge(s["b_scan"], g + 1)
                    bf, bb = before(Bd)
                    gp.tensor_tensor(out=D1[:, 0, :, :], in0=EX[:, 0, :, :], in1=bf, op=ALU.mult
                                     ).then_inc(s["dpart"], 1)
                    gp.tensor_tensor(out=D1[:, 1, :, :], in0=EX[:, 1, :, :], in1=bb, op=ALU.mult
                                     ).then_inc(s["dpart"], 1)

                rsqrt(gp, s["var"], s["rstd"], 1)
                rsqrt(gp, s["var"], s["rstd"], 2)
                front(0)
                with gp.Fori(0, NG - 2) as g:
                    front(g + 1, last=g)
                front(NG - 1, norms=False, last=NG - 2)
                rsqrt(gp, s["var2"], s["rstd2"], NG)

            @block.tensor
            def _(pe):
                def turn(src, ready, turned):
                    pe.wait_ge(*ready)
                    for c in range(2):
                        for j in range(3):
                            mm = pe.transpose(psT[0:HC, c, j * P:(j + 1) * P],
                                              src[:, j, c * HC:(c + 1) * HC], ident[:, :])
                    mm.then_inc(turned, 1)

                def embed(g):
                    pe.wait_ge(s["inputs"], g * 32 + 32)
                    for k in range(KC):
                        mm = pe.matmul(psT[:, 0, 0:C], px[:, k, :], cw[:, k, :], start=k == 0, stop=k == KC - 1)
                    mm.then_inc(s["embedded"], 1)

                def part(w, ps, second=None):
                    for half in range(2):
                        tok = slice(half * GT // 2, (half + 1) * GT // 2)
                        r = rows(ps)
                        for c in range(2):
                            if second is not None and half == 0 and c == 1:
                                pe.wait_ge(s["hT"], second)
                            pe.matmul(r[:, half * 4:half * 4 + 4, 0:T], wkvr[:, c, w, 0:P], hT[:, c, tok],
                                      start=c == 0, stop=c == 1)
                        for c in range(2):
                            mm = pe.matmul(r[64 * half:64 * half + 64, GB:GB + 4, 0:T],
                                           wkvr[:, c, w, P:C], hT[:, c, tok], start=c == 0, stop=c == 1)
                    mm.then_inc(s["kvr"], 1)

                def keys(g):
                    turn(hn, (s["norm1"], g * 3 + 3), s["turned1"])
                    pe.wait_ge(s["hT"], g * 4 + 2)
                    pe.wait_ge(s["done"], g if not isinstance(g, int) or g else 1)
                    part(0, psK, g * 4 + 4)

                def values_and_receptance():
                    part(1, psV)
                    part(2, psR)

                def project(g):
                    pe.wait_ge(s["y"], g * 2 + 2)
                    for j, (Y, r0, nr) in enumerate(((YP, 0, 8), (YX, 0, 4), (YX, 4, 4))):
                        Y = Y[:, :, :]
                        up = Y[:, r0:r0 + nr, :].rearrange("p r t -> p (r t)")
                        low = Y[:, GB:ROWS, :].rearrange("p r t -> p (r t)")
                        o = psT[:, j // 2, (j % 2) * 256:(j % 2) * 256 + C]
                        pe.matmul(o, up, wo[:, 0, :], start=True, stop=False,
                                  skip_group_check=True)
                        if j == 0:
                            for q in (0, 64):
                                mm = pe.matmul(o[q:q + 64, :], low[q:q + 64, :], wo[q:q + 64, 1, :],
                                               start=False, stop=True, skip_group_check=True)
                        else:
                            q = 64 * (j - 1)
                            mm = pe.matmul(o, low[q:q + 64, :], wo[q:q + 64, 1, :],
                                           start=False, stop=True, skip_group_check=True)
                    mm.then_inc(s["attn"], 1)

                def channel_mix(g, last=False):
                    turn(hn2, (s["norm2"], g * 3 + 3), s["turned2"])
                    pe.wait_ge(s["hT2"], g * 2 + 1)
                    for m in range(HCH):
                        if not last and m % 2 == 0:
                            got, n = (("k_in", 2), ("v_in", 2), ("r_in", 1))[m // 2]
                            pe.wait_ge(s[got], (g + 2) * n)
                        for c in range(2):
                            if m == 0 and c == 1:
                                pe.wait_ge(s["hT2"], g * 2 + 2)
                            mm = pe.matmul(PS[:, 2 + m, 0:GT], wkf[:, c, m * P:(m + 1) * P], hT2[:, c, :],
                                           start=c == 0, stop=c == 1)
                        mm.then_inc(s["up"], 1)
                    for j in range(3):
                        for c in range(2):
                            mm = pe.matmul(psT[:, j // 2, (j % 2) * 256:(j % 2) * 256 + C],
                                           hT2[:, c, j * P:(j + 1) * P], wrf[:, c, :], start=c == 0, stop=c == 1)
                    mm.then_inc(s["gatemm"], 1)
                    pe.wait_ge(s["relu"], g * HCH + HCH)
                    for j in range(3):
                        for m in range(HCH):
                            mm = pe.matmul(psK[:, j // 2, (j % 2) * 256:(j % 2) * 256 + C],
                                           kf[:, m, j * P:(j + 1) * P], wvf[:, m, :],
                                           start=m == 0, stop=m == HCH - 1)
                    mm.then_inc(s["down"], 1)
                    pe.wait_ge(s["gate"], g + 1)

                pe.wait_ge(s["conv_w"], 16)
                embed(0)
                pe.wait_ge(s["weights"], 16 * NW)
                pe.wait_ge(s["consts"], 1)
                keys(0)
                values_and_receptance()
                embed(1)
                pe.wait_ge(s["patches_in"], 2)
                with pe.Fori(0, NG - 2) as g:
                    keys(g + 1)
                    project(g)
                    values_and_receptance()
                    pe.wait_ge(s["x1"], g + 1)
                    embed(g + 2)
                    pe.wait_ge(s["patches_in"], g + 3)
                    channel_mix(g)
                keys(NG - 1)
                project(NG - 2)
                values_and_receptance()
                pe.wait_ge(s["x1"], NG - 1)
                channel_mix(NG - 2)
                project(NG - 1)
                channel_mix(NG - 1, last=True)

            def tiles(ps):
                return ps.rearrange("p k (j c) -> p (k j) c", c=256)[:, 0:3, 0:C]

            @block.scalar
            def _(act):
                def load(dst, src):
                    act.dma_start(dst, src).then_inc(s["weights"], 16)
                load(wkf[:, :, :], a["Wk_f"])
                load(wrf[:, :, :], a["Wr_f"])
                load(wvf[:, :, :], a["Wv_f"])
                def embedded(g):
                    act.wait_ge(s["embedded"], g + 1)
                    if not (isinstance(g, int) and g == 0):
                        act.wait_ge(s["patches_out"], g)
                    act.activation(em[:, :], psT[:, 0, 0:C], ACT.Copy).then_inc(s["patches_in"], 1)

                def keep(g):
                    act.wait_ge(s["norm1"], g * 3 + 3)
                    if not (isinstance(g, int) and g == 0):
                        act.wait_ge(s["hc_free"], g)
                    act.activation(x0k[:, :, :], x0[:, :, :], ACT.Copy).then_inc(s["kept"], 1)
                    act.activation(hck[:, :, :], hc[:, :, :], ACT.Copy).then_inc(s["kept"], 1)

                def text(g):
                    act.wait_ge(s["inputs"], g * 32 + 32)
                    if not (isinstance(g, int) and g == 0):
                        act.wait_ge(s["kept"], g * 2)
                    act.activation(hc[:, 1:3, :], tb[:, :, :], ACT.Copy).then_inc(s["text_taken"], 1)

                def rows_turned(g):
                    act.wait_ge(s["turned1"], g + 1)
                    for c in range(2):
                        for j0, j1, t0, t1 in ((0, P, 0, TP), (P, GT, TP, T)):
                            act.activation(hT[:, c, :].rearrange("p (b t) -> p b t", t=T)[:, :, t0:t1],
                                           psT[0:HC, c, j0:j1].rearrange("p (b t) -> p b t", t=t1 - t0),
                                           ACT.Identity, bias=lnv[:, 1, c:c + 1], scale=lnv[:, 0, c:c + 1]
                                           ).then_inc(s["hT"], 1)

                def mirrored(g, w, ps, dst, got):
                    act.wait_ge(s["kvr"], g * 3 + w + 1)
                    act.activation(dst[:, 0:ROWS, 1:TS], rows(ps)[:, 0:ROWS, 0:T], ACT.Identity
                                   ).then_inc(s[got], 1)
                    act.activation(dst[:, ROWS:2 * ROWS, 1:TS], rows(ps)[:, 0:ROWS, T - 1::-1],
                                   ACT.Identity).then_inc(s[got], 1)

                def keys(g):
                    mirrored(g, 0, psK, KK, "k_in")

                def values(g):
                    if not (isinstance(g, int) and g == 0):
                        act.wait_ge(s["y"], g * 2)
                    mirrored(g, 1, psV, VV, "v_in")

                def receptance(g):
                    act.wait_ge(s["kvr"], g * 3 + 3)
                    act.activation(SR[:, :, :], rows(psR)[:, 0:ROWS, 0:T], ACT.Tanh, scale=0.5
                                   ).then_inc(s["r_in"], 1)

                def decays(g):
                    act.wait_ge(s["d2"], g + 1)
                    act.activation(flat(E2[:, :, :]), flat(E2[:, :, :]), ACT.Exp).then_inc(s["e2"], 1)
                    act.wait_ge(s["e1"], g * 2 + 1)
                    act.activation(flat(E1[:, :, :]), flat(E1[:, :, :]), ACT.Exp).then_inc(s["e1"], 1)

                def shares(g):
                    act.wait_ge(s["mm"], g + 1)
                    act.activation(EX[:, :, :, :].rearrange("p k r t -> p (k r t)"),
                                   EX[:, :, :, :].rearrange("p k r t -> p (k r t)"), ACT.Exp
                                   ).then_inc(s["ex"], 1)

                def turned(g):
                    act.wait_ge(s["turned2"], g + 1)
                    for c in range(2):
                        act.activation(hT2[:, c, :], psT[0:HC, c, 0:GT], ACT.Identity, bias=lnv[:, 3, c:c + 1],
                                       scale=lnv[:, 2, c:c + 1]).then_inc(s["hT2"], 1)

                def relu_squared(g, ms):
                    for m in ms:
                        act.wait_ge(s["up"], g * HCH + m + 1)
                        act.activation(kf[:, m, :], PS[:, 2 + m, 0:GT], ACT.Relu).then_inc(s["relu0"], 1)
                        act.wait_ge(s["relu0"], g * HCH + m + 1)
                        act.activation(kf[:, m, :], kf[:, m, :], ACT.Square).then_inc(s["relu"], 1)

                def gates(g):
                    act.wait_ge(s["gatemm"], g + 1)
                    act.activation(gate[:, :, :], tiles(psT), ACT.Tanh, scale=0.5).then_inc(s["gate"], 1)

                def turn(g, last=False):
                    rows_turned(g + 1)
                    keys(g + 1)
                    decays(g + 1)
                    values(g + 1)
                    keep(g + 1)
                    if not last:
                        text(g + 2)
                    receptance(g + 1)
                    if not last:
                        embedded(g + 2)
                    turned(g)
                    relu_squared(g, (0, 1, 2))
                    shares(g + 1)
                    relu_squared(g, (3, 4, 5))
                    gates(g)

                embedded(0)
                text(0)
                act.wait_ge(s["weights"], 16 * NW)
                act.wait_ge(s["consts"], 1)
                rows_turned(0)
                keys(0)
                decays(0)
                values(0)
                receptance(0)
                embedded(1)
                keep(0)
                text(1)
                shares(0)
                with act.Fori(0, NG - 2) as g:
                    turn(g)
                turn(NG - 2, last=True)
                turned(NG - 1)
                relu_squared(NG - 1, range(HCH))
                gates(NG - 1)

            @block.vector
            def _(v):
                st = straight.on(v)
                st.did(v.memset(Wf[:, :, :], 0.0))
                st.did(v.memset(Uf[:, :, :], 0.0))
                v.wait_ge(s["positions"], 16 * (GB + 1))
                st.did(v.tensor_tensor(pos[:, :], pos[:, :], cb[:, :], ALU.add))
                st.settle()
                loop = Steps(v, s["loop_dve"], FRONT_DVE)
                back = Steps(v, s["back_dve"], BACK_DVE)

                norms = Steps(v, s["norm_dve"], NORM_DVE)

                def first_norm(g):
                    norms.turn(g)
                    v.wait_ge(s["text_taken"], g + 1)
                    v.wait_ge(s["patches_in"], g + 1)
                    v.tensor_tensor(hc[:, 0, :], em[:, :], pos[:, :], ALU.add).then_inc(s["patches_out"], 1)
                    v.wait_ge(s["patches_out"], g + 1)
                    seen(v, passed)
                    norm(v, norms, hc, x0, s["var"], s["rstd"], g * 2 + 1)
                    norms.settle()

                def second_norm(g):
                    norm(v, norms, x0, hn, s["var"], s["rstd"], g * 2 + 2, s["norm1"])
                    norms.end()

                def front(g, following=True, last=None):
                    loop.turn(g)
                    v.wait_ge(s["k_in"], g * 2 + 2)
                    v.tensor_tensor_scan(M[:, 1:1 + 2 * ROWS * TS], flat(Wf[:, :, :]), flat(KK[:, :, :]), NEG,
                                         ALU.add, ALU.max).then_inc(s["m"], 1)
                    v.wait_ge(s["m"], g + 1)
                    loop.did(v.tensor_tensor(flat(E1[:, :, :]), M[:, 0:2 * ROWS * TS], flat(Wf[:, :, :]), ALU.add))
                    loop.settle()
                    v.tensor_tensor(flat(E1[:, :, :]), flat(E1[:, :, :]), M[:, 1:1 + 2 * ROWS * TS],
                                    ALU.subtract).then_inc(s["e1"], 1)
                    if last is not None:
                        mixed(last)
                    mf, mb = before(M)
                    loop.did(v.tensor_tensor(MM[:, :, :], mf, mb, ALU.max))
                    v.wait_ge(s["ku"], g + 1)
                    loop.settle()
                    loop.did(v.tensor_tensor(MM[:, :, :], MM[:, :, :], EX[:, 2, :, :], ALU.max))
                    loop.settle()
                    loop.did(v.tensor_tensor(EX[:, 0, :, :], mf, MM[:, :, :], ALU.subtract))
                    loop.did(v.tensor_tensor(EX[:, 1, :, :], mb, MM[:, :, :], ALU.subtract))
                    v.tensor_tensor(EX[:, 2, :, :], EX[:, 2, :, :], MM[:, :, :], ALU.subtract
                                    ).then_inc(s["mm"], 1)
                    v.wait_ge(s["e1"], g * 2 + 2)
                    v.wait_ge(s["e2"], g + 1)
                    v.tensor_tensor_scan(Bd[:, 1:1 + 2 * ROWS * TS], flat(E1[:, :, :]), flat(E2[:, :, :]), 0.0,
                                         ALU.mult, ALU.add).then_inc(s["b_scan"], 1)
                    v.wait_ge(s["ev"], g + 1)
                    v.tensor_tensor_scan(A[:, 1:1 + 2 * ROWS * TS], flat(E1[:, :, :]), flat(EV[:, :, :]), 0.0,
                                         ALU.mult, ALU.add).then_inc(s["a_scan"], 1)
                    if following:
                        first_norm(g + 1)
                        second_norm(g + 1)
                    af, ab = before(A)
                    v.wait_ge(s["ex"], g + 1)
                    v.wait_ge(s["a_scan"], g + 1)
                    loop.did(v.tensor_tensor(N1[:, 0, :, :], EX[:, 0, :, :], af, ALU.mult))
                    loop.did(v.tensor_tensor(N1[:, 1, :, :], EX[:, 1, :, :], ab, ALU.mult))
                    loop.did(v.tensor_tensor(N1[:, 2, :, :], EX[:, 2, :, :], VV[:, 0:ROWS, 1:TS], ALU.mult))
                    loop.settle()
                    loop.did(v.tensor_tensor(N1[:, 0, :, :], N1[:, 0, :, :], N1[:, 1, :, :], ALU.add))
                    v.wait_ge(s["dpart"], g * 2 + 2)
                    loop.did(v.tensor_tensor(D1[:, 0, :, :], D1[:, 0, :, :], D1[:, 1, :, :], ALU.add))
                    loop.settle()
                    loop.did(v.tensor_tensor(N1[:, 0, :, :], N1[:, 0, :, :], N1[:, 2, :, :], ALU.add))
                    loop.did(v.tensor_tensor(D1[:, 0, :, :], D1[:, 0, :, :], EX[:, 2, :, :], ALU.add))
                    loop.settle()
                    loop.did(v.reciprocal(D1[:, 1, :, :], D1[:, 0, :, :]))
                    if last is not None:
                        finish(last)
                    v.wait_ge(s["r_in"], g + 1)
                    loop.did(v.scalar_tensor_tensor(N1[:, 1, :, :], SR[:, :, :], 1.0, N1[:, 0, :, :], ALU.add,
                                                    ALU.mult))
                    loop.settle()
                    for Y, t0, t1 in ((YP, 0, TP), (YX, TP, T)):
                        v.scalar_tensor_tensor(Y[:, :, :], N1[:, 1, :, t0:t1], 0.5, D1[:, 1, :, t0:t1], ALU.mult,
                                               ALU.mult).then_inc(s["y"], 1)
                    loop.end()

                def mixed(g):
                    back.turn(g)
                    v.wait_ge(s["attn"], g + 1)
                    v.wait_ge(s["kept"], g * 2 + 2)
                    v.tensor_tensor(x1[:, :, :], tiles(psT), x0k[:, :, :], ALU.add).then_inc(s["x1"], 1)
                    v.wait_ge(s["x1"], g + 1)
                    seen(v, passed)

                    def meanwhile():
                        v.tensor_tensor(xh[:, :, :], x1[:, :, :], hck[:, :, :], ALU.add).then_inc(s["hc_free"], 1)
                    norm(v, back, x1, hn2, s["var2"], s["rstd2"], g + 1, s["norm2"], meanwhile)

                def finish(g):
                    v.wait_ge(s["down"], g + 1)
                    v.wait_ge(s["gate"], g + 1)
                    v.wait_ge(s["hc_free"], g + 1)
                    back.did(v.scalar_tensor_tensor(ff[:, :, :], gate[:, :, :], 1.0, tiles(psK), ALU.add, ALU.mult))
                    back.settle()
                    v.scalar_tensor_tensor(H[:, bass.ds(g * 3, 3), :], ff[:, :, :], 0.5, xh[:, :, :], ALU.mult,
                                           ALU.add).then_inc(s["done"], 1)
                    back.end()

                v.sem_inc(s["done"], 1)
                first_norm(0)
                second_norm(0)
                v.wait_ge(s["weights"], 16 * NW)
                st.settle()
                for k, (r0, r1) in enumerate(((0, GB), (GB, ROWS))):
                    for d in range(2):
                        st.did(v.tensor_scalar(Wf[:, d * ROWS + r0:d * ROWS + r1, :],
                                               Wf[:, d * ROWS + r0:d * ROWS + r1, :], dec[:, 0, k:k + 1], 1.0 / T,
                                               ALU.add, ALU.mult))
                    st.did(v.tensor_scalar(Uf[:, r0:r1, :], Uf[:, r0:r1, :], dec[:, 1, k:k + 1], 1.0 / T,
                                           ALU.add, ALU.mult))
                st.settle()
                v.wait_ge(s["consts"], 1)
                v.memset(Wf[:, :, 0:1], 3 * NEG).then_inc(s["setup"], 1)
                v.wait_ge(s["setup"], 1)
                front(0)
                with v.Fori(0, NG - 2) as g:
                    front(g + 1, last=g)
                    v.wait_ge(s["done"], g + 2)
                front(NG - 1, following=False, last=NG - 2)
                v.wait_ge(s["done"], NG)
                mixed(NG - 1)
                finish(NG - 1)

def _layouts(np_, i):
    t = {}
    x = i["x"].reshape(NG, GB, 3, 4, 16, 4, 16)
    x = x.transpose(0, 2, 4, 6, 1, 3, 5).reshape(NG, KC, P, P)
    t["patches"] = x.transpose(0, 2, 1, 3)
    t["text"] = i["txt"].reshape(NG, 2, P, C).transpose(0, 2, 1, 3)
    t["conv_w"] = i["L0_tok_conv_w"].reshape(C, KC, P).transpose(2, 1, 0)
    t["conv_b"] = i["L0_tok_conv_b"].reshape(1, C)
    t["pos"] = i["L0_tok_pos_table"].reshape(32, 32, C)[::8, ::8].reshape(TP, C)
    t["ln"] = np_.stack([i["L0_attn_" + n].reshape(2, HC).T for n in ("ln1_w", "ln1_b", "ln2_w", "ln2_b")], 1)

    def fold(w):
        return w.T.reshape(2, HC, w.shape[0]).transpose(1, 0, 2)

    t["w_kvr"] = np_.stack([fold(i["L0_attn_" + n]) for n in ("Wk_a", "Wv_a", "Wr_a")], 2)
    t["Wo"] = i["L0_attn_Wo_a"].T
    t["Wk_f"] = fold(i["L0_attn_Wk_f"])
    t["Wr_f"] = fold(i["L0_attn_Wr_f"])
    t["Wv_f"] = i["L0_attn_Wv_f"].T.reshape(HCH, P, C).transpose(1, 0, 2)
    t["w_fc"] = fold(i["L0_ffn_w_fc"])
    t["w_proj"] = i["L0_ffn_w_proj"].T.reshape(HCH, P, C).transpose(1, 0, 2)
    t["w_in"] = fold(i["L1_attn_w_in"])
    wo = i["L1_attn_w_out"].T.reshape(3, 2, 2, DH, C).transpose(2, 1, 0, 3, 4)
    t["w_out"] = wo.reshape(2, HC, C).transpose(1, 0, 2)
    t["alpha_e"] = i["L0_ffn_alpha_e"].reshape(1, 3)
    t["alpha_r"] = i["L0_ffn_alpha_r"].reshape(1, 3)
    t["b_fc"] = i["L0_ffn_b_fc"].reshape(HCH, P).T
    t["b_proj"] = i["L0_ffn_b_proj"].reshape(1, C)
    widths = np_.array([r * e for e in EMBEDS for r in RATIOS])
    t["hmask"] = (np_.arange(HID).reshape(HCH, P).T[:, :, None] < widths).astype(np_.float32)
    t["cut"] = (np_.arange(P)[:, None] < EMBEDS[1] - HC).astype(np_.float32)
    t["iota8"] = np_.arange(NE, dtype=np_.float32).reshape(1, NE)
    t["tri"] = np_.triu(np_.ones((P, P), np_.float32), 1)
    t["home"] = np_.arange(2 * B * T, dtype=np_.float32).reshape(2, P, NT).transpose(1, 0, 2)
    t["lane"] = np_.arange(P, dtype=np_.float32).reshape(P, 1)
    t["blocks"] = np_.arange(NBLK, dtype=np_.float32).reshape(1, NBLK)
    t["router"] = fold(i["L1_ffn_router_w"])
    t["w1"] = i["L1_ffn_w1"].transpose(0, 2, 1).reshape(NE * 2, HC, ID).transpose(1, 0, 2)
    t["w2"] = i["L1_ffn_w2"].transpose(0, 2, 1).reshape(NE * 4, P, C).transpose(1, 0, 2)
    df = np_.stack([i["L0_attn_decay"], i["L0_attn_first"]])
    t["decfirst"] = np_.stack([df[:, 0:P], np_.concatenate([df[:, P:C], df[:, P:C]], 1)], 2).transpose(1, 0, 2)
    return {n: np_.ascontiguousarray(v) for n, v in t.items()}


def kernel(**inputs):
    import numpy as _np
    import concourse.bacc as _bacc
    from concourse import mybir as _mybir
    from concourse.bass_utils import run_bass_kernel_spmd as _run

    nc = _bacc.Bacc("TRN2", target_bir_lowering=False, num_devices=1)
    laid = _layouts(_np, {n: _np.asarray(v) for n, v in inputs.items()})
    a = {n: nc.dram_tensor("in_" + n, v.shape, _mybir.dt.from_np(v.dtype), kind="ExternalInput").ap()
         for n, v in laid.items()}
    out = nc.dram_tensor("out_dram", (P, NT, C), F32, kind="ExternalOutput").ap()
    rows = [nc.dram_tensor(n, shape, F32, kind="Internal").ap()
            for n, shape in (("x_rows", (NE * ROOM, C + 1)), ("y_rows", (2 * B * T, C)))]
    program(nc, a, out, *rows)
    r = _run(nc, [{"in_" + n: v for n, v in laid.items()}], core_ids=[0])
    o = r.results[0]["out_dram"].reshape(P, NG, 3, C).transpose(1, 2, 0, 3)
    got = _np.empty((B, T, C), _np.float32)
    got[:, 0:TP] = o[:, 0].reshape(B, TP, C)
    got[:, TP:T] = o[:, 1:3].reshape(B, TX, C)
    return got
```
